# Optimizing a Trainium2 kernel written in Bass

```python
import numpy as np
import jax
import jax.numpy as jnp

def _softmax(x, axis=-1):
    return jax.nn.softmax(x, axis=axis)

def _gelu(x):
    return jax.nn.gelu(x, approximate=True)

def _silu(x):
    return jax.nn.silu(x)

def _sigmoid(x):
    return jax.nn.sigmoid(x)

def _layernorm(x, axis=-1, eps=1e-05):
    m = jnp.mean(x, axis=axis, keepdims=True)
    v = jnp.var(x, axis=axis, keepdims=True)
    return (x - m) / jnp.sqrt(v + eps)

def _scatter_add(tgt, idx, src, axis=0):
    return tgt.at[idx].add(src)

def _segment_sum(src, seg, n):
    return jax.ops.segment_sum(src, seg, n)
kernel_name = 'mk_hybrid_d1_jaxref_r4_9f74d3'

def setup_inputs(seed: int=0):
    np.random.seed(seed)
    _w = jnp.asarray

    def _L0_attn_a_setup():
        import jax, jax.numpy as jnp
        import numpy as np
        B, T, D = (2, 512, 256)
        H = 16
        DH = D // H
        EPS = 1e-06

        def _feature_map(x):
            return jax.nn.elu(x) + 1.0
        key = jax.random.key(seed)
        ks = jax.random.split(key, 9)
        s = 0.02
        return {'x': jax.random.normal(ks[0], (B, T, D), dtype=jnp.float32), 'Wq': jax.random.normal(ks[1], (D, D), dtype=jnp.float32) * s, 'bq': jnp.zeros((D,), dtype=jnp.float32), 'Wk': jax.random.normal(ks[2], (D, D), dtype=jnp.float32) * s, 'bk': jnp.zeros((D,), dtype=jnp.float32), 'Wv': jax.random.normal(ks[3], (D, D), dtype=jnp.float32) * s, 'bv': jnp.zeros((D,), dtype=jnp.float32), 'Wo': jax.random.normal(ks[4], (D, D), dtype=jnp.float32) * s, 'bo': jnp.zeros((D,), dtype=jnp.float32)}
    _L0_attn_a_in = _L0_attn_a_setup()

    def _L0_attn_b_setup():
        import jax, jax.numpy as jnp
        import numpy as np
        HEADS = 16
        NUM_LANDMARKS = 64
        PINV_ITERS = 6
        D_MODEL = 256

        def _moore_penrose_pinv(x, num_iters):
            m = x.shape[-1]
            I = jnp.eye(m, dtype=x.dtype)
            V = x
            for _ in range(num_iters):
                KV = x @ V
                V = 0.25 * V @ (13.0 * I - KV @ (15.0 * I - KV @ (7.0 * I - KV)))
            return V
        key = jax.random.key(seed)
        k1, k2, k3 = jax.random.split(key, 3)
        b, n, d = (4, 1024, D_MODEL)
        hidden_states = jax.random.normal(k1, (b, n, d), dtype=jnp.float32)
        Wqkv = jax.random.normal(k2, (d, 3 * d), dtype=jnp.float32) * 0.02
        bqkv = jnp.zeros((3 * d,), dtype=jnp.float32)
        Wout = jax.random.normal(k3, (d, d), dtype=jnp.float32) * 0.02
        bout = jnp.zeros((d,), dtype=jnp.float32)
        return {'hidden_states': hidden_states, 'Wqkv': Wqkv, 'bqkv': bqkv, 'Wout': Wout, 'bout': bout}
    _L0_attn_b_in = _L0_attn_b_setup()

    def _L0_ffn_setup():
        import math
        import jax, jax.numpy as jnp
        import numpy as np
        NUM_EXPERTS = 16
        TOP_K = 2
        CAPACITY_FACTOR = 1.25
        key = jax.random.key(seed)
        k1, k2, k3, k4 = jax.random.split(key, 4)
        d, dff, E = (256, 1024, NUM_EXPERTS)
        x = jax.random.normal(k1, (4, 512, d), dtype=jnp.float32)
        router_w = jax.random.normal(k2, (E, d), dtype=jnp.float32) * d ** (-0.5)
        router_b = jnp.zeros((E,), dtype=jnp.float32)
        w1 = jax.random.normal(k3, (E, d, dff), dtype=jnp.float32) * 0.02
        b1 = jnp.zeros((E, dff), dtype=jnp.float32)
        w2 = jax.random.normal(k4, (E, dff, d), dtype=jnp.float32) * 0.02
        b2 = jnp.zeros((E, d), dtype=jnp.float32)
        return {'x': x, 'router_w': router_w, 'router_b': router_b, 'w1': w1, 'b1': b1, 'w2': w2, 'b2': b2}
    _L0_ffn_in = _L0_ffn_setup()
    _d = {'L0_attn_a_x': _L0_attn_a_in['x'], 'L0_attn_a_Wq': _L0_attn_a_in['Wq'], 'L0_attn_a_bq': _L0_attn_a_in['bq'], 'L0_attn_a_Wk': _L0_attn_a_in['Wk'], 'L0_attn_a_bk': _L0_attn_a_in['bk'], 'L0_attn_a_Wv': _L0_attn_a_in['Wv'], 'L0_attn_a_bv': _L0_attn_a_in['bv'], 'L0_attn_a_Wo': _L0_attn_a_in['Wo'], 'L0_attn_a_bo': _L0_attn_a_in['bo'], 'L0_attn_b_Wqkv': _L0_attn_b_in['Wqkv'], 'L0_attn_b_bqkv': _L0_attn_b_in['bqkv'], 'L0_attn_b_Wout': _L0_attn_b_in['Wout'], 'L0_attn_b_bout': _L0_attn_b_in['bout'], 'L0_ffn_router_w': _L0_ffn_in['router_w'], 'L0_ffn_router_b': _L0_ffn_in['router_b'], 'L0_ffn_w1': _L0_ffn_in['w1'], 'L0_ffn_b1': _L0_ffn_in['b1'], 'L0_ffn_w2': _L0_ffn_in['w2'], 'L0_ffn_b2': _L0_ffn_in['b2']}
    _x0 = _d['L0_attn_a_x']
    _d['L0_attn_a_x'] = jax.random.normal(jax.random.fold_in(jax.random.key(seed), 1), (4, 1024, 256), dtype=_x0.dtype)
    del _x0
    return _d

def reference(L0_attn_a_x, L0_attn_a_Wq, L0_attn_a_bq, L0_attn_a_Wk, L0_attn_a_bk, L0_attn_a_Wv, L0_attn_a_bv, L0_attn_a_Wo, L0_attn_a_bo, L0_attn_b_Wqkv, L0_attn_b_bqkv, L0_attn_b_Wout, L0_attn_b_bout, L0_ffn_router_w, L0_ffn_router_b, L0_ffn_w1, L0_ffn_b1, L0_ffn_w2, L0_ffn_b2):

    def _L0_attn_a_ref(x, Wq, bq, Wk, bk, Wv, bv, Wo, bo):
        import jax, jax.numpy as jnp
        import numpy as np
        B, T, D = (2, 512, 256)
        H = 16
        DH = D // H
        EPS = 1e-06

        def _feature_map(x):
            return jax.nn.elu(x) + 1.0
        b, t, d = x.shape
        q = (x @ Wq.T + bq).reshape(b, t, H, DH).transpose(0, 2, 1, 3)
        k = (x @ Wk.T + bk).reshape(b, t, H, DH).transpose(0, 2, 1, 3)
        v = (x @ Wv.T + bv).reshape(b, t, H, DH).transpose(0, 2, 1, 3)
        q = _feature_map(q)
        k = _feature_map(k)
        kv = jnp.einsum('bhtd,bhte->bhtde', k, v)
        kv_cum = jnp.cumsum(kv, axis=2)
        numerator = jnp.einsum('bhtd,bhtde->bhte', q, kv_cum)
        k_cum = jnp.cumsum(k, axis=2)
        denominator = jnp.einsum('bhtd,bhtd->bht', q, k_cum)
        denominator = jnp.maximum(denominator, EPS)[..., None]
        out = numerator / denominator
        out = out.transpose(0, 2, 1, 3).reshape(b, t, d)
        return out @ Wo.T + bo

    def _L0_attn_b_ref(hidden_states, Wqkv, bqkv, Wout, bout):
        import jax, jax.numpy as jnp
        import numpy as np
        HEADS = 16
        NUM_LANDMARKS = 64
        PINV_ITERS = 6
        D_MODEL = 256

        def _moore_penrose_pinv(x, num_iters):
            m = x.shape[-1]
            I = jnp.eye(m, dtype=x.dtype)
            V = x
            for _ in range(num_iters):
                KV = x @ V
                V = 0.25 * V @ (13.0 * I - KV @ (15.0 * I - KV @ (7.0 * I - KV)))
            return V
        b, n, d = hidden_states.shape
        h, m = (HEADS, NUM_LANDMARKS)
        dh = d // h
        scale = 1.0 / np.sqrt(dh).astype(np.float32)
        l = n // m
        qkv = hidden_states @ Wqkv + bqkv
        q, k, v = jnp.split(qkv, 3, axis=-1)

        def to_heads(t):
            return t.reshape(b, n, h, dh).transpose(0, 2, 1, 3)
        q, k, v = (to_heads(q), to_heads(k), to_heads(v))
        q = q * scale
        q_l = q.reshape(b, h, m, l, dh).mean(axis=3)
        k_l = k.reshape(b, h, m, l, dh).mean(axis=3)
        sim1 = jnp.einsum('bhid,bhjd->bhij', q, k_l)
        sim2 = jnp.einsum('bhid,bhjd->bhij', q_l, k_l)
        sim3 = jnp.einsum('bhid,bhjd->bhij', q_l, k)
        attn1 = jax.nn.softmax(sim1, axis=-1)
        attn2 = jax.nn.softmax(sim2, axis=-1)
        attn3 = jax.nn.softmax(sim3, axis=-1)
        attn2_inv = _moore_penrose_pinv(attn2, PINV_ITERS)
        out = attn1 @ (attn2_inv @ (attn3 @ v))
        out = out.transpose(0, 2, 1, 3).reshape(b, n, d)
        out = out @ Wout + bout
        return out

    def _L0_ffn_ref(x, router_w, router_b, w1, b1, w2, b2):
        import math
        import jax, jax.numpy as jnp
        import numpy as np
        NUM_EXPERTS = 16
        TOP_K = 2
        CAPACITY_FACTOR = 1.25
        E, k = (NUM_EXPERTS, TOP_K)
        B, S, d = x.shape
        tokens = B * S
        capacity = max(1, int(math.ceil(CAPACITY_FACTOR * tokens * k / E)))
        x2d = x.reshape(tokens, d)
        logits = x2d @ router_w.T + router_b
        vals, idx = jax.lax.top_k(logits, k)
        gates = jax.nn.softmax(vals, axis=-1)
        flat_e = idx.reshape(-1)
        oh = (flat_e[:, None] == jnp.arange(E)[None, :]).astype(jnp.int32)
        pos = jnp.take_along_axis(jnp.cumsum(oh, axis=0) - 1, flat_e[:, None], axis=1)[:, 0]
        kept = pos < capacity
        kept2 = kept.reshape(tokens, k)
        denom = jnp.sum(gates * kept2, axis=-1, keepdims=True)
        gates = jnp.where(kept2, gates / (denom + 1e-09), 0.0)
        slot = flat_e * capacity + pos
        slot_safe = jnp.where(kept, slot, E * capacity)
        x_rep = jnp.repeat(x2d, k, axis=0)
        buf = jnp.zeros((E * capacity + 1, d), x.dtype).at[slot_safe].set(x_rep)
        packed = buf[:E * capacity].reshape(E, capacity, d)
        h = jax.nn.gelu(jnp.einsum('ecd,edf->ecf', packed, w1) + b1[:, None, :], approximate=False)
        expert_out = jnp.einsum('ecf,efd->ecd', h, w2) + b2[:, None, :]
        eflat = expert_out.reshape(E * capacity, d)
        gathered = eflat[jnp.clip(slot, 0, E * capacity - 1)]
        w = (gates.reshape(-1) * kept.astype(x.dtype))[:, None]
        out = (gathered * w).reshape(tokens, k, d).sum(axis=1)
        return out.reshape(B, S, d)
    x = L0_attn_a_x
    x = x + _L0_attn_a_ref(_layernorm(x, axis=-1), L0_attn_a_Wq, L0_attn_a_bq, L0_attn_a_Wk, L0_attn_a_bk, L0_attn_a_Wv, L0_attn_a_bv, L0_attn_a_Wo, L0_attn_a_bo)
    x = x + _L0_ffn_ref(_layernorm(x, axis=-1), L0_ffn_router_w, L0_ffn_router_b, L0_ffn_w1, L0_ffn_b1, L0_ffn_w2, L0_ffn_b2)
    x = x + _L0_attn_b_ref(_layernorm(x, axis=-1), L0_attn_b_Wqkv, L0_attn_b_bqkv, L0_attn_b_Wout, L0_attn_b_bout)
    x = x + _L0_ffn_ref(_layernorm(x, axis=-1), L0_ffn_router_w, L0_ffn_router_b, L0_ffn_w1, L0_ffn_b1, L0_ffn_w2, L0_ffn_b2)
    return x

_drawn_inputs = setup_inputs


def setup_inputs(seed=0):
    import zlib

    import numpy as np

    out = dict(_drawn_inputs(seed))
    spreads = {'L0_attn_a_bq': (0.0, 0.8),
     'L0_attn_a_bk': (0.0, 0.8),
     'L0_attn_a_bv': (0.0, 0.1),
     'L0_attn_a_bo': (0.0, 0.1),
     'L0_attn_b_bqkv': (0.0, 0.1),
     'L0_attn_b_bout': (0.0, 0.1),
     'L0_ffn_router_b': (0.0, 0.1),
     'L0_ffn_b1': (0.0, 0.1),
     'L0_ffn_b2': (0.0, 0.1)}
    factors = {'L0_attn_a_Wq': 8.0, 'L0_attn_a_Wk': 8.0, 'L0_attn_a_Wv': 3.839, 'L0_attn_b_Wqkv': 3.226}
    for name, (base, spread) in spreads.items():
        noise = np.random.default_rng([zlib.crc32(name.encode()), seed]).standard_normal(out[name].shape)
        drawn = base * np.exp(spread * noise) if base else spread * noise
        out[name] = jnp.asarray(drawn.astype(out[name].dtype))
    for name, factor in factors.items():
        out[name] = (out[name] * factor).astype(out[name].dtype)
    return out
```

```python
from contextlib import ExitStack

import concourse.bass as bass
import numpy as np
from concourse import mybir

F32 = mybir.dt.float32
BF16 = mybir.dt.bfloat16
I32 = mybir.dt.int32
ALU = mybir.AluOpType
ACT = mybir.ActivationFunctionType
AX_X = mybir.AxisListType.X
AX_XY = mybir.AxisListType.XY

P = 128
LN_EPS = 1e-5
DEN_EPS = 1e-6

C_IDENT = 0
C_CAUSAL = 128
C_HEAD8 = 256
C_BLOCK = 264
C_KEEP = 536
C_STRICT = 568
C_IOTA = 696
C_EYE7 = 712
C_TRASH = 904
C_WIDTH = 968


def constants(batch_tiles, tiles):
    c = np.zeros((P, C_WIDTH), np.float32)
    p = np.arange(P)[:, None]
    col = np.arange(P)[None, :]
    c[:, C_IDENT:C_IDENT + P] = p == col
    c[:, C_CAUSAL:C_CAUSAL + P] = p <= col
    c[:, C_HEAD8:C_HEAD8 + 8] = p // 16 == np.arange(8)[None, :]
    c[:, C_BLOCK:C_BLOCK + 272] = p // 16 == (np.arange(272) // 17 % 8)[None, :]
    c[:, C_KEEP:C_KEEP + tiles] = (np.arange(tiles) + 1) % batch_tiles != 0
    c[:, C_STRICT:C_STRICT + P] = p < col
    c[:, C_IOTA:C_IOTA + 16] = np.arange(16)
    for n, f in enumerate((7.0, 15.0, 13.0)):
        c[:, C_EYE7 + 64 * n:C_EYE7 + 64 * n + 64] = f * (p % 64 == np.arange(64)[None, :])
    c[:, C_TRASH:C_TRASH + 2 * tiles] = np.arange(2 * tiles)[None, :] * P + p
    return c


def at_least(eng, sem, count):
    if isinstance(count, int) and count <= 0:
        return
    eng.wait_ge(sem, count)


def pipeline(eng, tiles, depth, step):
    first = depth + depth % 2
    last = first + (tiles - first) // 2 * 2
    for it in range(first):
        step(it, it % 2, lambda lag, it=it: 0 <= it - lag < tiles)
    with eng.Fori(first // 2, last // 2) as turn:
        for u in range(2):
            step(2 * turn + u, u, lambda lag: True)
    for it in range(last, tiles + depth):
        step(it, it % 2, lambda lag, it=it: 0 <= it - lag < tiles)


class Buffers:

    def __init__(self, nc, stack):
        self.nc, self.stack = nc, stack

    def sb(self, name, shape, dt=F32):
        return self.stack.enter_context(self.nc.sbuf_tensor(name, shape, dt))

    def ps(self, name, shape=(P, 512), dt=F32):
        return self.stack.enter_context(self.nc.psum_tensor(name, list(shape), dt))

    def sem(self, name):
        return self.stack.enter_context(self.nc.semaphore(name))


def linear_attention(nc, core, x_in, wqkT, wvT, woT, bqk, bv, bo, rwT, rb, logits):
    x, xn_all, cst, NT = core.x, core.xn, core.cst, core.NT
    NH, DH = 16, 16
    KD = 2
    LX, LA, LB, LC, LD = 0, 1, 2, 3, 4
    with ExitStack() as stack:
        B = Buffers(nc, stack)
        wqk = B.sb("a_wqk", [P, KD, 512])
        wv = B.sb("a_wv", [P, KD, 256])
        wo = B.sb("a_wo", [P, KD, 256])
        rw = B.sb("a_rw", [P, KD, 16])
        bias_qk = B.sb("a_bias_qk", [P, 4])
        bias_v = B.sb("a_bias_v", [P, 256])
        bias_o = B.sb("a_bias_o", [P, 256])
        bias_r = B.sb("a_bias_r", [P, 16])
        tick = B.sb("a_tick", [P, 2])
        stats = B.sb("a_stats", [P, 2, 6])
        mv = B.sb("a_mv", [P, 2, 2])
        rstd = B.sb("a_rstd", [P, 2])
        xln = B.sb("a_xln", [P, 2, 256])
        xlnT = B.sb("a_xlnT", [P, 2, KD, P])
        er = B.sb("a_er", [P, 2, 2, 4, P])
        phi = B.sb("a_phi", [P, 2, 4, P])
        qbd = B.sb("a_qbd", [P, 2, 2, 8, P])
        vaug = B.sb("a_vaug", [P, 2, NH, DH + 1])
        ktok = B.sb("a_ktok", [P, 256])
        sc = B.sb("a_sc", [P, NH, P])
        state = B.sb("a_state", [P, 2, 136])
        stmp = B.sb("a_stmp", [P, 272])
        den = B.sb("a_den", [P, NH])
        rec = B.sb("a_rec", [P, NH])
        o = B.sb("a_o", [P, 2, 256])
        oT = B.sb("a_oT", [P, KD, P])
        stats2 = B.sb("a_stats2", [P, 2, 6])
        mv2 = B.sb("a_mv2", [P, 2, 2])
        rstd2 = B.sb("a_rstd2", [P, 2])
        xr = B.sb("a_xr", [P, 2, 256])
        xrT = B.sb("a_xrT", [P, KD, P])

        b_t, b_qk, b_v, b_s0, b_s1, b_o, b_st, b_c = [core.bank[i] for i in range(8)]
        b_s = [b_s0, b_s1]

        loaded = B.sem("a_loaded")
        x_here = B.sem("a_x_here")
        zero_made = B.sem("a_zero_made")
        zero = B.sb("a_zero", [P, 2560])
        made = B.sem("a_made")
        ln_chain = B.sem("a_ln_chain")
        ln_rstd = B.sem("a_ln_rstd")
        xln_ready = B.sem("a_xln_ready")
        xlnT_psum = B.sem("a_xlnT_psum")
        xlnT_ready = B.sem("a_xlnT_ready")
        qk_psum = B.sem("a_qk_psum")
        v_psum = B.sem("a_v_psum")
        er_ready = B.sem("a_er_ready")
        phi_ready = B.sem("a_phi_ready")
        v_ready = B.sem("a_v_ready")
        qbd_ready = B.sem("a_qbd_ready")
        k_psum = B.sem("a_k_psum")
        ktok_ready = B.sem("a_ktok_ready")
        s_psum = B.sem("a_s_psum")
        s_ready = B.sem("a_s_ready")
        o_psum = B.sem("a_o_psum")
        o_chain = B.sem("a_o_chain")
        o_ready = B.sem("a_o_ready")
        st_psum = B.sem("a_st_psum")
        st_chain = B.sem("a_st_chain")
        st_ready = B.sem("a_st_ready")
        oT_psum = B.sem("a_oT_psum")
        oT_ready = B.sem("a_oT_ready")
        y_psum = B.sem("a_y_psum")
        x_chain = B.sem("a_x_chain")
        r_rstd = B.sem("a_r_rstd")
        xr_ready = B.sem("a_xr_ready")
        xr_kept = B.sem("a_xr_kept")
        xrT_psum = B.sem("a_xrT_psum")
        xrT_ready = B.sem("a_xrT_ready")
        logits_psum = B.sem("a_logits_psum")
        logits_read = B.sem("a_logits_read")

        ident = cst[:, C_IDENT:C_IDENT + P]
        N_LOADS = 9

        with nc.Block() as block:

            @block.sync
            def _(sp):
                sp.dma_start(cst[:, :], core.cst_dram).then_inc(loaded, 16)
                for b in range(4):
                    sp.dma_start(x[:, 8 * b:8 * b + 8, :],
                                 x_in[1024 * b:1024 * b + 1024, :].rearrange("(t p) d -> p t d", p=P)).then_inc(x_here, 16)
                    if b == 0:
                        sp.dma_start(wqk[:, :, :], wqkT.rearrange("(k p) n -> p k n", p=P)).then_inc(loaded, 16)
                        sp.dma_start(wv[:, :, :], wvT.rearrange("(k p) n -> p k n", p=P)).then_inc(loaded, 16)
                sp.dma_start(wo[:, :, :], woT.rearrange("(k p) n -> p k n", p=P)).then_inc(loaded, 16)
                sp.dma_start(rw[:, :, :], rwT.rearrange("(k p) n -> p k n", p=P)).then_inc(loaded, 16)
                sp.dma_start(bias_qk[:, :], bqk.rearrange("(g p) -> p g", p=P), allow_slow_non_contiguous=True).then_inc(loaded, 16)
                sp.dma_start(bias_v[:, :], bv[None, :].to_broadcast([P, 256])).then_inc(loaded, 16)
                sp.dma_start(bias_o[:, :], bo[None, :].to_broadcast([P, 256])).then_inc(loaded, 16)
                sp.dma_start(bias_r[:, :], rb[None, :].to_broadcast([P, 16])).then_inc(loaded, 16)
                sp.wait_ge(zero_made, 1)
                slots = core.NE * core.CAP
                sp.dma_start(core.slots_dram[0:slots, :].rearrange("(p a b) d -> p a (b d)", p=P, b=10),
                             zero[:, :].unsqueeze(1).to_broadcast([P, slots // P // 10, 2560])).then_inc(core.zeroed, 16)

            @block.gpsimd
            def _(pool):
                pool.memset(zero[:, :], 0.0).then_inc(zero_made, 1)
                pool.memset(core.minus_half[:, :], -0.5).then_inc(made, 1)
                pool.memset(state[:, :, :], 0.0).then_inc(made, 1)
                pool.memset(vaug[:, :, :, :], 1.0).then_inc(made, 1)
                pool.wait_ge(made, 3)
                pool.wait_ge(loaded, 16 * N_LOADS)

                def step(it, par, live):
                    if live(LX):
                        i = it
                        at_least(pool, ln_chain, 3 * i + 3)
                        pool.tensor_tensor(rstd[:, par:par + 1], mv[:, par, 1:2], core.minus_half[:, :], ALU.pow).then_inc(ln_rstd, 1)
                    if live(LC):
                        i = it - LC
                        q = (par + LC) % 2
                        at_least(pool, x_chain, 5 * i + 5)
                        pool.tensor_tensor(rstd2[:, q:q + 1], mv2[:, q, 1:2], core.minus_half[:, :], ALU.pow).then_inc(r_rstd, 1)
                    if live(LA):
                        i = it - LA
                        q = (par + LA) % 2
                        at_least(pool, phi_ready, i + 1)
                        at_least(pool, s_psum, 4 * (i - 1))
                        for half in range(2):
                            ins = pool.tensor_tensor(
                                qbd[:, q, half, :, :],
                                phi[:, q, half:half + 1, :].to_broadcast([P, 8, P]),
                                cst[:, C_HEAD8:C_HEAD8 + 8].unsqueeze(2).to_broadcast([P, 8, P]), ALU.mult)
                        ins.then_inc(qbd_ready, 1)
                    if live(LC):
                        i = it - LC
                        q = (par + LC) % 2
                        at_least(pool, xr_ready, i + 1)
                        pool.tensor_copy(xn_all[:, i, :], xr[:, q, :]).then_inc(xr_kept, 1)

                pipeline(pool, NT, LD, step)

            @block.scalar
            def _(act):
                act.wait_ge(loaded, 16 * N_LOADS)

                def step(it, par, live):
                    if live(LA):
                        i, q = it - LA, (par + LA) % 2
                        at_least(act, xlnT_psum, i + 1)
                        at_least(act, v_psum, i - 1)
                        act.activation(xlnT[:, q, :, :], b_t[:, 0:256].rearrange("p (k t) -> p k t", k=KD), ACT.Copy).then_inc(xlnT_ready, 1)
                    if live(LD):
                        i = it - LD
                        at_least(act, xrT_psum, i + 1)
                        at_least(act, logits_psum, i)
                        act.activation(xrT[:, :, :], b_t[:, 256:512].rearrange("p (k t) -> p k t", k=KD), ACT.Copy).then_inc(xrT_ready, 1)
                    if live(LC):
                        i = it - LC
                        at_least(act, oT_psum, i + 1)
                        at_least(act, y_psum, i)
                        act.activation(oT[:, :, :], b_c[:, 0:256].rearrange("p (k t) -> p k t", k=KD), ACT.Copy).then_inc(oT_ready, 1)
                    if live(LB):
                        i = it - LB
                        at_least(act, k_psum, i + 1)
                        at_least(act, st_psum, i)
                        act.activation(ktok[:, :], b_v[:, 256:512], ACT.Copy).then_inc(ktok_ready, 1)
                    if live(LA):
                        i, q = it - LA, (par + LA) % 2
                        at_least(act, qk_psum, i + 1)
                        at_least(act, phi_ready, i - 1)
                        for g in range(4):
                            act.activation(er[:, q, 0, g, :], b_qk[:, P * g:P * g + P], ACT.Exp, bias=bias_qk[:, g:g + 1])
                        for g in range(4):
                            ins = act.activation(er[:, q, 1, g, :], b_qk[:, P * g:P * g + P], ACT.Relu, bias=bias_qk[:, g:g + 1])
                        ins.then_inc(er_ready, 1)

                pipeline(act, NT, LD, step)

            @block.tensor
            def _(pe):
                pe.wait_ge(loaded, 16 * N_LOADS)
                pe.wait_ge(made, 3)

                def step(it, par, live):
                    if live(LA):
                        i, q = it - LA, (par + LA) % 2
                        at_least(pe, xln_ready, i + 1)
                        at_least(pe, xlnT_ready, i)
                        at_least(pe, xrT_ready, it - LD)
                        for k in range(KD):
                            ins = pe.transpose(b_t[:, P * k:P * k + P], xln[:, q, P * k:P * k + P], ident)
                        ins.then_inc(xlnT_psum, 1)
                    if live(LD):
                        i, q = it - LD, (par + LD) % 2
                        at_least(pe, xr_ready, i + 1)
                        if live(LA):
                            at_least(pe, xlnT_ready, it - LA + 1)
                        for k in range(KD):
                            ins = pe.transpose(b_t[:, 256 + P * k:256 + P * k + P], xr[:, q, P * k:P * k + P], ident)
                        ins.then_inc(xrT_psum, 1)
                    if live(LC):
                        i, q = it - LC, (par + LC) % 2
                        at_least(pe, o_ready, i + 1)
                        at_least(pe, x_chain, 5 * (i - 1) + 1)
                        for k in range(KD):
                            ins = pe.transpose(b_c[:, P * k:P * k + P], o[:, q, P * k:P * k + P], ident)
                        ins.then_inc(oT_psum, 1)
                    if live(LB):
                        i, q = it - LB, (par + LB) % 2
                        at_least(pe, phi_ready, i + 1)
                        at_least(pe, v_ready, i + 1)
                        for k in range(KD):
                            ins = pe.transpose(b_v[:, 256 + P * k:256 + P * k + P], phi[:, q, 2 + k, :], ident)
                        ins.then_inc(k_psum, 1)
                        at_least(pe, qbd_ready, i + 1)
                        for g in range(4):
                            half = g // 2
                            at_least(pe, s_ready, 4 * i + g - 1)
                            pe.matmul(b_s[g % 2][:, :], phi[:, q, 2 + half, :],
                                      qbd[:, q, half, 4 * (g % 2):4 * (g % 2) + 4, :],
                                      start=True, stop=True).then_inc(s_psum, 1)
                    if live(LA):
                        i, q = it - LA, (par + LA) % 2
                        at_least(pe, xlnT_ready, i + 1)
                        at_least(pe, er_ready, i)
                        for g in range(4):
                            for k in range(KD):
                                ins = pe.matmul(b_qk[:, P * g:P * g + P], wqk[:, k, P * g:P * g + P], xlnT[:, q, k, :],
                                                start=(k == 0), stop=(k == KD - 1))
                        ins.then_inc(qk_psum, 1)
                        at_least(pe, v_ready, i)
                        at_least(pe, ktok_ready, i)
                        for k in range(KD):
                            ins = pe.matmul(b_v[:, 0:256], xlnT[:, q, k, :], wv[:, k, :], start=(k == 0), stop=(k == KD - 1))
                        ins.then_inc(v_psum, 1)
                    if live(LC):
                        i = it - LC
                        at_least(pe, oT_ready, i + 1)
                        for k in range(KD):
                            ins = pe.matmul(b_c[:, 256:512], oT[:, k, :], wo[:, k, :], start=(k == 0), stop=(k == KD - 1))
                        ins.then_inc(y_psum, 1)
                    if live(LB):
                        i, q = it - LB, (par + LB) % 2
                        at_least(pe, st_ready, i)
                        at_least(pe, o_ready, i)
                        for half in range(2):
                            pe.matmul(b_o[:, 136 * half:136 * half + 136], phi[:, q, half, :], state[:, half, :],
                                      start=(half == 0), stop=False, skip_group_check=True)
                        for h in range(NH):
                            if h % 4 == 0:
                                at_least(pe, s_ready, 4 * i + h // 4 + 1)
                            ins = pe.matmul(b_o[:, 17 * h:17 * h + 17], sc[:, h, :], vaug[:, q, h, :],
                                            start=False, stop=(h == NH - 1), skip_group_check=True)
                        ins.then_inc(o_psum, 1)
                    if live(LD):
                        i = it - LD
                        at_least(pe, xrT_ready, i + 1)
                        at_least(pe, st_ready, it - LB if live(LB) else NT)
                        at_least(pe, logits_read, i)
                        for k in range(KD):
                            ins = pe.matmul(b_st[:, 272:288], xrT[:, k, :], rw[:, k, :], start=(k == 0), stop=(k == KD - 1))
                        ins.then_inc(logits_psum, 1)
                    if live(LB):
                        i, q = it - LB, (par + LB) % 2
                        at_least(pe, ktok_ready, i + 1)
                        at_least(pe, logits_read, it - LD + 1)
                        for half in range(2):
                            ins = pe.matmul(b_st[:, 136 * half:136 * half + 136], ktok[:, P * half:P * half + P],
                                            vaug[:, q, 8 * half:8 * half + 8, :], start=True, stop=True)
                        ins.then_inc(st_psum, 1)

                pipeline(pe, NT, LD, step)

            @block.vector
            def _(dve):
                dve.wait_ge(x_here, 64)
                dve.wait_ge(loaded, 16 * N_LOADS)
                dve.wait_ge(made, 3)

                def variance(src, st, m, chain, done):
                    dve.memset(tick[:, 0:1], 0.0)
                    dve.bn_stats(st, src).then_inc(chain, 1)
                    at_least(dve, chain, done + 1)
                    dve.memset(tick[:, 1:2], 0.0)
                    dve.bn_aggr(m, st).then_inc(chain, 1)
                    at_least(dve, chain, done + 2)
                    dve.tensor_scalar(m[:, 1:2], m[:, 1:2], LN_EPS, None, ALU.add).then_inc(chain, 1)

                def step(it, par, live):
                    if live(LX):
                        variance(x[:, it, :], stats[:, par, :], mv[:, par, :], ln_chain, 3 * it)
                    if live(LB):
                        i = it - LB
                        for g in range(4):
                            at_least(dve, s_psum, 4 * i + g + 1)
                            at_least(dve, o_psum, i)
                            dve.tensor_tensor(sc[:, 4 * g:4 * g + 4, :],
                                              b_s[g % 2][:, :].rearrange("p (h t) -> p h t", h=4),
                                              cst[:, C_CAUSAL:C_CAUSAL + P].unsqueeze(1).to_broadcast([P, 4, P]),
                                              ALU.mult).then_inc(s_ready, 1)
                    if live(LA):
                        i, q = it - LA, (par + LA) % 2
                        at_least(dve, er_ready, i + 1)
                        at_least(dve, o_psum, i - 1)
                        at_least(dve, qbd_ready, i - 1)
                        dve.scalar_tensor_tensor(phi[:, q, :, :], er[:, q, 0, :, :], 1.0, er[:, q, 1, :, :],
                                                 ALU.min, ALU.add).then_inc(phi_ready, 1)
                        at_least(dve, v_psum, i + 1)
                        at_least(dve, st_psum, i - 1)
                        dve.tensor_tensor(vaug[:, q, :, 0:DH], b_v[:, 0:256].rearrange("p (h e) -> p h e", h=NH),
                                          bias_v[:, :].rearrange("p (h e) -> p h e", h=NH), ALU.add).then_inc(v_ready, 1)
                    if live(LC):
                        i, q = it - LC, (par + LC) % 2
                        at_least(dve, y_psum, i + 1)
                        dve.tensor_tensor(x[:, i, :], x[:, i, :], b_c[:, 256:512], ALU.add).then_inc(x_chain, 1)
                        at_least(dve, x_chain, 5 * i + 1)
                        dve.tensor_tensor(x[:, i, :], x[:, i, :], bias_o[:, :], ALU.add).then_inc(x_chain, 1)
                        at_least(dve, x_chain, 5 * i + 2)
                        variance(x[:, i, :], stats2[:, q, :], mv2[:, q, :], x_chain, 5 * i + 2)
                    if live(LX):
                        at_least(dve, ln_rstd, it + 1)
                        at_least(dve, xlnT_psum, it - 1)
                        dve.tensor_scalar(xln[:, par, :], x[:, it, :], mv[:, par, 0:1], rstd[:, par:par + 1],
                                          ALU.subtract, ALU.mult).then_inc(xln_ready, 1)
                    if live(LB):
                        i, q = it - LB, (par + LB) % 2
                        at_least(dve, o_psum, i + 1)
                        ops = b_o[:, 0:272].rearrange("p (h e) -> p h e", h=NH)
                        dve.tensor_scalar(den[:, :], ops[:, :, DH], DEN_EPS, None, ALU.max).then_inc(o_chain, 1)
                        at_least(dve, o_chain, 2 * i + 1)
                        dve.reciprocal(rec[:, :], den[:, :]).then_inc(o_chain, 1)
                        at_least(dve, o_chain, 2 * i + 2)
                        at_least(dve, oT_psum, i - 1)
                        dve.tensor_tensor(o[:, q, :].rearrange("p (h e) -> p h e", h=NH), ops[:, :, 0:DH],
                                          rec[:, :].unsqueeze(2).to_broadcast([P, NH, DH]), ALU.mult).then_inc(o_ready, 1)
                    if live(LC):
                        i, q = it - LC, (par + LC) % 2
                        at_least(dve, r_rstd, i + 1)
                        at_least(dve, xrT_psum, i - 1)
                        at_least(dve, xr_kept, i - 1)
                        dve.tensor_scalar(xr[:, q, :], x[:, i, :], mv2[:, q, 0:1], rstd2[:, q:q + 1],
                                          ALU.subtract, ALU.mult).then_inc(xr_ready, 1)
                    if live(LD):
                        i = it - LD
                        at_least(dve, logits_psum, i + 1)
                        dve.tensor_tensor(logits[:, i, :], b_st[:, 272:288], bias_r[:, :], ALU.add).then_inc(logits_read, 1)
                    if live(LB):
                        i, q = it - LB, (par + LB) % 2
                        keep = cst[:, bass.ds(i + C_KEEP, 1)]
                        at_least(dve, st_psum, i + 1)
                        dve.scalar_tensor_tensor(stmp[:, :], b_st[:, 0:272], keep, cst[:, C_BLOCK:C_BLOCK + 272],
                                                 ALU.mult, ALU.mult).then_inc(st_chain, 1)
                        at_least(dve, st_chain, i + 1)
                        dve.scalar_tensor_tensor(state[:, :, :].rearrange("p a b -> p (a b)"),
                                                 state[:, :, :].rearrange("p a b -> p (a b)"), keep, stmp[:, :],
                                                 ALU.mult, ALU.add).then_inc(st_ready, 1)

                pipeline(dve, NT, LD, step)


def route_and_dispatch(nc, core, logits, name):
    NT, NE, CAP = core.NT, core.NE, core.CAP
    SLOTS = NE * CAP
    cst, xn = core.cst, core.xn
    with ExitStack() as stack:
        B = Buffers(nc, stack)
        wide = [P, NT, NE]
        key = B.sb(name + "r_key", wide)
        eq = B.sb(name + "r_eq", wide)
        rest = B.sb(name + "r_rest", wide)
        hot = B.sb(name + "r_hot", [P, 2, NT, NE])
        hot_pad = B.sb(name + "r_hot_pad", [P, NE + NT * NE], BF16)
        hot_sum = hot_pad[:, NE:NE + NT * NE]
        strict = B.sb(name + "r_strict", [P, P], BF16)
        ones = B.sb(name + "r_ones", [P, P], BF16)
        top = B.sb(name + "r_top", [P, 2, NT])
        which = B.sb(name + "r_which", [P, 2, NT])
        pos = B.sb(name + "r_pos", [P, 2, NT])
        kept = B.sb(name + "r_kept", [P, 2, NT])
        gate = B.sb(name + "r_gate", [P, 2, NT])
        tmp = B.sb(name + "r_tmp", [P, 2, NT])
        total = B.sb(name + "r_total", [P, NT])
        scatter_at = B.sb(name + "r_scatter_at", [P, 2 * NT], I32)
        counts = core.bank[0]

        chain = B.sem(name + "r_chain")
        gap_ready = B.sem(name + "r_gap_ready")
        exp_ready = B.sem(name + "r_exp_ready")
        hot_ready = B.sem(name + "r_hot_ready")
        counts_psum = B.sem(name + "r_counts_psum")
        slots_ready = B.sem(name + "r_slots_ready")
        scattered = B.sem(name + "r_scattered")

        with nc.Block() as block:

            @block.vector
            def _(dve):
                n = [0]

                def link(ins):
                    n[0] += 1
                    ins.then_inc(chain, 1)
                    dve.wait_ge(chain, n[0])

                iota = cst[:, C_IOTA:C_IOTA + NE].unsqueeze(1).to_broadcast(wide)
                dve.tensor_copy(strict[:, :], cst[:, C_STRICT:C_STRICT + P])
                dve.memset(ones[:, :], 1.0)
                dve.memset(hot_pad[:, 0:NE], 0.0)
                scores = logits[:, :, :]
                for r in range(2):
                    link(dve.tensor_reduce(top[:, r, :], scores, AX_X, ALU.max))
                    link(dve.tensor_tensor(eq[:, :, :], scores, top[:, r, :].unsqueeze(2).to_broadcast(wide), ALU.is_equal))
                    link(dve.scalar_tensor_tensor(key[:, :, :], eq[:, :, :], -float(NE), iota, ALU.mult, ALU.add))
                    link(dve.tensor_reduce(which[:, r, :], key[:, :, :], AX_X, ALU.min))
                    link(dve.tensor_tensor(hot[:, r, :, :], key[:, :, :], which[:, r, :].unsqueeze(2).to_broadcast(wide), ALU.is_equal))
                    if r == 0:
                        link(dve.scalar_tensor_tensor(rest[:, :, :], hot[:, 0, :, :], -3.0e38, scores, ALU.mult, ALU.add))
                        scores = rest[:, :, :]
                link(dve.tensor_tensor(hot_sum.rearrange("p (t e) -> p t e", e=NE), hot[:, 0, :, :], hot[:, 1, :, :], ALU.add))
                dve.tensor_tensor(tmp[:, 0, :], top[:, 1, :], top[:, 0, :], ALU.subtract).then_inc(gap_ready, 1)
                dve.wait_ge(exp_ready, 1)
                link(dve.tensor_scalar(total[:, :], tmp[:, 1, :], 1.0, None, ALU.add))
                link(dve.reciprocal(gate[:, 0, :], total[:, :]))
                link(dve.tensor_tensor(gate[:, 1, :], gate[:, 0, :], tmp[:, 1, :], ALU.mult))
                dve.wait_ge(counts_psum, 1)
                for r in range(2):
                    link(dve.tensor_tensor(key[:, :, :], hot[:, r, :, :], counts[:, 0:NT * NE].rearrange("p (t e) -> p t e", e=NE), ALU.mult))
                    link(dve.tensor_reduce(pos[:, r, :], key[:, :, :], AX_X, ALU.add))
                link(dve.tensor_scalar(kept[:, :, :], pos[:, :, :], float(CAP), None, ALU.is_lt))
                link(dve.scalar_tensor_tensor(pos[:, :, :], which[:, :, :], float(CAP), pos[:, :, :], ALU.mult, ALU.add))
                trash = cst[:, C_TRASH:C_TRASH + 2 * NT].rearrange("p (r t) -> p r t", r=2)
                link(dve.tensor_tensor(tmp[:, :, :], pos[:, :, :], trash, ALU.subtract))
                link(dve.tensor_tensor(tmp[:, :, :], tmp[:, :, :], kept[:, :, :], ALU.mult))
                link(dve.tensor_tensor(tmp[:, :, :], tmp[:, :, :], trash, ALU.add))
                dve.tensor_scalar(scatter_at[:, :].rearrange("p (r t) -> p r t", r=2), tmp[:, :, :], float(SLOTS), None,
                                  ALU.add).then_inc(slots_ready, 1)
                link(dve.scalar_tensor_tensor(core.gather_at[:, :].rearrange("p (r t) -> p r t", r=2), pos[:, :, :],
                                              float(SLOTS), kept[:, :, :], ALU.add, ALU.mult))
                link(dve.tensor_tensor(gate[:, :, :], gate[:, :, :], kept[:, :, :], ALU.mult))
                link(dve.tensor_tensor(total[:, :], gate[:, 0, :], gate[:, 1, :], ALU.add))
                link(dve.tensor_scalar(total[:, :], total[:, :], 1e-9, None, ALU.add))
                link(dve.reciprocal(total[:, :], total[:, :]))
                link(dve.tensor_tensor(core.weight[:, :, :], gate[:, :, :], total[:, :].unsqueeze(1).to_broadcast([P, 2, NT]), ALU.mult))

            @block.scalar
            def _(act):
                act.wait_ge(gap_ready, 1)
                act.activation(tmp[:, 1, :], tmp[:, 0, :], ACT.Exp).then_inc(exp_ready, 1)

            @block.tensor
            def _(pe):
                pe.wait_ge(gap_ready, 1)
                pe.matmul(counts[:, 0:NT * NE], strict[:, :], hot_sum, start=True, stop=False)
                for back in range(2, NT):
                    pe.matmul(counts[:, NE * back:NE * NT], ones[:, :], hot_pad[:, NE:NE + NE * (NT - back)],
                              start=False, stop=False, skip_group_check=True)
                pe.matmul(counts[:, 0:NE * NT], ones[:, :], hot_pad[:, 0:NE * NT], start=False, stop=True).then_inc(counts_psum, 1)

            @block.gpsimd
            def _(pool):
                pool.wait_ge(core.zeroed, 16)
                pool.wait_ge(slots_ready, 1)
                for j in range(2 * NT):
                    pool.indirect_dma_start(
                        out=core.slots_dram[:, :], out_offset=bass.IndirectOffsetOnAxis(ap=scatter_at[:, j:j + 1], axis=0),
                        in_=xn[:, j % NT, :], in_offset=None).then_inc(scattered, 16)
                pool.wait_ge(scattered, 16 * 2 * NT)


def experts(nc, core, w1, b1, w2, b2, name):
    NE, CAP = core.NE, core.CAP
    D, F = w1.shape[1], w1.shape[2]
    KD, KF, TS = D // P, F // P, CAP // P
    HALF = CAP // 2
    LT, LM = 0, 1
    with ExitStack() as stack:
        B = Buffers(nc, stack)
        w1b = B.sb(name + "e_w1", [P, 2, KD, F])
        w2b = B.sb(name + "e_w2", [P, 2, KF, D])
        b1b = B.sb(name + "e_b1", [P, 2, KF])
        b2b = B.sb(name + "e_b2", [P, 2, D])
        tok = B.sb(name + "e_tok", [P, 2, TS, D])
        tokT = B.sb(name + "e_tokT", [P, 2, KD, CAP])
        hT = B.sb(name + "e_hT", [P, KF, CAP])
        y = B.sb(name + "e_y", [P, 2, TS, D])
        psum, bank = core.psum, core.bank

        w_loaded = [B.sem(f"{name}e_w_loaded{u}") for u in range(2)]
        tok_loaded = [B.sem(f"{name}e_tok_loaded{u}") for u in range(2)]
        tokT_psum = B.sem(name + "e_tokT_psum")
        tokT_ready = B.sem(name + "e_tokT_ready")
        h_psum = B.sem(name + "e_h_psum")
        h_ready = B.sem(name + "e_h_ready")
        y_psum = B.sem(name + "e_y_psum")
        y_ready = B.sem(name + "e_y_ready")
        y_stored = [B.sem(f"{name}e_y_stored{u}") for u in range(2)]
        ident = core.cst[:, C_IDENT:C_IDENT + P]
        T_GROUPS = [(6, [(0, 0, 4)]), (7, [(1, 0, 4)]), (6, [(0, 4, TS - 4), (1, 4, TS - 4)])]

        def turns(eng, depth, step):
            first = 2
            for it in range(first):
                step(it, it % 2, it // 2, lambda lag, it=it: 0 <= it - lag < NE)
            with eng.Fori(first // 2, NE // 2) as turn:
                for u in range(2):
                    step(2 * turn + u, u, turn, lambda lag: True)
            for it in range(NE, NE + depth):
                step(it, it % 2, it // 2, lambda lag, it=it: 0 <= it - lag < NE)

        with nc.Block() as block:

            @block.sync
            def _(sp):
                def step(it, u, turn, live):
                    if live(0):
                        e = it
                        at_least(sp, y_ready, TS * (e - 1))
                        sp.dma_start(tok[:, u, :, :], core.slots_dram[bass.ds(e * CAP, CAP), :].rearrange("(p t) d -> p t d", t=TS)).then_inc(tok_loaded[u], 16)
                        sp.dma_start(w1b[:, u, :, :], w1[bass.ds(e, 1), :, :].rearrange("o (k p) f -> p (o k) f", p=P)).then_inc(w_loaded[u], 16)
                        sp.dma_start(b1b[:, u, :], b1[bass.ds(e, 1), :, :].rearrange("o p c -> (o p) c")).then_inc(w_loaded[u], 16)
                        sp.dma_start(w2b[:, u, :, :], w2[bass.ds(e, 1), :, :].rearrange("o (c p) d -> p (o c) d", p=P)).then_inc(w_loaded[u], 16)
                        sp.dma_start(b2b[:, u, :], b2[bass.ds(e, 1), :].to_broadcast([P, D])).then_inc(w_loaded[u], 16)
                    if live(2):
                        e = it - 2
                        at_least(sp, y_ready, TS * (e + 1))
                        sp.dma_start(core.expert_out[bass.ds(e * CAP, CAP), :].rearrange("(p t) d -> p t d", t=TS), y[:, u, :, :]).then_inc(y_stored[u], 16)

                turns(sp, 2, step)
                for u in range(2):
                    sp.wait_ge(y_stored[u], 16 * (NE // 2))

            @block.tensor
            def _(pe):
                def step(it, u, turn, live):
                    if live(LM):
                        e, v = it - LM, 1 - u
                        before = turn - 1 if u == 0 else turn
                        pe.wait_ge(w_loaded[v], 64 * (before + 1))
                        pe.wait_ge(tokT_ready, 3 * (e + 1))
                        for c in range(KF):
                            at_least(pe, h_ready, KF * e + c - 1)
                            for half in range(2):
                                for k in range(KD):
                                    ins = pe.matmul(bank[2 * (c % 2) + half][:, 0:HALF], w1b[:, v, k, P * c:P * c + P],
                                                    tokT[:, v, k, HALF * half:HALF * half + HALF],
                                                    start=(k == 0), stop=(k == KD - 1))
                            ins.then_inc(h_psum, 1)
                    if live(LT):
                        e = it
                        pe.wait_ge(tok_loaded[u], 16 * (turn + 1))
                        for n, (b, runs) in enumerate(T_GROUPS):
                            at_least(pe, tokT_ready, 3 * e + n - 1 if n != 1 else 3 * e - 1)
                            at = 0
                            for k, t0, m in runs:
                                for t in range(t0, t0 + m):
                                    ins = pe.transpose(bank[b][:, at:at + P], tok[:, u, t, P * k:P * k + P], ident)
                                    at += P
                            ins.then_inc(tokT_psum, 1)
                    if live(LM):
                        e, v = it - LM, 1 - u
                        pe.wait_ge(h_ready, KF * (e + 1))
                        for t in range(TS):
                            at_least(pe, y_ready, TS * e + max(t - 1, 0))
                            for c in range(KF):
                                ins = pe.matmul(bank[4 + t % 2][:, 0:D], hT[:, c, P * t:P * t + P], w2b[:, v, c, :],
                                                start=(c == 0), stop=(c == KF - 1))
                            ins.then_inc(y_psum, 1)

                turns(pe, 1, step)

            @block.scalar
            def _(act):
                def step(it, u, turn, live):
                    e, v = it, u
                    act.wait_ge(w_loaded[v], 64 * (turn + 1))
                    at_least(act, y_psum, TS * e)
                    for c in range(KF):
                        act.wait_ge(h_psum, KF * e + c + 1)
                        act.activation(hT[:, c, :].rearrange("p (a b) -> p a b", a=2), psum[:, 2 * (c % 2):2 * (c % 2) + 2, 0:HALF],
                                       ACT.Gelu, bias=b1b[:, v, c:c + 1]).then_inc(h_ready, 1)

                turns(act, 0, step)

            @block.vector
            def _(dve):
                def step(it, u, turn, live):
                    if live(LT):
                        e = it
                        at_least(dve, h_psum, KF * (e - 1))
                        for n, (b, runs) in enumerate(T_GROUPS):
                            dve.wait_ge(tokT_psum, 3 * e + n + 1)
                            k0, t0, m = runs[0]
                            if len(runs) == 1:
                                dve.tensor_copy(tokT[:, u, k0, P * t0:P * (t0 + m)], bank[b][:, 0:P * m]).then_inc(tokT_ready, 1)
                            else:
                                dve.tensor_copy(tokT[:, u, :, P * t0:P * (t0 + m)],
                                                bank[b][:, 0:KD * P * m].rearrange("p (k s) -> p k s", k=KD)).then_inc(tokT_ready, 1)
                    if live(LM):
                        e, v = it - LM, 1 - u
                        before = turn - 1 if u == 0 else turn
                        at_least(dve, y_stored[v], 16 * before)
                        for t in range(TS):
                            dve.wait_ge(y_psum, TS * e + t + 1)
                            dve.tensor_tensor(y[:, v, t, :], bank[4 + t % 2][:, 0:D], b2b[:, v, :], ALU.add).then_inc(y_ready, 1)

                turns(dve, 1, step)


def combine(nc, core, out, name):
    NT, x = core.NT, core.x
    R = 4
    with ExitStack() as stack:
        B = Buffers(nc, stack)
        rows = B.sb(name + "c_rows", [P, R, 2, 256])
        fetched = [B.sem(f"{name}c_fetched{u}") for u in range(R)]
        added = B.sem(name + "c_added")
        stored = B.sem(name + "c_stored")
        with nc.Block() as block:

            @block.gpsimd
            def _(pool):
                for i in range(NT):
                    at_least(pool, added, 2 * (i - R + 1))
                    for r in range(2):
                        pool.indirect_dma_start(
                            out=rows[:, i % R, r, :], out_offset=None, in_=core.expert_out[:, :],
                            in_offset=bass.IndirectOffsetOnAxis(ap=core.gather_at[:, r * NT + i:r * NT + i + 1], axis=0),
                        ).then_inc(fetched[i % R], 16)

            @block.vector
            def _(dve):
                with dve.Fori(0, NT // R) as turn:
                    for u in range(R):
                        i = R * turn + u
                        dve.wait_ge(fetched[u], 32 * (turn + 1))
                        for r in range(2):
                            if r == 1:
                                dve.wait_ge(added, 2 * i + 1)
                            dve.scalar_tensor_tensor(x[:, i, :], rows[:, u, r, :], core.weight[:, r, bass.ds(i, 1)], x[:, i, :],
                                                     ALU.mult, ALU.add).then_inc(added, 1)

            if out is not None:
                @block.sync
                def _(sp):
                    with sp.Fori(0, NT // R) as turn:
                        sp.wait_ge(added, 2 * R * (turn + 1))
                        sp.dma_start(out[bass.ds(turn * R * P, R * P), :].rearrange("(t p) d -> p t d", p=P),
                                     x[:, bass.ds(turn * R, R), :]).then_inc(stored, 16)
                    sp.wait_ge(stored, 16 * (NT // R))


def nystrom_attention(nc, core, wqkT, wvT, woT, bqk, bv, bo, rwT, rb, logits):
    x, xn_all, cst, NT = core.x, core.xn, core.cst, core.NT
    KD, BT = 2, 8
    NB = NT // BT
    PR = 8
    ITERS = 6
    SIM1, SIM2, SIM3 = 1.0 / 64, 1.0 / 1024, 1.0 / 64
    with ExitStack() as stack:
        B = Buffers(nc, stack)
        wqk = B.sb("n_wqk", [P, KD, 512])
        wv = B.sb("n_wv", [P, KD, 256])
        wo = B.sb("n_wo", [P, KD, 256])
        rw = B.sb("n_rw", [P, KD, 16])
        bias_qk = B.sb("n_bias_qk", [P, 4])
        bias_v = B.sb("n_bias_v", [P, 256])
        bias_o = B.sb("n_bias_o", [P, 256])
        bias_r = B.sb("n_bias_r", [P, 16])
        tick = B.sb("n_tick", [P, 2])
        stats = B.sb("n_stats", [P, 6])
        mv = B.sb("n_mv", [P, 2])
        rstd = B.sb("n_rstd", [P, 1])
        xln = B.sb("n_xln", [P, 2, 256])
        xlnT = B.sb("n_xlnT", [P, 2, KD, P])
        q_next = B.sb("n_q_next", [P, KD, BT * P])
        qT = B.sb("n_qT", [P, KD, BT * P])
        kT = B.sb("n_kT", [P, KD, BT * P])
        v = B.sb("n_v", [P, BT, 256])
        q_sum = B.sb("n_q_sum", [P, KD, 64])
        k_sum = B.sb("n_k_sum", [P, KD, 64])
        q_blk = B.sb("n_q_blk", [P, KD, 8, 64])
        k_blk = B.sb("n_k_blk", [P, KD, 8, 64])
        e3 = B.sb("n_e3", [P, 2, BT * P])
        e3T = B.sb("n_e3T", [P, 2, BT, P])
        max3 = B.sb("n_max3", [P, PR])
        neg3 = B.sb("n_neg3", [P, PR])
        sum3 = B.sb("n_sum3", [P, PR])
        rec3 = B.sb("n_rec3", [P, PR])
        max2 = B.sb("n_max2", [P, PR])
        sum2 = B.sb("n_sum2", [P, PR])
        s2 = B.sb("n_s2", [P, PR, 64])
        pw = B.sb("n_pw", [P, PR, 80])
        p_blk = B.sb("n_p_blk", [P, PR, P])
        q1 = B.sb("n_q1", [P, PR, 64])
        q2 = B.sb("n_q2", [P, PR, 64])
        q3 = B.sb("n_q3", [P, PR, 64])
        q3_blk = B.sb("n_q3_blk", [P, PR, P])
        z_blk = B.sb("n_z_blk", [P, PR, 34])
        max1 = B.sb("n_max1", [P, 2, 8])
        s1 = B.sb("n_s1", [P, 2, 8, 64])
        e1 = B.sb("n_e1", [P, 2, 16, 64])
        e1T = B.sb("n_e1T", [P, PR, P])
        den = B.sb("n_den", [P, 16])
        o = B.sb("n_o", [P, 2, 256])
        oT = B.sb("n_oT", [P, KD, P])
        stats2 = B.sb("n_stats2", [P, 6])
        mv2 = B.sb("n_mv2", [P, 2])
        rstd2 = B.sb("n_rstd2", [P, 1])
        xr = B.sb("n_xr", [P, 2, 256])
        xrT = B.sb("n_xrT", [P, KD, P])
        psum, bank = core.psum, core.bank

        names = ("loaded made ln_chain rstd_ready xln_ready xlnT_psum xlnT_ready qk_psum v_psum qk_ready v_ready sums_ready "
                 "q_moved q_blk_ready k_blk_ready s2_psum s2_chain s2_shifted e2_ready k_ready kT_psum kT_ready kT_blk_ready "
                 "s3_psum s3_chain neg3_ready e3_ready e3T_psum e3Ta_ready e3Tb_ready b3_psum b3_chain w_ready "
                 "xa_psum xb_psum xa_read xb_read ya_psum yb_psum ya_read yb_read "
                 "s1_psum s1_chain s1_shifted e1_ready e1T_psum e1Ta_ready e1Tb_ready o_psum o_chain o_ready oT_psum oT_ready "
                 "y_psum x_chain r_rstd xr_ready xr_kept xrT_psum xrT_ready logits_psum logits_read").split()
        S = {name: B.sem("n_" + name) for name in names}
        ident = cst[:, C_IDENT:C_IDENT + P]
        eye = [cst[:, C_EYE7 + 64 * n:C_EYE7 + 64 * n + 64].unsqueeze(1).to_broadcast([P, 4, 64]) for n in range(3)]
        TOP, LOW = slice(0, 64), slice(64, P)

        X_PER, Y_PER = 1 + 3 * ITERS - 1, 1 + ITERS

        def x_count(b, n, what):
            return X_PER * b + (1 if n < 0 else 1 + 3 * n + what + 1)

        def y_count(b, n):
            return Y_PER * b + n + 2

        def schedule(more):
            tiles = 0
            for n in range(-1, ITERS):
                for what in ((2,) if n < 0 else (0, 1, 2)):
                    for group in range(2):
                        yield "inverse", (n, what, group)
                if more and tiles < BT and n >= 0:
                    for _ in range(2 if n < 2 else 1):
                        if tiles < BT:
                            yield "project", tiles
                            tiles += 1
            while more and tiles < BT:
                yield "project", tiles
                tiles += 1

        def batches(eng, project, pairs, inverse, rows):
            for t in range(BT):
                project(0, t)

            def body(b, more):
                pairs(b)
                for kind, what in schedule(more):
                    if kind == "project":
                        project(b + 1, what)
                    else:
                        inverse(b, *what)
                rows(b)

            with eng.Fori(0, NB - 1) as b:
                body(b, True)
            body(NB - 1, False)

        with nc.Block() as block:

            @block.sync
            def _(sp):
                for dst, src in ((wqk, wqkT), (wv, wvT), (wo, woT), (rw, rwT)):
                    sp.dma_start(dst[:, :, :], src.rearrange("(k p) n -> p k n", p=P)).then_inc(S["loaded"], 16)
                sp.dma_start(bias_qk[:, :], bqk.rearrange("(g p) -> p g", p=P), allow_slow_non_contiguous=True).then_inc(S["loaded"], 16)
                sp.dma_start(bias_v[:, :], bv[None, :].to_broadcast([P, 256])).then_inc(S["loaded"], 16)
                sp.dma_start(bias_o[:, :], bo[None, :].to_broadcast([P, 256])).then_inc(S["loaded"], 16)
                sp.dma_start(bias_r[:, :], rb[None, :].to_broadcast([P, 16])).then_inc(S["loaded"], 16)

            @block.gpsimd
            def _(pool):
                pool.memset(p_blk[:, :, :], 0.0).then_inc(S["made"], 1)
                pool.memset(q3_blk[:, :, :], 0.0).then_inc(S["made"], 1)
                pool.memset(z_blk[:, :, :], 0.0).then_inc(S["made"], 1)
                pool.wait_ge(S["made"], 3)
                pool.memset(z_blk[TOP, :, 16:17], 1.0).then_inc(S["made"], 1)
                pool.memset(z_blk[LOW, :, 33:34], 1.0).then_inc(S["made"], 1)

                def project(b, t):
                    i = BT * b + t
                    pool.wait_ge(S["ln_chain"], 3 * i + 3)
                    pool.tensor_tensor(rstd[:, :], mv[:, 1:2], core.minus_half[:, :], ALU.pow).then_inc(S["rstd_ready"], 1)

                def pairs(b):
                    pool.wait_ge(S["qk_ready"], BT * b + BT)
                    at_least(pool, S["s1_psum"], 2 * BT * b)
                    pool.wait_ge(S["sums_ready"], 2 * BT * b + 2 * BT)
                    for k in range(KD):
                        ins = pool.tensor_tensor(k_blk[:, k, :, :], k_sum[:, k:k + 1, :].to_broadcast([P, 8, 64]),
                                                 cst[:, C_HEAD8:C_HEAD8 + 8].unsqueeze(2).to_broadcast([P, 8, 64]), ALU.mult)
                    ins.then_inc(S["k_blk_ready"], 1)
                    pool.tensor_copy(qT[:, :, :], q_next[:, :, :]).then_inc(S["q_moved"], 1)

                def inverse(b, n, what, group):
                    pass

                def rows(b):
                    for step in range(BT + 3):
                        if 0 <= step - 2 < BT:
                            i = BT * b + step - 2
                            pool.wait_ge(S["x_chain"], 5 * i + 5)
                            pool.tensor_tensor(rstd2[:, :], mv2[:, 1:2], core.minus_half[:, :], ALU.pow).then_inc(S["r_rstd"], 1)
                            pool.wait_ge(S["xr_ready"], i + 1)
                            pool.tensor_copy(xn_all[:, i, :], xr[:, step % 2, :]).then_inc(S["xr_kept"], 1)

                batches(pool, project, pairs, inverse, rows)

            @block.scalar
            def _(act):
                act.wait_ge(S["loaded"], 16 * 8)
                act.wait_ge(S["made"], 5)

                def project(b, t):
                    i = BT * b + t
                    act.wait_ge(S["xlnT_psum"], i + 1)
                    at_least(act, S["v_psum"], i - 1)
                    act.activation(xlnT[:, t % 2, :, :], bank[4][:, 0:256].rearrange("p (k t) -> p k t", k=KD), ACT.Copy).then_inc(S["xlnT_ready"], 1)
                    act.wait_ge(S["qk_psum"], i + 1)
                    if t == 0:
                        at_least(act, S["q_moved"], b)
                        at_least(act, S["s3_psum"], PR * b)
                    for g in range(4):
                        dst = (q_next, kT)[g // 2]
                        ins = act.activation(dst[:, g % 2, P * t:P * t + P], bank[5][:, P * g:P * g + P], ACT.Identity, bias=bias_qk[:, g:g + 1])
                    ins.then_inc(S["qk_ready"], 1)

                def pairs(b):
                    act.wait_ge(S["s2_shifted"], b + 1)
                    act.activation(s2[:, :, :], s2[:, :, :], ACT.Exp, scale=SIM2).then_inc(S["e2_ready"], 1)
                    for step in range(PR + 1):
                        if step < PR:
                            n = PR * b + step
                            act.wait_ge(S["neg3_ready"], n + 1)
                            at_least(act, S["e3T_psum"], 2 * (PR * b + max(step - 1, 0)))
                            act.activation(e3[:, step % 2, :].rearrange("p (a s) -> p a s", a=2),
                                           psum[:, 2 * (step % 2):2 * (step % 2) + 2, :], ACT.Exp, scale=SIM3,
                                           bias=neg3[:, step:step + 1], accum_out=sum3[:, step:step + 1]).then_inc(S["e3_ready"], 1)
                        if step >= 1:
                            n, u = PR * b + step - 1, (step - 1) % 2
                            act.wait_ge(S["e3T_psum"], 2 * n + 1)
                            at_least(act, S["b3_psum"], PR * b + max(step - 2, 0))
                            act.activation(e3T[:, u, 0:4, :], bank[4][:, :].rearrange("p (a s) -> p a s", a=4), ACT.Copy).then_inc(S["e3Ta_ready"], 1)
                    act.wait_ge(S["kT_psum"], 2 * b + 2)
                    for half in range(2):
                        src = bank[4 + half][:, :].rearrange("p (a s) -> p a s", a=4)
                        act.activation(q3_blk[TOP, 4 * half:4 * half + 4, 0:64], src[TOP, :, 0:64], ACT.Copy)
                        act.activation(q3_blk[LOW, 4 * half:4 * half + 4, 64:P], src[LOW, :, 64:P], ACT.Copy).then_inc(S["kT_blk_ready"], 1)

                def inverse(b, n, what, group):
                    if what != 2:
                        return
                    g4 = slice(4 * group, 4 * group + 4)
                    scale = 1.0 if n < 0 else 0.25
                    y = bank[1 + 2 * group][:, 0:320].rearrange("p (a c) -> p a c", a=4)
                    act.wait_ge(S["y%s_psum" % "ab"[group]], y_count(b, n))
                    if n == ITERS - 1:
                        at_least(act, S["o_psum"], BT * b)
                        act.activation(z_blk[TOP, g4, 0:16], y[TOP, :, 64:80], ACT.Copy, scale=scale)
                        act.activation(z_blk[LOW, g4, 17:33], y[LOW, :, 64:80], ACT.Copy, scale=scale).then_inc(S["y%s_read" % "ab"[group]], 1)
                        return
                    act.wait_ge(S["x%s_psum" % "ab"[group]], x_count(b, n, 2))
                    act.activation(p_blk[TOP, g4, 0:64], y[TOP, :, 0:64], ACT.Copy, scale=scale)
                    act.activation(p_blk[LOW, g4, 64:P], y[LOW, :, 0:64], ACT.Copy, scale=scale)
                    act.activation(pw[:, g4, :], y[:, :, :], ACT.Copy, scale=scale).then_inc(S["y%s_read" % "ab"[group]], 1)

                def rows(b):
                    for step in range(BT + 3):
                        if step < BT:
                            for half in range(2):
                                n = 2 * (BT * b + step) + half
                                act.wait_ge(S["s1_shifted"], n + 1)
                                at_least(act, S["e1T_psum"], 2 * (BT * b + max(step - 1, 0)))
                                act.activation(e1[:, step % 2, 8 * half:8 * half + 8, :], s1[:, half, :, :], ACT.Exp, scale=SIM1).then_inc(S["e1_ready"], 1)
                        if 0 <= step - 1 < BT:
                            i = BT * b + step - 1
                            act.wait_ge(S["e1T_psum"], 2 * i + 1)
                            at_least(act, S["o_psum"], i)
                            act.activation(e1T[:, 0:4, :], bank[2][:, :].rearrange("p (a s) -> p a s", a=4), ACT.Copy).then_inc(S["e1Ta_ready"], 1)
                        if 0 <= step - 2 < BT:
                            i = BT * b + step - 2
                            act.wait_ge(S["oT_psum"], i + 1)
                            at_least(act, S["y_psum"], i)
                            act.activation(oT[:, :, :], bank[5][:, 0:256].rearrange("p (k t) -> p k t", k=KD), ACT.Copy).then_inc(S["oT_ready"], 1)
                        if 0 <= step - 3 < BT:
                            i = BT * b + step - 3
                            act.wait_ge(S["xrT_psum"], i + 1)
                            at_least(act, S["logits_psum"], i)
                            act.activation(xrT[:, :, :], bank[6][:, 0:256].rearrange("p (k t) -> p k t", k=KD), ACT.Copy).then_inc(S["xrT_ready"], 1)

                batches(act, project, pairs, inverse, rows)

            @block.tensor
            def _(pe):
                pe.wait_ge(S["loaded"], 16 * 8)
                pe.wait_ge(S["made"], 5)

                def project(b, t):
                    i, u = BT * b + t, t % 2
                    pe.wait_ge(S["xln_ready"], i + 1)
                    at_least(pe, S["xlnT_ready"], i)
                    for k in range(KD):
                        ins = pe.transpose(bank[4][:, P * k:P * k + P], xln[:, u, P * k:P * k + P], ident)
                    ins.then_inc(S["xlnT_psum"], 1)
                    pe.wait_ge(S["xlnT_ready"], i + 1)
                    at_least(pe, S["qk_ready"], i)
                    for g in range(4):
                        for k in range(KD):
                            ins = pe.matmul(bank[5][:, P * g:P * g + P], wqk[:, k, P * g:P * g + P], xlnT[:, u, k, :],
                                            start=(k == 0), stop=(k == KD - 1))
                    ins.then_inc(S["qk_psum"], 1)
                    at_least(pe, S["v_ready"], i)
                    for k in range(KD):
                        ins = pe.matmul(bank[6][:, 0:256], xlnT[:, u, k, :], wv[:, k, :], start=(k == 0), stop=(k == KD - 1))
                    ins.then_inc(S["v_psum"], 1)

                def pairs(b):
                    pe.wait_ge(S["q_blk_ready"], b + 1)
                    at_least(pe, S["logits_read"], BT * b)
                    for pr in range(PR):
                        ins = pe.matmul(bank[7][:, 64 * pr:64 * pr + 64], q_blk[:, pr // 4, 2 * (pr % 4):2 * (pr % 4) + 2, :],
                                        k_sum[:, pr // 4, :], start=True, stop=True)
                    ins.then_inc(S["s2_psum"], 1)
                    for step in range(PR + 2):
                        if step < PR:
                            n, pr = PR * b + step, step
                            at_least(pe, S["e3_ready"], PR * b + max(step - 1, 0))
                            for c in range(2):
                                ins = pe.matmul(bank[2 * (step % 2) + c][:, :], q_blk[:, pr // 4, 2 * (pr % 4):2 * (pr % 4) + 2, :],
                                                kT[:, pr // 4, 512 * c:512 * c + 512], start=True, stop=True)
                            ins.then_inc(S["s3_psum"], 1)
                        if step >= 2:
                            n, pr, u = PR * b + step - 2, step - 2, step % 2
                            pe.wait_ge(S["e3Ta_ready"], n + 1)
                            pe.wait_ge(S["e3Tb_ready"], n + 1)
                            for s in range(BT):
                                ins = pe.matmul(bank[6][:, 32 * pr:32 * pr + 32], e3T[:, u, s, :], v[:, s, 32 * pr:32 * pr + 32],
                                                start=(s == 0), stop=(s == BT - 1))
                            ins.then_inc(S["b3_psum"], 1)
                        if 1 <= step <= PR:
                            n, u = PR * b + step - 1, (step - 1) % 2
                            pe.wait_ge(S["e3_ready"], n + 1)
                            for c in range(2):
                                at_least(pe, S["e3T%s_ready" % "ab"[c]], n)
                                for s in range(4 * c, 4 * c + 4):
                                    ins = pe.transpose(bank[4 + c][:, P * (s % 4):P * (s % 4) + P], e3[:, u, P * s:P * s + P], ident)
                                ins.then_inc(S["e3T_psum"], 1)
                    pe.wait_ge(S["k_ready"], b + 1)
                    for half in range(2):
                        at_least(pe, S["e3T%s_ready" % "ab"[half]], PR * b + PR)
                        for pr in range(4 * half, 4 * half + 4):
                            ins = pe.transpose(bank[4 + half][:, P * (pr % 4):P * (pr % 4) + P], p_blk[:, pr, :], ident)
                        ins.then_inc(S["kT_psum"], 1)

                def inverse(b, n, what, group):
                    ab = "ab"[group]
                    xb, yb = bank[2 * group], bank[1 + 2 * group]
                    xs, ys = S["x%s_psum" % ab], S["y%s_psum" % ab]
                    g4 = range(4 * group, 4 * group + 4)
                    if n < 0:
                        pe.wait_ge(S["kT_blk_ready"], 2 * b + 2)
                        pe.wait_ge(S["kT_ready"], b + 1)
                        pe.wait_ge(S["w_ready"], b + 1)
                    else:
                        pe.wait_ge(S["x%s_read" % ab], x_count(b, n, what - 1) if what else x_count(b, n - 1, 2))
                        if what == 0:
                            pe.wait_ge(S["y%s_read" % ab], y_count(b, n - 1))
                    if what < 2:
                        for pr in g4:
                            ins = pe.matmul(xb[:, 64 * (pr % 4):64 * (pr % 4) + 64], p_blk[:, pr, :], (q1, q2)[what][:, pr, :],
                                            start=True, stop=True)
                        ins.then_inc(xs, 1)
                        return
                    lo = 0 if n < ITERS - 1 else 64
                    for pr in g4:
                        ins = pe.matmul(yb[:, 80 * (pr % 4) + lo:80 * (pr % 4) + 80], q3_blk[:, pr, :], pw[:, pr, lo:80],
                                        start=True, stop=True)
                    ins.then_inc(ys, 1)
                    if n < ITERS - 1:
                        for pr in g4:
                            ins = pe.matmul(xb[:, 64 * (pr % 4):64 * (pr % 4) + 64], p_blk[:, pr, :], q3[:, pr, :],
                                            start=True, stop=True)
                        ins.then_inc(xs, 1)

                def rows(b):
                    for step in range(BT + 3):
                        if step < BT:
                            i = BT * b + step
                            if step == 0:
                                pe.wait_ge(S["q_moved"], b + 1)
                                pe.wait_ge(S["k_blk_ready"], b + 1)
                                for ab in "ab":
                                    pe.wait_ge(S["y%s_read" % ab], Y_PER * (b + 1))
                            for half in range(2):
                                at_least(pe, S["s1_shifted"], 2 * BT * b + max(2 * step + half - 1, 0))
                                pe.matmul(bank[half][:, :], qT[:, half, P * step:P * step + P], k_blk[:, half, :, :],
                                          start=True, stop=True).then_inc(S["s1_psum"], 1)
                        if 0 <= step - 2 < BT:
                            i, u = BT * b + step - 2, step % 2
                            pe.wait_ge(S["o_ready"], i + 1)
                            at_least(pe, S["x_chain"], 5 * BT * b + max(5 * (step - 3) + 1, 0))
                            for k in range(KD):
                                ins = pe.transpose(bank[5][:, P * k:P * k + P], o[:, u, P * k:P * k + P], ident)
                            ins.then_inc(S["oT_psum"], 1)
                        if 0 <= step - 3 < BT:
                            i, u = BT * b + step - 3, (step - 3) % 2
                            pe.wait_ge(S["xr_ready"], i + 1)
                            at_least(pe, S["logits_read"], i)
                            for k in range(KD):
                                ins = pe.transpose(bank[6][:, P * k:P * k + P], xr[:, u, P * k:P * k + P], ident)
                            ins.then_inc(S["xrT_psum"], 1)
                        if 0 <= step - 1 < BT:
                            i, u = BT * b + step - 1, (step - 1) % 2
                            pe.wait_ge(S["e1_ready"], 2 * i + 2)
                            for c in range(2):
                                at_least(pe, S["e1T%s_ready" % "ab"[c]], i)
                                for pr in range(4 * c, 4 * c + 4):
                                    ins = pe.transpose(bank[2 + c][:, P * (pr % 4):P * (pr % 4) + P], e1[:, u, 2 * pr:2 * pr + 2, :], ident)
                                ins.then_inc(S["e1T_psum"], 1)
                            at_least(pe, S["o_ready"], i)
                            for pr in range(PR):
                                if pr % 4 == 0:
                                    pe.wait_ge(S["e1T%s_ready" % "ab"[pr // 4]], i + 1)
                                ins = pe.matmul(bank[4][:, 34 * pr:34 * pr + 34], e1T[:, pr, :], z_blk[:, pr, :], start=True, stop=True)
                            ins.then_inc(S["o_psum"], 1)
                        if 0 <= step - 2 < BT:
                            i = BT * b + step - 2
                            pe.wait_ge(S["oT_ready"], i + 1)
                            for k in range(KD):
                                ins = pe.matmul(bank[5][:, 256:512], oT[:, k, :], wo[:, k, :], start=(k == 0), stop=(k == KD - 1))
                            ins.then_inc(S["y_psum"], 1)
                        if 0 <= step - 3 < BT:
                            i = BT * b + step - 3
                            pe.wait_ge(S["xrT_ready"], i + 1)
                            for k in range(KD):
                                ins = pe.matmul(bank[6][:, 256:272], xrT[:, k, :], rw[:, k, :], start=(k == 0), stop=(k == KD - 1))
                            ins.then_inc(S["logits_psum"], 1)

                batches(pe, project, pairs, inverse, rows)

            @block.vector
            def _(dve):
                dve.wait_ge(S["loaded"], 16 * 8)
                dve.wait_ge(S["made"], 5)

                def variance(src, st, m, chain, done):
                    dve.memset(tick[:, 0:1], 0.0)
                    dve.bn_stats(st, src).then_inc(chain, 1)
                    at_least(dve, chain, done + 1)
                    dve.memset(tick[:, 1:2], 0.0)
                    dve.bn_aggr(m, st).then_inc(chain, 1)
                    at_least(dve, chain, done + 2)
                    dve.tensor_scalar(m[:, 1:2], m[:, 1:2], LN_EPS, None, ALU.add).then_inc(chain, 1)

                def project(b, t):
                    i, u = BT * b + t, t % 2
                    at_least(dve, S["xln_ready"], i)
                    variance(x[:, i, :], stats[:, :], mv[:, :], S["ln_chain"], 3 * i)
                    dve.wait_ge(S["rstd_ready"], i + 1)
                    at_least(dve, S["xlnT_psum"], i - 1)
                    dve.tensor_scalar(xln[:, u, :], x[:, i, :], mv[:, 0:1], rstd[:, :], ALU.subtract, ALU.mult).then_inc(S["xln_ready"], 1)
                    dve.wait_ge(S["v_psum"], i + 1)
                    if t == 0:
                        at_least(dve, S["b3_psum"], PR * b)
                    dve.tensor_tensor(v[:, t, :], bank[6][:, 0:256], bias_v[:, :], ALU.add).then_inc(S["v_ready"], 1)
                    dve.wait_ge(S["qk_ready"], i + 1)
                    if t == 0:
                        at_least(dve, S["k_blk_ready"], b)
                        at_least(dve, S["s2_psum"], b)
                    for dst, src in ((q_sum, q_next), (k_sum, kT)):
                        dve.tensor_reduce(dst[:, :, 8 * t:8 * t + 8], src[:, :, P * t:P * t + P].rearrange("p k (j l) -> p k j l", l=16),
                                          AX_X, ALU.add).then_inc(S["sums_ready"], 1)

                def pairs(b):
                    dve.wait_ge(S["sums_ready"], 2 * BT * b + 2 * BT)
                    at_least(dve, S["s3_psum"], PR * b)
                    for k in range(KD):
                        ins = dve.tensor_tensor(q_blk[:, k, :, :], q_sum[:, k:k + 1, :].to_broadcast([P, 8, 64]),
                                                cst[:, C_HEAD8:C_HEAD8 + 8].unsqueeze(2).to_broadcast([P, 8, 64]), ALU.mult)
                    ins.then_inc(S["q_blk_ready"], 1)
                    s2_ps = bank[7][:, :].rearrange("p (a c) -> p a c", a=PR)
                    dve.wait_ge(S["s2_psum"], b + 1)
                    dve.tensor_reduce(max2[:, :], s2_ps, AX_X, ALU.max).then_inc(S["s2_chain"], 1)
                    dve.wait_ge(S["s2_chain"], 3 * b + 1)
                    dve.tensor_tensor(s2[:, :, :], s2_ps, max2[:, :].unsqueeze(2).to_broadcast([P, PR, 64]), ALU.subtract).then_inc(S["s2_shifted"], 1)
                    for step in range(PR + 1):
                        if step < PR:
                            n = PR * b + step
                            dve.wait_ge(S["s3_psum"], n + 1)
                            dve.tensor_reduce(max3[:, step:step + 1], psum[:, 2 * (step % 2):2 * (step % 2) + 2, :], AX_XY, ALU.max).then_inc(S["s3_chain"], 1)
                            dve.wait_ge(S["s3_chain"], n + 1)
                            at_least(dve, S["e3_ready"], PR * b)
                            dve.tensor_scalar(neg3[:, step:step + 1], max3[:, step:step + 1], -SIM3, None, ALU.mult).then_inc(S["neg3_ready"], 1)
                        if step >= 1:
                            n, u = PR * b + step - 1, (step - 1) % 2
                            dve.wait_ge(S["e3T_psum"], 2 * n + 2)
                            at_least(dve, S["b3_psum"], PR * b + max(step - 2, 0))
                            dve.tensor_copy(e3T[:, u, 4:8, :], bank[5][:, :].rearrange("p (a s) -> p a s", a=4)).then_inc(S["e3Tb_ready"], 1)
                        if step == 2:
                            dve.wait_ge(S["e2_ready"], b + 1)
                            dve.tensor_reduce(sum2[:, :], s2[:, :, :], AX_X, ALU.add).then_inc(S["s2_chain"], 1)
                            dve.wait_ge(S["s2_chain"], 3 * b + 2)
                            dve.reciprocal(max2[:, :], sum2[:, :]).then_inc(S["s2_chain"], 1)
                            dve.wait_ge(S["s2_chain"], 3 * b + 3)
                            rec2 = max2[:, :].unsqueeze(2).to_broadcast([P, PR, 64])
                            dve.tensor_tensor(pw[:, :, 0:64], s2[:, :, :], rec2, ALU.mult)
                            dve.tensor_tensor(p_blk[TOP, :, 0:64], s2[TOP, :, :], rec2[TOP], ALU.mult)
                            dve.tensor_tensor(p_blk[LOW, :, 64:P], s2[LOW, :, :], rec2[LOW], ALU.mult).then_inc(S["k_ready"], 1)
                    dve.wait_ge(S["e3_ready"], PR * b + PR)
                    dve.reciprocal(rec3[:, :], sum3[:, :]).then_inc(S["b3_chain"], 1)
                    dve.wait_ge(S["b3_psum"], PR * b + PR)
                    dve.wait_ge(S["b3_chain"], b + 1)
                    b3 = bank[6][:, 0:256].rearrange("p (a c) -> p a c", a=PR)
                    r3 = rec3[:, :].unsqueeze(2).to_broadcast([P, PR, 16])
                    dve.tensor_tensor(pw[TOP, :, 64:80], b3[TOP, :, 0:16], r3[TOP], ALU.mult)
                    dve.tensor_tensor(pw[LOW, :, 64:80], b3[LOW, :, 16:32], r3[LOW], ALU.mult).then_inc(S["w_ready"], 1)
                    dve.wait_ge(S["kT_blk_ready"], 2 * b + 2)
                    for half in range(2):
                        src = bank[4 + half][:, :].rearrange("p (a s) -> p a s", a=4)
                        dve.tensor_copy(q3[TOP, 4 * half:4 * half + 4, :], src[TOP, :, 0:64])
                        ins = dve.tensor_copy(q3[LOW, 4 * half:4 * half + 4, :], src[LOW, :, 64:P])
                    ins.then_inc(S["kT_ready"], 1)

                def inverse(b, n, what, group):
                    ab = "ab"[group]
                    g4 = slice(4 * group, 4 * group + 4)
                    xb = bank[2 * group][:, 0:256].rearrange("p (a c) -> p a c", a=4)
                    if what == 2 and n == ITERS - 1:
                        return
                    dve.wait_ge(S["x%s_psum" % ab], x_count(b, n, what))
                    done = S["x%s_read" % ab]
                    if what == 2:
                        dve.scalar_tensor_tensor(q1[:, g4, :], xb, -1.0 if n < 0 else -0.25, eye[0], ALU.mult, ALU.add).then_inc(done, 1)
                    elif what == 0:
                        dve.scalar_tensor_tensor(q2[:, g4, :], xb, -1.0, eye[1], ALU.mult, ALU.add).then_inc(done, 1)
                    else:
                        dve.scalar_tensor_tensor(q3_blk[TOP, g4, 0:64], xb[TOP], -1.0, eye[2][TOP], ALU.mult, ALU.add)
                        dve.scalar_tensor_tensor(q3_blk[LOW, g4, 64:P], xb[LOW], -1.0, eye[2][LOW], ALU.mult, ALU.add)
                        dve.scalar_tensor_tensor(q3[:, g4, :], xb, -1.0, eye[2], ALU.mult, ALU.add).then_inc(done, 1)

                def rows(b):
                    for step in range(BT + 3):
                        if step < BT:
                            for half in range(2):
                                n = 2 * (BT * b + step) + half
                                s_ps = bank[half][:, :].rearrange("p (h j) -> p h j", h=8)
                                dve.wait_ge(S["s1_psum"], n + 1)
                                dve.tensor_reduce(max1[:, half, :], s_ps, AX_X, ALU.max).then_inc(S["s1_chain"], 1)
                                dve.wait_ge(S["s1_chain"], n + 1)
                                at_least(dve, S["e1_ready"], 2 * BT * b + max(2 * step + half - 1, 0))
                                dve.tensor_tensor(s1[:, half, :, :], s_ps, max1[:, half, :].unsqueeze(2).to_broadcast([P, 8, 64]),
                                                  ALU.subtract).then_inc(S["s1_shifted"], 1)
                        if 0 <= step - 1 < BT:
                            i, u = BT * b + step - 1, (step - 1) % 2
                            dve.wait_ge(S["e1T_psum"], 2 * i + 2)
                            at_least(dve, S["o_psum"], i)
                            dve.tensor_copy(e1T[:, 4:8, :], bank[3][:, :].rearrange("p (a s) -> p a s", a=4)).then_inc(S["e1Tb_ready"], 1)
                        if 0 <= step - 2 < BT:
                            i, u = BT * b + step - 2, step % 2
                            dve.wait_ge(S["y_psum"], i + 1)
                            dve.tensor_tensor(x[:, i, :], x[:, i, :], bank[5][:, 256:512], ALU.add).then_inc(S["x_chain"], 1)
                            dve.wait_ge(S["x_chain"], 5 * i + 1)
                            dve.tensor_tensor(x[:, i, :], x[:, i, :], bias_o[:, :], ALU.add).then_inc(S["x_chain"], 1)
                            dve.wait_ge(S["x_chain"], 5 * i + 2)
                            variance(x[:, i, :], stats2[:, :], mv2[:, :], S["x_chain"], 5 * i + 2)
                        if 0 <= step - 1 < BT:
                            i, u = BT * b + step - 1, (step - 1) % 2
                            ops = bank[4][:, 0:272].rearrange("p (h e) -> p h e", h=16)
                            dve.wait_ge(S["o_psum"], i + 1)
                            dve.reciprocal(den[:, :], ops[:, :, 16]).then_inc(S["o_chain"], 1)
                            dve.wait_ge(S["o_chain"], i + 1)
                            at_least(dve, S["oT_psum"], BT * b + max(step - 2, 0))
                            dve.tensor_tensor(o[:, u, :].rearrange("p (h e) -> p h e", h=16), ops[:, :, 0:16],
                                              den[:, :].unsqueeze(2).to_broadcast([P, 16, 16]), ALU.mult).then_inc(S["o_ready"], 1)
                        if 0 <= step - 2 < BT:
                            i, u = BT * b + step - 2, step % 2
                            dve.wait_ge(S["r_rstd"], i + 1)
                            at_least(dve, S["xrT_psum"], BT * b + max(step - 3, 0))
                            at_least(dve, S["xr_kept"], BT * b + max(step - 3, 0))
                            dve.tensor_scalar(xr[:, u, :], x[:, i, :], mv2[:, 0:1], rstd2[:, :], ALU.subtract, ALU.mult).then_inc(S["xr_ready"], 1)
                        if 0 <= step - 3 < BT:
                            i = BT * b + step - 3
                            dve.wait_ge(S["logits_psum"], i + 1)
                            dve.tensor_tensor(logits[:, i, :], bank[6][:, 256:272], bias_r[:, :], ALU.add).then_inc(S["logits_read"], 1)

                batches(dve, project, pairs, inverse, rows)


class Core:
    pass


def build_program(nc, a, out):
    with ExitStack() as stack:
        B = Buffers(nc, stack)
        core = Core()
        core.NT, core.NE, core.CAP = 32, 16, 640
        slots, spare = core.NE * core.CAP, 2 * core.NT * P
        core.x = B.sb("x_tokens", [P, core.NT, 256])
        core.xn = B.sb("xn_tokens", [P, core.NT, 256])
        core.cst = B.sb("const", [P, C_WIDTH])
        core.cst_dram = a["const"]
        core.minus_half = B.sb("minus_half", [P, 1])
        core.gather_at = B.sb("gather_at", [P, 2 * core.NT], I32)
        core.weight = B.sb("gate_weight", [P, 2, core.NT])
        logits = B.sb("logits", [P, core.NT, core.NE])
        core.psum = B.ps("psum", [P, 8, 512])
        core.bank = [core.psum[:, i, :] for i in range(8)]
        core.slots_dram = nc.dram_tensor("slots_dram", [slots + spare, 256], F32, kind="Internal").ap()
        core.expert_out = nc.dram_tensor("expert_out", [slots, 256], F32, kind="Internal").ap()
        core.zeroed = B.sem("zeroed")

        linear_attention(nc, core, a["x"], a["a_wqkT"], a["a_wvT"], a["a_woT"], a["a_bqk"], a["a_bv"], a["a_bo"],
                         a["rwT"], a["rb"], logits)
        route_and_dispatch(nc, core, logits, "f_")
        experts(nc, core, a["w1"], a["b1"], a["w2"], a["b2"], "f_")
        combine(nc, core, None, "f_")
        nystrom_attention(nc, core, a["n_wqk"], a["n_wv"], a["n_wo"], a["n_bqk"], a["n_bv"], a["n_bo"],
                          a["rwT"], a["rb"], logits)
        route_and_dispatch(nc, core, logits, "g_")
        experts(nc, core, a["w1"], a["b1"], a["w2"], a["b2"], "g_")
        combine(nc, core, out, "g_")


def kernel(**inputs):
    import concourse.bacc as _bacc
    from concourse.bass_utils import run_bass_kernel_spmd as _run

    z = {k.removeprefix("L0_"): np.asarray(v) for k, v in inputs.items()}
    wqkv, bqkv = z["attn_b_Wqkv"], z["attn_b_bqkv"]
    arrays = {
        "x": z["attn_a_x"].reshape(4096, 256),
        "const": constants(8, 32),
        "a_wqkT": np.concatenate([z["attn_a_Wq"], z["attn_a_Wk"]]).T,
        "a_wvT": z["attn_a_Wv"].T,
        "a_woT": z["attn_a_Wo"].T,
        "a_bqk": np.concatenate([z["attn_a_bq"], z["attn_a_bk"]]),
        "a_bv": z["attn_a_bv"],
        "a_bo": z["attn_a_bo"],
        "rwT": z["ffn_router_w"].T,
        "rb": z["ffn_router_b"],
        "w1": z["ffn_w1"],
        "b1": z["ffn_b1"].reshape(16, 8, P).transpose(0, 2, 1),
        "w2": z["ffn_w2"],
        "b2": z["ffn_b2"],
        "n_wqk": wqkv[:, :512],
        "n_wv": wqkv[:, 512:],
        "n_wo": z["attn_b_Wout"],
        "n_bqk": bqkv[:512],
        "n_bv": bqkv[512:],
        "n_bo": z["attn_b_bout"],
    }
    arrays = {k: np.ascontiguousarray(v) for k, v in arrays.items()}
    nc = _bacc.Bacc("TRN2", target_bir_lowering=False, num_devices=1)
    aps = {k: nc.dram_tensor("in_" + k, v.shape, mybir.dt.from_np(v.dtype), kind="ExternalInput").ap() for k, v in arrays.items()}
    out = nc.dram_tensor("out", [4096, 256], F32, kind="ExternalOutput").ap()
    build_program(nc, aps, out)
    r = _run(nc, [{"in_" + k: v for k, v in arrays.items()}], core_ids=[0])
    return np.asarray(r.results[0]["out"]).reshape(4, 1024, 256)
```

```python
from contextlib import ExitStack

import concourse.bass as bass
import numpy as np
from concourse import mybir

F32 = mybir.dt.float32
BF16 = mybir.dt.bfloat16
F32R = mybir.dt.float32r
I32 = mybir.dt.int32
ALU = mybir.AluOpType
ACT = mybir.ActivationFunctionType
AX_X = mybir.AxisListType.X
AX_XY = mybir.AxisListType.XY

P = 128
LN_EPS = 1e-5
DEN_EPS = 1e-6

C_IDENT = 0
C_CAUSAL = 128
C_HEAD8 = 256
C_BLOCK = 264
C_KEEP = 536
C_STRICT = 568
C_IOTA = 696
C_EYE7 = 712
C_TRASH = 904
C_WIDTH = 968


def constants(batch_tiles, tiles):
    c = np.zeros((P, C_WIDTH), np.float32)
    p = np.arange(P)[:, None]
    col = np.arange(P)[None, :]
    c[:, C_IDENT:C_IDENT + P] = p == col
    c[:, C_CAUSAL:C_CAUSAL + P] = p <= col
    c[:, C_HEAD8:C_HEAD8 + 8] = p // 16 == np.arange(8)[None, :]
    c[:, C_BLOCK:C_BLOCK + 272] = p // 16 == (np.arange(272) // 17 % 8)[None, :]
    c[:, C_KEEP:C_KEEP + tiles] = (np.arange(tiles) + 1) % batch_tiles != 0
    c[:, C_STRICT:C_STRICT + P] = p < col
    c[:, C_IOTA:C_IOTA + 16] = np.arange(16)
    for n, f in enumerate((7.0, 15.0, 13.0)):
        c[:, C_EYE7 + 64 * n:C_EYE7 + 64 * n + 64] = f * (p % 64 == np.arange(64)[None, :])
    c[:, C_TRASH:C_TRASH + 2 * tiles] = np.arange(2 * tiles)[None, :] * P + p
    return c


def at_least(eng, sem, count):
    if isinstance(count, int) and count <= 0:
        return
    eng.wait_ge(sem, count)


def pipeline(eng, tiles, depth, step):
    first = depth + 2 - depth % 2
    last = first + (tiles - first) // 2 * 2
    for it in range(first):
        step(it, it % 2, lambda lag, it=it: 0 <= it - lag < tiles)
    with eng.Fori(first // 2, last // 2) as turn:
        for u in range(2):
            step(2 * turn + u, u, lambda lag: True)
    for it in range(last, tiles + depth):
        step(it, it % 2, lambda lag, it=it: 0 <= it - lag < tiles)


class Buffers:

    def __init__(self, nc, stack):
        self.nc, self.stack = nc, stack

    def sb(self, name, shape, dt=F32):
        return self.stack.enter_context(self.nc.sbuf_tensor(name, shape, dt))

    def ps(self, name, shape=(P, 512), dt=F32):
        return self.stack.enter_context(self.nc.psum_tensor(name, list(shape), dt))

    def sem(self, name):
        return self.stack.enter_context(self.nc.semaphore(name))


class Shared:

    def __init__(self, buffers):
        self.buffers, self.made = buffers, {}

    def sem(self, name):
        if name not in self.made:
            self.made[name] = self.buffers.sem(name)
        return self.made[name]


def linear_attention(nc, core, x_in, wqkT, wvT, woT, bqk, bv, bo, rwT, rb, logits):
    x, xn_all, cst, NT = core.x, core.xn, core.cst, core.NT
    NH, DH = 16, 16
    KD = 2
    LX, LA, LB, LC, LD, LE = 0, 1, 2, 3, 4, 5
    with ExitStack() as stack:
        B = Buffers(nc, stack)
        wqk = B.sb("a_wqk", [P, KD, 512])
        wv = B.sb("a_wv", [P, KD, 256])
        wo = B.sb("a_wo", [P, KD, 256])
        rw = B.sb("a_rw", [P, KD, 16])
        bias_qk = B.sb("a_bias_qk", [P, 4])
        bias_v = B.sb("a_bias_v", [P, 256])
        bias_o = B.sb("a_bias_o", [P, 256])
        bias_r = B.sb("a_bias_r", [P, 16])
        tick = B.sb("a_tick", [P, 2])
        stats = B.sb("a_stats", [P, 2, 6])
        mv = B.sb("a_mv", [P, 2, 2])
        rstd = B.sb("a_rstd", [P, 2])
        xln = B.sb("a_xln", [P, 2, 256])
        xlnT = B.sb("a_xlnT", [P, 2, KD, P])
        er = B.sb("a_er", [P, 2, 2, 4, P])
        phi = B.sb("a_phi", [P, 2, 4, P])
        qbd = B.sb("a_qbd", [P, 2, 2, 8, P])
        vaug = B.sb("a_vaug", [P, 2, NH, DH + 1])
        ktok = B.sb("a_ktok", [P, 256])
        sc = B.sb("a_sc", [P, NH, P])
        state = B.sb("a_state", [P, 2, 136])
        stmp = B.sb("a_stmp", [P, 272])
        den = B.sb("a_den", [P, NH])
        rec = B.sb("a_rec", [P, NH])
        o = B.sb("a_o", [P, 2, 256])
        oT = B.sb("a_oT", [P, KD, P])
        stats2 = B.sb("a_stats2", [P, 2, 6])
        mv2 = B.sb("a_mv2", [P, 2, 2])
        rstd2 = B.sb("a_rstd2", [P, 2])
        xr = B.sb("a_xr", [P, 2, 256])
        xrT = B.sb("a_xrT", [P, KD, P])

        b_t, b_qk, b_v, b_s0, b_s1, b_o, b_st, b_c = [core.bank[i] for i in range(8)]
        b_s = [b_s0, b_s1]

        loaded = B.sem("a_loaded")
        x_here = B.sem("a_x_here")
        zero_made = B.sem("a_zero_made")
        zero = B.sb("a_zero", [P, 2560])
        made = B.sem("a_made")
        ln_chain = B.sem("a_ln_chain")
        ln_rstd = B.sem("a_ln_rstd")
        xln_ready = B.sem("a_xln_ready")
        xlnT_psum = B.sem("a_xlnT_psum")
        xlnT_ready = B.sem("a_xlnT_ready")
        qk_psum = B.sem("a_qk_psum")
        v_psum = B.sem("a_v_psum")
        er_ready = B.sem("a_er_ready")
        phi_ready = B.sem("a_phi_ready")
        v_ready = B.sem("a_v_ready")
        qbd_ready = B.sem("a_qbd_ready")
        k_psum = B.sem("a_k_psum")
        ktok_ready = B.sem("a_ktok_ready")
        s_psum = B.sem("a_s_psum")
        s_ready = B.sem("a_s_ready")
        o_psum = B.sem("a_o_psum")
        o_chain = B.sem("a_o_chain")
        o_ready = B.sem("a_o_ready")
        st_psum = B.sem("a_st_psum")
        st_chain = B.sem("a_st_chain")
        st_ready = B.sem("a_st_ready")
        oT_psum = B.sem("a_oT_psum")
        oT_ready = B.sem("a_oT_ready")
        y_psum = B.sem("a_y_psum")
        x_chain = B.sem("a_x_chain")
        r_rstd = B.sem("a_r_rstd")
        xr_ready = B.sem("a_xr_ready")
        xr_kept = B.sem("a_xr_kept")
        xrT_psum = B.sem("a_xrT_psum")
        xrT_ready = B.sem("a_xrT_ready")
        logits_psum = B.sem("a_logits_psum")
        logits_read = B.sem("a_logits_read")

        ident = cst[:, C_IDENT:C_IDENT + P]
        N_LOADS = 9

        with nc.Block() as block:

            @block.sync
            def _(sp):
                def tokens(b):
                    sp.dma_start(x[:, 8 * b:8 * b + 8, :],
                                 x_in[1024 * b:1024 * b + 1024, :].rearrange("(t p) d -> p t d", p=P)).then_inc(x_here, 16)

                tokens(0)
                sp.dma_start(cst[:, :], core.cst_dram).then_inc(loaded, 16)
                for dst, src in ((wqk, wqkT), (wv, wvT), (wo, woT), (rw, rwT)):
                    sp.dma_start(dst[:, :, :], src.rearrange("(k p) n -> p k n", p=P)).then_inc(loaded, 16)
                sp.dma_start(bias_qk[:, :], bqk.rearrange("(g p) -> p g", p=P), allow_slow_non_contiguous=True).then_inc(loaded, 16)
                for dst, src, width in ((bias_v, bv, 256), (bias_o, bo, 256), (bias_r, rb, 16)):
                    sp.dma_start(dst[:, :], src[None, :].to_broadcast([P, width])).then_inc(loaded, 16)
                sp.wait_ge(x_here, 16)
                for b in range(1, 4):
                    tokens(b)
                sp.wait_ge(zero_made, 1)
                slots = core.NE * core.CAP
                sp.dma_start(core.slots_dram[0:slots, :].rearrange("(p a b) d -> p a (b d)", p=P, b=10),
                             zero[:, :].unsqueeze(1).to_broadcast([P, slots // P // 10, 2560])).then_inc(core.zeroed, 16)

            @block.gpsimd
            def _(pool):
                pool.memset(zero[:, :], 0.0).then_inc(zero_made, 1)
                pool.memset(core.minus_half[:, :], -0.5).then_inc(made, 1)
                pool.memset(state[:, :, :], 0.0).then_inc(made, 1)
                pool.memset(vaug[:, :, :, :], 1.0).then_inc(made, 1)
                pool.wait_ge(made, 3)
                pool.wait_ge(loaded, 16 * N_LOADS)

                def step(it, par, live):
                    if live(LX):
                        i = it
                        at_least(pool, ln_chain, 3 * i + 3)
                        pool.tensor_tensor(rstd[:, par:par + 1], mv[:, par, 1:2], core.minus_half[:, :], ALU.pow).then_inc(ln_rstd, 1)
                    if live(LA):
                        i = it - LA
                        q = (par + LA) % 2
                        at_least(pool, phi_ready, i + 1)
                        at_least(pool, s_psum, 4 * (i - 1))
                        for half in range(2):
                            ins = pool.tensor_tensor(
                                qbd[:, q, half, :, :],
                                phi[:, q, half:half + 1, :].to_broadcast([P, 8, P]),
                                cst[:, C_HEAD8:C_HEAD8 + 8].unsqueeze(2).to_broadcast([P, 8, P]), ALU.mult)
                        ins.then_inc(qbd_ready, 1)
                    if live(LC):
                        i = it - LC
                        q = (par + LC) % 2
                        at_least(pool, x_chain, 5 * i + 5)
                        pool.tensor_tensor(rstd2[:, q:q + 1], mv2[:, q, 1:2], core.minus_half[:, :], ALU.pow).then_inc(r_rstd, 1)
                    if live(LC):
                        i = it - LC
                        q = (par + LC) % 2
                        at_least(pool, xr_ready, i + 1)
                        pool.tensor_copy(xn_all[:, i, :], xr[:, q, :]).then_inc(xr_kept, 1)

                pipeline(pool, NT, LE, step)

            @block.scalar
            def _(act):
                act.wait_ge(loaded, 16 * N_LOADS)

                def step(it, par, live):
                    if live(LA):
                        i, q = it - LA, (par + LA) % 2
                        at_least(act, xlnT_psum, i + 1)
                        at_least(act, v_psum, i - 1)
                        act.activation(xlnT[:, q, :, :], b_t[:, 0:256].rearrange("p (k t) -> p k t", k=KD), ACT.Copy).then_inc(xlnT_ready, 1)
                    if live(LC):
                        i = it - LC
                        at_least(act, oT_psum, i + 1)
                        at_least(act, y_psum, i)
                        act.activation(oT[:, :, :], b_c[:, 0:256].rearrange("p (k t) -> p k t", k=KD), ACT.Copy).then_inc(oT_ready, 1)
                    if live(LA):
                        i, q = it - LA, (par + LA) % 2
                        at_least(act, qk_psum, i + 1)
                        at_least(act, phi_ready, i - 1)
                        for g in range(4):
                            act.activation(er[:, q, 0, g, :], b_qk[:, P * g:P * g + P], ACT.Exp, bias=bias_qk[:, g:g + 1])
                        for g in range(4):
                            ins = act.activation(er[:, q, 1, g, :], b_qk[:, P * g:P * g + P], ACT.Relu, bias=bias_qk[:, g:g + 1])
                        ins.then_inc(er_ready, 1)
                    if live(LD):
                        i = it - LD
                        at_least(act, xrT_psum, i + 1)
                        at_least(act, logits_psum, i)
                        act.activation(xrT[:, :, :], b_t[:, 256:512].rearrange("p (k t) -> p k t", k=KD), ACT.Copy).then_inc(xrT_ready, 1)
                    if live(LB):
                        i = it - LB
                        at_least(act, k_psum, i + 1)
                        at_least(act, st_psum, i)
                        act.activation(ktok[:, :], b_v[:, 256:512], ACT.Copy).then_inc(ktok_ready, 1)

                pipeline(act, NT, LE, step)

            @block.tensor
            def _(pe):
                pe.wait_ge(loaded, 16 * N_LOADS)
                pe.wait_ge(made, 3)

                def scores(it, par, live, g):
                    if live(LB):
                        i, q, half = it - LB, (par + LB) % 2, g // 2
                        if g == 0:
                            at_least(pe, phi_ready, i + 1)
                            at_least(pe, qbd_ready, i + 1)
                        at_least(pe, s_ready, 4 * i + g - 1)
                        pe.matmul(b_s[g % 2][:, :], phi[:, q, 2 + half, :],
                                  qbd[:, q, half, 4 * (g % 2):4 * (g % 2) + 4, :],
                                  start=True, stop=True).then_inc(s_psum, 1)

                def heads(it, par, live, g):
                    if live(LB):
                        i, q = it - LB, (par + LB) % 2
                        if g == 0:
                            at_least(pe, st_ready, i)
                            at_least(pe, o_ready, i)
                            for half in range(2):
                                pe.matmul(b_o[:, 136 * half:136 * half + 136], phi[:, q, half, :], state[:, half, :],
                                          start=(half == 0), stop=False, skip_group_check=True)
                        at_least(pe, s_ready, 4 * i + g + 1)
                        for h in range(4 * g, 4 * g + 4):
                            ins = pe.matmul(b_o[:, 17 * h:17 * h + 17], sc[:, h, :], vaug[:, q, h, :],
                                            start=False, stop=(h == NH - 1), skip_group_check=True)
                        if g == 3:
                            ins.then_inc(o_psum, 1)

                def step(it, par, live):
                    if live(LA):
                        i, q = it - LA, (par + LA) % 2
                        at_least(pe, xln_ready, i + 1)
                        at_least(pe, xlnT_ready, i)
                        at_least(pe, xrT_ready, it - LD)
                        for k in range(KD):
                            ins = pe.transpose(b_t[:, P * k:P * k + P], xln[:, q, P * k:P * k + P], ident)
                        ins.then_inc(xlnT_psum, 1)
                    scores(it, par, live, 0)
                    if live(LC):
                        i, q = it - LC, (par + LC) % 2
                        at_least(pe, o_ready, i + 1)
                        at_least(pe, x_chain, 5 * (i - 1) + 1)
                        for k in range(KD):
                            ins = pe.transpose(b_c[:, P * k:P * k + P], o[:, q, P * k:P * k + P], ident)
                        ins.then_inc(oT_psum, 1)
                    if live(LA):
                        i, q = it - LA, (par + LA) % 2
                        at_least(pe, xlnT_ready, i + 1)
                        at_least(pe, er_ready, i)
                        for g in range(4):
                            for k in range(KD):
                                ins = pe.matmul(b_qk[:, P * g:P * g + P], wqk[:, k, P * g:P * g + P], xlnT[:, q, k, :],
                                                start=(k == 0), stop=(k == KD - 1))
                        ins.then_inc(qk_psum, 1)
                    scores(it, par, live, 1)
                    if live(LE):
                        i = it - LE
                        at_least(pe, xrT_ready, i + 1)
                        at_least(pe, st_ready, min(it, NT + LB) - LB if isinstance(it, int) else it - LB)
                        at_least(pe, logits_read, i)
                        for k in range(KD):
                            ins = pe.matmul(b_st[:, 272:288], xrT[:, k, :], rw[:, k, :], start=(k == 0), stop=(k == KD - 1))
                        ins.then_inc(logits_psum, 1)
                    heads(it, par, live, 0)
                    if live(LA):
                        i, q = it - LA, (par + LA) % 2
                        at_least(pe, v_ready, i)
                        at_least(pe, ktok_ready, i - 1)
                        for k in range(KD):
                            ins = pe.matmul(b_v[:, 0:256], xlnT[:, q, k, :], wv[:, k, :], start=(k == 0), stop=(k == KD - 1))
                        ins.then_inc(v_psum, 1)
                    scores(it, par, live, 2)
                    heads(it, par, live, 1)
                    if live(LC):
                        i = it - LC
                        at_least(pe, oT_ready, i + 1)
                        for k in range(KD):
                            ins = pe.matmul(b_c[:, 256:512], oT[:, k, :], wo[:, k, :], start=(k == 0), stop=(k == KD - 1))
                        ins.then_inc(y_psum, 1)
                    scores(it, par, live, 3)
                    heads(it, par, live, 2)
                    if live(LD):
                        i, q = it - LD, (par + LD) % 2
                        at_least(pe, xr_ready, i + 1)
                        if live(LA):
                            at_least(pe, xlnT_ready, it - LA + 1)
                        for k in range(KD):
                            ins = pe.transpose(b_t[:, 256 + P * k:256 + P * k + P], xr[:, q, P * k:P * k + P], ident)
                        ins.then_inc(xrT_psum, 1)
                    if live(LB):
                        i, q = it - LB, (par + LB) % 2
                        at_least(pe, v_ready, it - LA + 1 if live(LA) else i + 1)
                        for k in range(KD):
                            ins = pe.transpose(b_v[:, 256 + P * k:256 + P * k + P], phi[:, q, 2 + k, :], ident)
                        ins.then_inc(k_psum, 1)
                    heads(it, par, live, 3)
                    if live(LB):
                        i, q = it - LB, (par + LB) % 2
                        at_least(pe, ktok_ready, i + 1)
                        at_least(pe, logits_read, it - LE + 1)
                        for half in range(2):
                            ins = pe.matmul(b_st[:, 136 * half:136 * half + 136], ktok[:, P * half:P * half + P],
                                            vaug[:, q, 8 * half:8 * half + 8, :], start=True, stop=True)
                        ins.then_inc(st_psum, 1)

                pipeline(pe, NT, LE, step)

            @block.vector
            def _(dve):
                dve.wait_ge(loaded, 16 * N_LOADS)
                dve.wait_ge(made, 3)

                def variance(src, st, m, chain, done):
                    dve.memset(tick[:, 0:1], 0.0)
                    dve.bn_stats(st, src).then_inc(chain, 1)
                    at_least(dve, chain, done + 1)
                    dve.memset(tick[:, 1:2], 0.0)
                    dve.bn_aggr(m, st).then_inc(chain, 1)
                    at_least(dve, chain, done + 2)
                    dve.tensor_scalar(m[:, 1:2], m[:, 1:2], LN_EPS, None, ALU.add).then_inc(chain, 1)

                def mask(it, live, g):
                    if live(LB):
                        i = it - LB
                        at_least(dve, s_psum, 4 * i + g + 1)
                        at_least(dve, o_psum, i)
                        dve.tensor_tensor(sc[:, 4 * g:4 * g + 4, :],
                                          b_s[g % 2][:, :].rearrange("p (h t) -> p h t", h=4),
                                          cst[:, C_CAUSAL:C_CAUSAL + P].unsqueeze(1).to_broadcast([P, 4, P]),
                                          ALU.mult).then_inc(s_ready, 1)

                def step(it, par, live):
                    if live(LX):
                        if isinstance(it, int) and it in (0, 5):
                            dve.wait_ge(x_here, 16 if it == 0 else 64)
                        variance(x[:, it, :], stats[:, par, :], mv[:, par, :], ln_chain, 3 * it)
                    mask(it, live, 0)
                    if live(LX):
                        at_least(dve, ln_rstd, it + 1)
                        at_least(dve, xlnT_psum, it - 1)
                        dve.tensor_scalar(xln[:, par, :], x[:, it, :], mv[:, par, 0:1], rstd[:, par:par + 1],
                                          ALU.subtract, ALU.mult).then_inc(xln_ready, 1)
                    mask(it, live, 1)
                    if live(LE):
                        i = it - LE
                        at_least(dve, logits_psum, i + 1)
                        dve.tensor_tensor(logits[:, i, :], b_st[:, 272:288], bias_r[:, :], ALU.add).then_inc(logits_read, 1)
                    if live(LA):
                        i, q = it - LA, (par + LA) % 2
                        at_least(dve, er_ready, i + 1)
                        at_least(dve, o_psum, i - 1)
                        at_least(dve, qbd_ready, i - 1)
                        dve.scalar_tensor_tensor(phi[:, q, :, :], er[:, q, 0, :, :], 1.0, er[:, q, 1, :, :],
                                                 ALU.min, ALU.add).then_inc(phi_ready, 1)
                    if live(LA):
                        i, q = it - LA, (par + LA) % 2
                        at_least(dve, v_psum, i + 1)
                        at_least(dve, st_psum, i - 1)
                        dve.tensor_tensor(vaug[:, q, :, 0:DH], b_v[:, 0:256].rearrange("p (h e) -> p h e", h=NH),
                                          bias_v[:, :].rearrange("p (h e) -> p h e", h=NH), ALU.add).then_inc(v_ready, 1)
                    mask(it, live, 2)
                    mask(it, live, 3)
                    if live(LC):
                        i, q = it - LC, (par + LC) % 2
                        at_least(dve, y_psum, i + 1)
                        dve.tensor_tensor(x[:, i, :], x[:, i, :], b_c[:, 256:512], ALU.add).then_inc(x_chain, 1)
                        at_least(dve, x_chain, 5 * i + 1)
                        dve.tensor_tensor(x[:, i, :], x[:, i, :], bias_o[:, :], ALU.add).then_inc(x_chain, 1)
                        at_least(dve, x_chain, 5 * i + 2)
                        variance(x[:, i, :], stats2[:, q, :], mv2[:, q, :], x_chain, 5 * i + 2)
                    if live(LB):
                        i, q = it - LB, (par + LB) % 2
                        at_least(dve, o_psum, i + 1)
                        ops = b_o[:, 0:272].rearrange("p (h e) -> p h e", h=NH)
                        dve.tensor_scalar(den[:, :], ops[:, :, DH], DEN_EPS, None, ALU.max).then_inc(o_chain, 1)
                        at_least(dve, o_chain, 2 * i + 1)
                        dve.reciprocal(rec[:, :], den[:, :]).then_inc(o_chain, 1)
                        at_least(dve, o_chain, 2 * i + 2)
                        at_least(dve, oT_psum, i - 1)
                        dve.tensor_tensor(o[:, q, :].rearrange("p (h e) -> p h e", h=NH), ops[:, :, 0:DH],
                                          rec[:, :].unsqueeze(2).to_broadcast([P, NH, DH]), ALU.mult).then_inc(o_ready, 1)
                    if live(LB):
                        i, q = it - LB, (par + LB) % 2
                        keep = cst[:, bass.ds(i + C_KEEP, 1)]
                        at_least(dve, st_psum, i + 1)
                        dve.scalar_tensor_tensor(stmp[:, :], b_st[:, 0:272], keep, cst[:, C_BLOCK:C_BLOCK + 272],
                                                 ALU.mult, ALU.mult).then_inc(st_chain, 1)
                        at_least(dve, st_chain, i + 1)
                        dve.scalar_tensor_tensor(state[:, :, :].rearrange("p a b -> p (a b)"),
                                                 state[:, :, :].rearrange("p a b -> p (a b)"), keep, stmp[:, :],
                                                 ALU.mult, ALU.add).then_inc(st_ready, 1)
                    if live(LC):
                        i, q = it - LC, (par + LC) % 2
                        at_least(dve, r_rstd, i + 1)
                        at_least(dve, xrT_psum, i - 1)
                        at_least(dve, xr_kept, i - 1)
                        dve.tensor_scalar(xr[:, q, :], x[:, i, :], mv2[:, q, 0:1], rstd2[:, q:q + 1],
                                          ALU.subtract, ALU.mult).then_inc(xr_ready, 1)

                pipeline(dve, NT, LE, step)


def route_and_dispatch(nc, core, logits, name, call):
    NT, NE, CAP = core.NT, core.NE, core.CAP
    SLOTS = NE * CAP
    cst, xn = core.cst, core.xn
    with ExitStack() as stack:
        B = Buffers(nc, stack)
        wide = [P, NT, NE]
        key = B.sb(name + "r_key", wide)
        eq = B.sb(name + "r_eq", wide)
        rest = B.sb(name + "r_rest", wide)
        hot = B.sb(name + "r_hot", [P, 2, NT, NE])
        hot_pad = B.sb(name + "r_hot_pad", [P, NE + NT * NE], BF16)
        hot_sum = hot_pad[:, NE:NE + NT * NE]
        strict = B.sb(name + "r_strict", [P, P], BF16)
        ones = B.sb(name + "r_ones", [P, P], BF16)
        top = B.sb(name + "r_top", [P, 2, NT])
        which = B.sb(name + "r_which", [P, 2, NT])
        pos = B.sb(name + "r_pos", [P, 2, NT])
        kept = B.sb(name + "r_kept", [P, 2, NT])
        gate = B.sb(name + "r_gate", [P, 2, NT])
        tmp = B.sb(name + "r_tmp", [P, 2, NT])
        total = B.sb(name + "r_total", [P, NT])
        scatter_at = B.sb(name + "r_scatter_at", [P, 2 * NT], I32)
        counts = core.bank[0]

        chain = core.shared.sem("r_chain")
        gap_ready = core.shared.sem("r_gap_ready")
        exp_ready = core.shared.sem("r_exp_ready")
        hot_ready = core.shared.sem("r_hot_ready")
        counts_psum = core.shared.sem("r_counts_psum")
        slots_ready = core.shared.sem("r_slots_ready")
        scattered = core.shared.sem("r_scattered")

        with nc.Block() as block:

            @block.vector
            def _(dve):
                CHAIN = 30
                n = [CHAIN * call]

                def link(ins):
                    n[0] += 1
                    ins.then_inc(chain, 1)
                    dve.wait_ge(chain, n[0])

                iota = cst[:, C_IOTA:C_IOTA + NE].unsqueeze(1).to_broadcast(wide)
                dve.tensor_copy(strict[:, :], cst[:, C_STRICT:C_STRICT + P])
                dve.memset(ones[:, :], 1.0)
                dve.memset(hot_pad[:, 0:NE], 0.0)
                scores = logits[:, :, :]
                for r in range(2):
                    link(dve.tensor_reduce(top[:, r, :], scores, AX_X, ALU.max))
                    link(dve.tensor_tensor(eq[:, :, :], scores, top[:, r, :].unsqueeze(2).to_broadcast(wide), ALU.is_equal))
                    link(dve.scalar_tensor_tensor(key[:, :, :], eq[:, :, :], -float(NE), iota, ALU.mult, ALU.add))
                    link(dve.tensor_reduce(which[:, r, :], key[:, :, :], AX_X, ALU.min))
                    link(dve.tensor_tensor(hot[:, r, :, :], key[:, :, :], which[:, r, :].unsqueeze(2).to_broadcast(wide), ALU.is_equal))
                    if r == 0:
                        link(dve.scalar_tensor_tensor(rest[:, :, :], hot[:, 0, :, :], -3.0e38, scores, ALU.mult, ALU.add))
                        scores = rest[:, :, :]
                link(dve.tensor_tensor(hot_sum.rearrange("p (t e) -> p t e", e=NE), hot[:, 0, :, :], hot[:, 1, :, :], ALU.add))
                dve.tensor_tensor(tmp[:, 0, :], top[:, 1, :], top[:, 0, :], ALU.subtract).then_inc(gap_ready, 1)
                dve.wait_ge(exp_ready, call + 1)
                link(dve.tensor_scalar(total[:, :], tmp[:, 1, :], 1.0, None, ALU.add))
                link(dve.reciprocal(gate[:, 0, :], total[:, :]))
                link(dve.tensor_tensor(gate[:, 1, :], gate[:, 0, :], tmp[:, 1, :], ALU.mult))
                dve.wait_ge(counts_psum, call + 1)
                for r in range(2):
                    link(dve.tensor_tensor(key[:, :, :], hot[:, r, :, :], counts[:, 0:NT * NE].rearrange("p (t e) -> p t e", e=NE), ALU.mult))
                    link(dve.tensor_reduce(pos[:, r, :], key[:, :, :], AX_X, ALU.add))
                link(dve.tensor_scalar(kept[:, :, :], pos[:, :, :], float(CAP), None, ALU.is_lt))
                link(dve.scalar_tensor_tensor(pos[:, :, :], which[:, :, :], float(CAP), pos[:, :, :], ALU.mult, ALU.add))
                trash = cst[:, C_TRASH:C_TRASH + 2 * NT].rearrange("p (r t) -> p r t", r=2)
                link(dve.tensor_tensor(tmp[:, :, :], pos[:, :, :], trash, ALU.subtract))
                link(dve.tensor_tensor(tmp[:, :, :], tmp[:, :, :], kept[:, :, :], ALU.mult))
                link(dve.tensor_tensor(tmp[:, :, :], tmp[:, :, :], trash, ALU.add))
                dve.tensor_scalar(scatter_at[:, :].rearrange("p (r t) -> p r t", r=2), tmp[:, :, :], float(SLOTS), None,
                                  ALU.add).then_inc(slots_ready, 1)
                link(dve.scalar_tensor_tensor(core.gather_at[:, :].rearrange("p (r t) -> p r t", r=2), pos[:, :, :],
                                              float(SLOTS), kept[:, :, :], ALU.add, ALU.mult))
                link(dve.tensor_tensor(gate[:, :, :], gate[:, :, :], kept[:, :, :], ALU.mult))
                link(dve.tensor_tensor(total[:, :], gate[:, 0, :], gate[:, 1, :], ALU.add))
                link(dve.tensor_scalar(total[:, :], total[:, :], 1e-9, None, ALU.add))
                link(dve.reciprocal(total[:, :], total[:, :]))
                link(dve.tensor_tensor(core.weight[:, :, :], gate[:, :, :], total[:, :].unsqueeze(1).to_broadcast([P, 2, NT]), ALU.mult))
                assert n[0] == CHAIN * (call + 1)

            @block.scalar
            def _(act):
                act.wait_ge(gap_ready, call + 1)
                act.activation(tmp[:, 1, :], tmp[:, 0, :], ACT.Exp).then_inc(exp_ready, 1)

            @block.tensor
            def _(pe):
                pe.wait_ge(gap_ready, call + 1)
                pe.matmul(counts[:, 0:NT * NE], strict[:, :], hot_sum, start=True, stop=False)
                for back in range(2, NT):
                    pe.matmul(counts[:, NE * back:NE * NT], ones[:, :], hot_pad[:, NE:NE + NE * (NT - back)],
                              start=False, stop=False, skip_group_check=True)
                pe.matmul(counts[:, 0:NE * NT], ones[:, :], hot_pad[:, 0:NE * NT], start=False, stop=True).then_inc(counts_psum, 1)

            @block.gpsimd
            def _(pool):
                pool.wait_ge(core.zeroed, 16)
                pool.wait_ge(slots_ready, call + 1)
                for j in range(2 * NT):
                    pool.indirect_dma_start(
                        out=core.slots_dram[:, :], out_offset=bass.IndirectOffsetOnAxis(ap=scatter_at[:, j:j + 1], axis=0),
                        in_=xn[:, j % NT, :], in_offset=None).then_inc(scattered, 16)
                pool.wait_ge(scattered, 16 * 2 * NT * (call + 1))


def experts(nc, core, w1, b1, w2, b2, name, call):
    NE, CAP = core.NE, core.CAP
    D, F = w1.shape[1], w1.shape[2]
    KD, KF, TS = D // P, F // P, CAP // P
    HALF = CAP // 2
    LT, LM = 0, 1
    BEFORE = NE * call
    with ExitStack() as stack:
        B = Buffers(nc, stack)
        w1b = B.sb(name + "e_w1", [P, KD, F])
        w1_high = B.sb(name + "e_w1_high", [P, KD, F], F32R)
        w1_low = B.sb(name + "e_w1_low", [P, KD, F], F32R)
        w2b = B.sb(name + "e_w2", [P, KF, D])
        w2_high = B.sb(name + "e_w2_high", [P, KF, D], F32R)
        w2_low = B.sb(name + "e_w2_low", [P, KF, D], F32R)
        b1b = B.sb(name + "e_b1", [P, 2, KF])
        b2b = B.sb(name + "e_b2", [P, 2, D])
        tok = B.sb(name + "e_tok", [P, 2, TS, D])
        tokT_high = B.sb(name + "e_tokT_high", [P, 2, KD, CAP], F32R)
        tokT_low = B.sb(name + "e_tokT_low", [P, 2, KD, CAP], F32R)
        RING = 4
        h = B.sb(name + "e_h", [P, RING, CAP])
        hT_high = B.sb(name + "e_hT_high", [P, KF, CAP], F32R)
        hT_low = B.sb(name + "e_hT_low", [P, KF, CAP], F32R)
        y = B.sb(name + "e_y", [P, 2, TS, D])
        psum, bank = core.psum, core.bank

        w1_loaded = core.shared.sem("e_w1_loaded")
        w2_loaded = core.shared.sem("e_w2_loaded")
        b2_loaded = [core.shared.sem(f"e_b2_loaded{u}") for u in range(2)]
        tok_loaded = [core.shared.sem(f"e_tok_loaded{u}") for u in range(2)]
        w1_halved = core.shared.sem("e_w1_halved")
        w1_split = core.shared.sem("e_w1_split")
        w2_halved = core.shared.sem("e_w2_halved")
        w2_split = core.shared.sem("e_w2_split")
        tokT_psum = core.shared.sem("e_tokT_psum")
        tokT_chain = core.shared.sem("e_tokT_chain")
        tokT_ready = core.shared.sem("e_tokT_ready")
        h_psum = core.shared.sem("e_h_psum")
        h_made = core.shared.sem("e_h_made")
        h_high = core.shared.sem("e_h_high")
        h_split = core.shared.sem("e_h_split")
        y_psum = core.shared.sem("e_y_psum")
        y_ready = core.shared.sem("e_y_ready")
        y_stored = [core.shared.sem(f"e_y_stored{u}") for u in range(2)]
        ident = core.cst[:, C_IDENT:C_IDENT + P]
        T_AFTER = [1, 3, 5]
        T_GROUPS = [(6, [(0, 0, 4)]), (7, [(1, 0, 4)]), (6, [(0, 4, TS - 4), (1, 4, TS - 4)])]

        def turns(eng, depth, step):
            first = 4
            for it in range(first):
                step(it, it % 2, it // 2, lambda lag, it=it: 0 <= it - lag < NE)
            with eng.Fori(first // 2, NE // 2) as turn:
                for u in range(2):
                    step(2 * turn + u, u, turn, lambda lag: True)
            for it in range(NE, NE + depth):
                step(it, it % 2, it // 2, lambda lag, it=it: 0 <= it - lag < NE)

        with nc.Block() as block:

            @block.sync
            def _(sp):
                def step(it, u, turn, live):
                    if live(0):
                        e, g = it, it + BEFORE
                        at_least(sp, tokT_psum, 3 * (g - 1))
                        sp.dma_start(tok[:, u, :, :], core.slots_dram[bass.ds(e * CAP, CAP), :].rearrange("(p t) d -> p t d", t=TS)).then_inc(tok_loaded[u], 16)
                        at_least(sp, w1_split, g)
                        sp.dma_start(w1b[:, :, :], w1[bass.ds(e, 1), :, :].rearrange("o (k p) f -> p (o k) f", p=P)).then_inc(w1_loaded, 16)
                        sp.dma_start(b1b[:, u, :], b1[bass.ds(e, 1), :, :].rearrange("o p c -> (o p) c")).then_inc(w1_loaded, 16)
                        at_least(sp, y_ready, TS * (g - 1))
                        sp.dma_start(b2b[:, u, :], b2[bass.ds(e, 1), :].to_broadcast([P, D])).then_inc(b2_loaded[u], 16)
                        at_least(sp, w2_split, g)
                        sp.dma_start(w2b[:, :, :], w2[bass.ds(e, 1), :, :].rearrange("o (c p) d -> p (o c) d", p=P)).then_inc(w2_loaded, 16)
                    if live(2):
                        e, g = it - 2, it - 2 + BEFORE
                        at_least(sp, y_ready, TS * (g + 1))
                        sp.dma_start(core.expert_out[bass.ds(e * CAP, CAP), :].rearrange("(p t) d -> p t d", t=TS), y[:, u, :, :]).then_inc(y_stored[u], 16)

                turns(sp, 2, step)
                for u in range(2):
                    sp.wait_ge(y_stored[u], 16 * (NE // 2) * (call + 1))

            @block.gpsimd
            def _(pool):
                def step(it, u, turn, live):
                    e, g = it, it + BEFORE
                    pool.wait_ge(w1_halved, g + 1)
                    pool.tensor_tensor(w1_low[:, :, :], w1b[:, :, :], w1_high[:, :, :].bitcast(F32), ALU.subtract).then_inc(w1_split, 1)
                    pool.wait_ge(w2_halved, g + 1)
                    pool.tensor_tensor(w2_low[:, :, :], w2b[:, :, :], w2_high[:, :, :].bitcast(F32), ALU.subtract).then_inc(w2_split, 1)

                turns(pool, 0, step)

            @block.tensor
            def _(pe):
                def transposes(g, u, turn, n):
                    b, runs = T_GROUPS[n]
                    if n == 0:
                        pe.wait_ge(tok_loaded[u], 16 * ((turn + BEFORE // 2) + 1))
                    at_least(pe, tokT_ready, 3 * g + n - 1 if n != 1 else 3 * g - 1)
                    at = 0
                    for k, t0, m in runs:
                        for t in range(t0, t0 + m):
                            ins = pe.transpose(bank[b][:, at:at + P], tok[:, u, t, P * k:P * k + P], ident)
                            at += P
                    ins.then_inc(tokT_psum, 1)

                def step(it, u, turn, live):
                    if not live(LM):
                        for n in range(3):
                            transposes(it + BEFORE, u, turn, n)
                        return
                    e, g, v = it - LM, it - LM + BEFORE, 1 - u
                    pe.wait_ge(w1_split, g + 1)
                    pe.wait_ge(tokT_ready, 3 * (g + 1))
                    for c in range(KF):
                        at_least(pe, h_made, KF * g + c - 1)
                        f = slice(P * c, P * c + P)
                        for half in range(2):
                            s = slice(HALF * half, HALF * half + HALF)
                            for k in range(KD):
                                out = bank[2 * (c % 2) + half][:, 0:HALF]
                                high, low = w1_high[:, k, f], w1_low[:, k, f]
                                pe.matmul(out, high, tokT_high[:, v, k, s], start=(k == 0), stop=False)
                                pe.matmul(out, high, tokT_low[:, v, k, s], start=False, stop=False)
                                ins = pe.matmul(out, low, tokT_high[:, v, k, s], start=False, stop=(k == KD - 1))
                        ins.then_inc(h_psum, 1)
                        if live(LT) and c in T_AFTER:
                            transposes(it + BEFORE, u, turn, T_AFTER.index(c))
                    pe.wait_ge(w2_split, g + 1)

                    def product(t, chunks):
                        s = slice(P * t, P * t + P)
                        for c in chunks:
                            if t == 0 or c == KF - 1:
                                pe.wait_ge(h_split, KF * g + c + 1)
                            out = bank[4 + t % 2][:, 0:D]
                            high, low = hT_high[:, c, s], hT_low[:, c, s]
                            pe.matmul(out, high, w2_high[:, c, :], start=(c == 0), stop=False)
                            pe.matmul(out, high, w2_low[:, c, :], start=False, stop=False)
                            ins = pe.matmul(out, low, w2_high[:, c, :], start=False, stop=(c == KF - 1))
                        return ins

                    at_least(pe, y_ready, TS * g)
                    for t in range(2):
                        product(t, range(KF - 1))
                    for t in range(2):
                        product(t, [KF - 1]).then_inc(y_psum, 1)
                    for t in range(2, TS):
                        at_least(pe, y_ready, TS * g + t - 1)
                        product(t, range(KF)).then_inc(y_psum, 1)

                turns(pe, 1, step)

            @block.scalar
            def _(act):
                def step(it, u, turn, live):
                    if live(LM):
                        e, g, v = it - LM, it - LM + BEFORE, 1 - u
                        act.wait_ge(w2_loaded, 16 * (g + 1))
                        at_least(act, y_psum, TS * g)
                        act.activation(w2_high[:, :, :], w2b[:, :, :], ACT.Copy).then_inc(w2_halved, 1)
                        for c in range(KF + 1):
                            if c < KF:
                                act.wait_ge(h_psum, KF * g + c + 1)
                                at_least(act, h_split, KF * g + c - RING + 1)
                                act.activation(h[:, c % RING, :].rearrange("p (a b) -> p a b", a=2), psum[:, 2 * (c % 2):2 * (c % 2) + 2, 0:HALF],
                                               ACT.Gelu, bias=b1b[:, v, c:c + 1]).then_inc(h_made, 1)
                            if c >= 1:
                                act.wait_ge(h_made, KF * g + c)
                                act.activation(hT_high[:, c - 1, :], h[:, (c - 1) % RING, :], ACT.Copy).then_inc(h_high, 1)
                    if live(0):
                        e, g = it, it + BEFORE
                        act.wait_ge(w1_loaded, 32 * (g + 1))
                        at_least(act, h_psum, KF * g)
                        act.activation(w1_high[:, :, :], w1b[:, :, :], ACT.Copy).then_inc(w1_halved, 1)

                turns(act, 1, step)

            @block.vector
            def _(dve):
                def transposed(g, u, n):
                    b, runs = T_GROUPS[n]
                    dve.wait_ge(tokT_psum, 3 * g + n + 1)
                    k0, t0, m = runs[0]
                    if len(runs) == 1:
                        at, src = (slice(None), u, k0, slice(P * t0, P * (t0 + m))), bank[b][:, 0:P * m]
                    else:
                        at = (slice(None), u, slice(None), slice(P * t0, P * (t0 + m)))
                        src = bank[b][:, 0:KD * P * m].rearrange("p (k s) -> p k s", k=KD)
                    dve.tensor_copy(tokT_high[at], src).then_inc(tokT_chain, 1)
                    dve.wait_ge(tokT_chain, 3 * g + n + 1)
                    dve.tensor_tensor(tokT_low[at], src, tokT_high[at].bitcast(F32), ALU.subtract).then_inc(tokT_ready, 1)

                def step(it, u, turn, live):
                    if not live(LM):
                        for n in range(3):
                            transposed(it + BEFORE, u, n)
                    else:
                        e, g = it - LM, it - LM + BEFORE
                        for c in range(KF):
                            dve.wait_ge(h_high, KF * g + c + 1)
                            dve.tensor_tensor(hT_low[:, c, :], h[:, c % RING, :], hT_high[:, c, :].bitcast(F32), ALU.subtract).then_inc(h_split, 1)
                            if live(LT) and c in T_AFTER:
                                transposed(it + BEFORE, u, T_AFTER.index(c))
                    if live(LM):
                        e, g, v = it - LM, it - LM + BEFORE, 1 - u
                        before = turn - 1 if u == 0 else turn
                        at_least(dve, y_stored[v], 16 * (before + BEFORE // 2))
                        dve.wait_ge(b2_loaded[v], 16 * (before + 1 + BEFORE // 2))
                        for t in range(TS):
                            dve.wait_ge(y_psum, TS * g + t + 1)
                            dve.tensor_tensor(y[:, v, t, :], bank[4 + t % 2][:, 0:D], b2b[:, v, :], ALU.add).then_inc(y_ready, 1)

                turns(dve, 1, step)


def combine(nc, core, out, name, call):
    NT, x = core.NT, core.x
    R = 4
    with ExitStack() as stack:
        B = Buffers(nc, stack)
        rows = B.sb(name + "c_rows", [P, R, 2, 256])
        fetched = [core.shared.sem(f"c_fetched{u}") for u in range(R)]
        added = core.shared.sem("c_added")
        stored = core.shared.sem("c_stored")
        with nc.Block() as block:

            @block.gpsimd
            def _(pool):
                for i in range(NT):
                    if i >= R:
                        pool.wait_ge(added, 2 * (i - R + 1) + 2 * NT * call)
                    for r in range(2):
                        pool.indirect_dma_start(
                            out=rows[:, i % R, r, :], out_offset=None, in_=core.expert_out[:, :],
                            in_offset=bass.IndirectOffsetOnAxis(ap=core.gather_at[:, r * NT + i:r * NT + i + 1], axis=0),
                        ).then_inc(fetched[i % R], 16)

            @block.vector
            def _(dve):
                with dve.Fori(0, NT // R) as turn:
                    for u in range(R):
                        i = R * turn + u
                        dve.wait_ge(fetched[u], 32 * (turn + 1 + NT // R * call))
                        for r in range(2):
                            if r == 1:
                                dve.wait_ge(added, 2 * i + 1 + 2 * NT * call)
                            dve.scalar_tensor_tensor(x[:, i, :], rows[:, u, r, :], core.weight[:, r, bass.ds(i, 1)], x[:, i, :],
                                                     ALU.mult, ALU.add).then_inc(added, 1)

            if out is not None:
                @block.sync
                def _(sp):
                    with sp.Fori(0, NT // R) as turn:
                        sp.wait_ge(added, 2 * R * (turn + 1) + 2 * NT * call)
                        sp.dma_start(out[bass.ds(turn * R * P, R * P), :].rearrange("(t p) d -> p t d", p=P),
                                     x[:, bass.ds(turn * R, R), :]).then_inc(stored, 16)
                    sp.wait_ge(stored, 16 * (NT // R))


def nystrom_attention(nc, core, wqkT, wvT, woT, bqk, bv, bo, rwT, rb, logits):
    x, xn_all, cst, NT = core.x, core.xn, core.cst, core.NT
    KD, BT = 2, 8
    NB = NT // BT
    PR = 8
    ITERS = 6
    SIM1, SIM2, SIM3 = 1.0 / 64, 1.0 / 1024, 1.0 / 64
    with ExitStack() as stack:
        B = Buffers(nc, stack)
        wqk = B.sb("n_wqk", [P, KD, 512])
        wv = B.sb("n_wv", [P, KD, 256])
        wo = B.sb("n_wo", [P, KD, 256])
        rw = B.sb("n_rw", [P, KD, 16])
        bias_qk = B.sb("n_bias_qk", [P, 4])
        bias_v = B.sb("n_bias_v", [P, 256])
        bias_o = B.sb("n_bias_o", [P, 256])
        bias_r = B.sb("n_bias_r", [P, 16])
        tick = B.sb("n_tick", [P, 2])
        stats = B.sb("n_stats", [P, 6])
        mv = B.sb("n_mv", [P, 2])
        rstd = B.sb("n_rstd", [P, 1])
        xln = B.sb("n_xln", [P, 2, 256])
        xlnT = B.sb("n_xlnT", [P, 2, KD, P])
        q_next = B.sb("n_q_next", [P, KD, BT * P])
        qT = B.sb("n_qT", [P, KD, BT * P])
        kT = B.sb("n_kT", [P, KD, BT * P])
        v = B.sb("n_v", [P, BT, 256])
        q_sum = B.sb("n_q_sum", [P, KD, 64])
        k_sum = B.sb("n_k_sum", [P, KD, 64])
        q_blk = B.sb("n_q_blk", [P, KD, 8, 64])
        k_blk = B.sb("n_k_blk", [P, KD, 8, 64])
        e3 = B.sb("n_e3", [P, 2, BT * P])
        e3T = B.sb("n_e3T", [P, 2, BT, P])
        max3 = B.sb("n_max3", [P, PR])
        neg3 = B.sb("n_neg3", [P, PR])
        sum3 = B.sb("n_sum3", [P, PR])
        rec3 = B.sb("n_rec3", [P, PR])
        max2 = B.sb("n_max2", [P, PR])
        sum2 = B.sb("n_sum2", [P, PR])
        s2 = B.sb("n_s2", [P, PR, 64])
        pw = B.sb("n_pw", [P, PR, 80])
        p_blk = B.sb("n_p_blk", [P, PR, P])
        q1 = B.sb("n_q1", [P, PR, 64])
        q2 = B.sb("n_q2", [P, PR, 64])
        q3 = B.sb("n_q3", [P, PR, 64])
        q3_blk = B.sb("n_q3_blk", [P, PR, P])
        z_blk = B.sb("n_z_blk", [P, PR, 34])
        max1 = B.sb("n_max1", [P, 2, 8])
        s1 = B.sb("n_s1", [P, 2, 8, 64])
        e1 = B.sb("n_e1", [P, 2, 16, 64])
        e1T = B.sb("n_e1T", [P, PR, P])
        den = B.sb("n_den", [P, 16])
        o = B.sb("n_o", [P, 2, 256])
        oT = B.sb("n_oT", [P, KD, P])
        stats2 = B.sb("n_stats2", [P, 6])
        mv2 = B.sb("n_mv2", [P, 2])
        rstd2 = B.sb("n_rstd2", [P, 1])
        xr = B.sb("n_xr", [P, 2, 256])
        xrT = B.sb("n_xrT", [P, KD, P])
        psum, bank = core.psum, core.bank

        names = ("loaded made ln_chain rstd_ready xln_ready xlnT_psum xlnT_ready qk_psum v_psum qk_ready v_ready sums_ready "
                 "q_moved q_blk_ready k_blk_ready s2_psum s2_chain s2_shifted e2_ready k_ready kT_psum kT_ready kT_blk_ready "
                 "s3_psum s3_chain neg3_ready e3_ready e3T_psum e3Ta_ready e3Tb_ready b3_psum b3_chain w_ready "
                 "xa_psum xb_psum xa_read xb_read ya_psum yb_psum ya_read yb_read "
                 "s1_psum s1_chain s1_shifted e1_ready e1T_psum e1Ta_ready e1Tb_ready o_psum o_chain o_ready oT_psum oT_ready "
                 "y_psum x_chain r_rstd xr_ready xr_kept xrT_psum xrT_ready logits_psum logits_read").split()
        S = {name: B.sem("n_" + name) for name in names}
        ident = cst[:, C_IDENT:C_IDENT + P]
        eye = [cst[:, C_EYE7 + 64 * n:C_EYE7 + 64 * n + 64].unsqueeze(1).to_broadcast([P, 4, 64]) for n in range(3)]
        TOP, LOW = slice(0, 64), slice(64, P)

        X_PER, Y_PER = 1 + 3 * ITERS - 1, 1 + ITERS

        def x_count(b, n, what):
            return X_PER * b + (1 if n < 0 else 1 + 3 * n + what + 1)

        def y_count(b, n):
            return Y_PER * b + n + 2

        def projections(between, project, b):
            for slot in range(2 * BT + 3):
                between(slot)
                for lag, stage in ((0, "stats"), (1, "normalise"), (2, "transpose"), (4, "v"), (3, "qk")):
                    t, odd = divmod(slot - lag, 2)
                    if not odd and 0 <= t < BT:
                        project(b, t, stage)

        def batches(eng, project, pairs, inverse, rows):
            def tail(b, step):
                if not (isinstance(b, int) and b < 0):
                    rows(b, BT + step)

            def body(b, more):
                pairs(b, "open")
                tail(b - 1, 0)
                pairs(b, "landmarks")
                for step in range(PR + 1):
                    pairs(b, step)
                    if step < 2:
                        tail(b - 1, step + 1)
                pairs(b, "close")
                pairs(b, PR + 1)

                def products(slot):
                    for group in range(2):
                        inverse(b, (slot + 2) // 3 - 1, (slot + 2) % 3, group)

                if more:
                    projections(products, project, b + 1)
                else:
                    for slot in range(3 * ITERS + 1):
                        products(slot)
                for step in range(BT):
                    rows(b, step)

            projections(lambda slot: None, project, 0)
            body(0, True)
            with eng.Fori(1, NB - 1) as b:
                body(b, True)
            body(NB - 1, False)
            for step in range(3):
                tail(NB - 1, step)

        with nc.Block() as block:

            @block.sync
            def _(sp):
                for dst, src in ((wqk, wqkT), (wv, wvT), (wo, woT), (rw, rwT)):
                    sp.dma_start(dst[:, :, :], src.rearrange("(k p) n -> p k n", p=P)).then_inc(S["loaded"], 16)
                sp.dma_start(bias_qk[:, :], bqk.rearrange("(g p) -> p g", p=P), allow_slow_non_contiguous=True).then_inc(S["loaded"], 16)
                sp.dma_start(bias_v[:, :], bv[None, :].to_broadcast([P, 256])).then_inc(S["loaded"], 16)
                sp.dma_start(bias_o[:, :], bo[None, :].to_broadcast([P, 256])).then_inc(S["loaded"], 16)
                sp.dma_start(bias_r[:, :], rb[None, :].to_broadcast([P, 16])).then_inc(S["loaded"], 16)

            @block.gpsimd
            def _(pool):
                pool.memset(p_blk[:, :, :], 0.0).then_inc(S["made"], 1)
                pool.memset(q3_blk[:, :, :], 0.0).then_inc(S["made"], 1)
                pool.memset(z_blk[:, :, :], 0.0).then_inc(S["made"], 1)
                pool.wait_ge(S["made"], 3)
                pool.memset(z_blk[TOP, :, 16:17], 1.0).then_inc(S["made"], 1)
                pool.memset(z_blk[LOW, :, 33:34], 1.0).then_inc(S["made"], 1)

                def project(b, t, stage):
                    if stage == "stats":
                        pool.wait_ge(S["ln_chain"], 3 * (BT * b + t) + 3)
                        pool.tensor_tensor(rstd[:, :], mv[:, 1:2], core.minus_half[:, :], ALU.pow).then_inc(S["rstd_ready"], 1)

                def pairs(b, step):
                    if step == 2:
                        pool.wait_ge(S["sums_ready"], 2 * BT * b + 2 * BT)
                        at_least(pool, S["s1_psum"], 2 * BT * b)
                        for k in range(KD):
                            ins = pool.tensor_tensor(k_blk[:, k, :, :], k_sum[:, k:k + 1, :].to_broadcast([P, 8, 64]),
                                                     cst[:, C_HEAD8:C_HEAD8 + 8].unsqueeze(2).to_broadcast([P, 8, 64]), ALU.mult)
                        ins.then_inc(S["k_blk_ready"], 1)
                        pool.tensor_copy(qT[:, :, :], q_next[:, :, :]).then_inc(S["q_moved"], 1)

                def inverse(b, n, what, group):
                    pass

                def rows(b, step):
                    if 0 <= step - 2 < BT:
                        i = BT * b + step - 2
                        pool.wait_ge(S["x_chain"], 5 * i + 5)
                        pool.tensor_tensor(rstd2[:, :], mv2[:, 1:2], core.minus_half[:, :], ALU.pow).then_inc(S["r_rstd"], 1)
                        pool.wait_ge(S["xr_ready"], i + 1)
                        pool.tensor_copy(xn_all[:, i, :], xr[:, step % 2, :]).then_inc(S["xr_kept"], 1)

                batches(pool, project, pairs, inverse, rows)

            @block.scalar
            def _(act):
                act.wait_ge(S["loaded"], 16 * 8)
                act.wait_ge(S["made"], 5)

                def project(b, t, stage):
                    i = BT * b + t
                    if stage == "transpose":
                        act.wait_ge(S["xlnT_psum"], i + 1)
                        at_least(act, S["v_psum"], i - 1)
                        act.activation(xlnT[:, t % 2, :, :], bank[4][:, 0:256].rearrange("p (k t) -> p k t", k=KD), ACT.Copy).then_inc(S["xlnT_ready"], 1)
                    if stage == "qk":
                        act.wait_ge(S["qk_psum"], i + 1)
                        if t == 0:
                            at_least(act, S["q_moved"], b)
                            at_least(act, S["s3_psum"], PR * b)
                        for g in range(4):
                            dst = (q_next, kT)[g // 2]
                            ins = act.activation(dst[:, g % 2, P * t:P * t + P], bank[5][:, P * g:P * g + P], ACT.Identity, bias=bias_qk[:, g:g + 1])
                        ins.then_inc(S["qk_ready"], 1)

                def pairs(b, step):
                    if step == "landmarks":
                        act.wait_ge(S["s2_shifted"], b + 1)
                        act.activation(s2[:, :, :], s2[:, :, :], ACT.Exp, scale=SIM2).then_inc(S["e2_ready"], 1)
                    elif isinstance(step, int):
                        if step < PR:
                            n = PR * b + step
                            act.wait_ge(S["neg3_ready"], n + 1)
                            at_least(act, S["e3T_psum"], 2 * (PR * b + max(step - 1, 0)))
                            act.activation(e3[:, step % 2, :].rearrange("p (a s) -> p a s", a=2),
                                           psum[:, 2 * (step % 2):2 * (step % 2) + 2, :], ACT.Exp, scale=SIM3,
                                           bias=neg3[:, step:step + 1], accum_out=sum3[:, step:step + 1]).then_inc(S["e3_ready"], 1)
                        if 1 <= step <= PR:
                            n, u = PR * b + step - 1, (step - 1) % 2
                            act.wait_ge(S["e3T_psum"], 2 * n + 1)
                            at_least(act, S["b3_psum"], PR * b + max(step - 2, 0))
                            act.activation(e3T[:, u, 0:4, :], bank[4][:, :].rearrange("p (a s) -> p a s", a=4), ACT.Copy).then_inc(S["e3Ta_ready"], 1)
                    elif step == "close":
                        act.wait_ge(S["kT_psum"], 2 * b + 2)
                        for half in range(2):
                            src = bank[4 + half][:, :].rearrange("p (a s) -> p a s", a=4)
                            act.activation(q3_blk[TOP, 4 * half:4 * half + 4, 0:64], src[TOP, :, 0:64], ACT.Copy)
                            act.activation(q3_blk[LOW, 4 * half:4 * half + 4, 64:P], src[LOW, :, 64:P], ACT.Copy).then_inc(S["kT_blk_ready"], 1)

                def inverse(b, n, what, group):
                    if what != 2:
                        return
                    g4 = slice(4 * group, 4 * group + 4)
                    scale = 1.0 if n < 0 else 0.25
                    y = bank[1 + 2 * group][:, 0:320].rearrange("p (a c) -> p a c", a=4)
                    act.wait_ge(S["y%s_psum" % "ab"[group]], y_count(b, n))
                    if n == ITERS - 1:
                        at_least(act, S["o_psum"], BT * b)
                        act.activation(z_blk[TOP, g4, 0:16], y[TOP, :, 64:80], ACT.Copy, scale=scale)
                        act.activation(z_blk[LOW, g4, 17:33], y[LOW, :, 64:80], ACT.Copy, scale=scale).then_inc(S["y%s_read" % "ab"[group]], 1)
                        return
                    act.wait_ge(S["x%s_psum" % "ab"[group]], x_count(b, n, 2))
                    act.activation(p_blk[TOP, g4, 0:64], y[TOP, :, 0:64], ACT.Copy, scale=scale)
                    act.activation(p_blk[LOW, g4, 64:P], y[LOW, :, 0:64], ACT.Copy, scale=scale)
                    act.activation(pw[:, g4, :], y[:, :, :], ACT.Copy, scale=scale).then_inc(S["y%s_read" % "ab"[group]], 1)

                def rows(b, step):
                    def exponentials(half):
                        if step < BT:
                            act.wait_ge(S["s1_shifted"], 2 * (BT * b + step) + half + 1)
                            at_least(act, S["e1T_psum"], 2 * (BT * b + max(step - 1, 0)))
                            act.activation(e1[:, step % 2, 8 * half:8 * half + 8, :], s1[:, half, :, :], ACT.Exp, scale=SIM1).then_inc(S["e1_ready"], 1)

                    exponentials(0)
                    if 0 <= step - 2 < BT:
                        i = BT * b + step - 2
                        act.wait_ge(S["oT_psum"], i + 1)
                        at_least(act, S["y_psum"], i)
                        act.activation(oT[:, :, :], bank[5][:, 0:256].rearrange("p (k t) -> p k t", k=KD), ACT.Copy).then_inc(S["oT_ready"], 1)
                    exponentials(1)
                    if 0 <= step - 1 < BT:
                        i = BT * b + step - 1
                        act.wait_ge(S["e1T_psum"], 2 * i + 1)
                        at_least(act, S["o_psum"], i)
                        act.activation(e1T[:, 0:4, :], bank[2][:, :].rearrange("p (a s) -> p a s", a=4), ACT.Copy).then_inc(S["e1Ta_ready"], 1)
                    if 0 <= step - 3 < BT:
                        i = BT * b + step - 3
                        act.wait_ge(S["xrT_psum"], i + 1)
                        at_least(act, S["logits_psum"], i)
                        act.activation(xrT[:, :, :], bank[6][:, 0:256].rearrange("p (k t) -> p k t", k=KD), ACT.Copy).then_inc(S["xrT_ready"], 1)

                batches(act, project, pairs, inverse, rows)

            @block.tensor
            def _(pe):
                pe.wait_ge(S["loaded"], 16 * 8)
                pe.wait_ge(S["made"], 5)

                def project(b, t, stage):
                    i, u = BT * b + t, t % 2
                    if stage == "transpose":
                        pe.wait_ge(S["xln_ready"], i + 1)
                        at_least(pe, S["xlnT_ready"], i)
                        for k in range(KD):
                            ins = pe.transpose(bank[4][:, P * k:P * k + P], xln[:, u, P * k:P * k + P], ident)
                        ins.then_inc(S["xlnT_psum"], 1)
                    if stage == "qk":
                        pe.wait_ge(S["xlnT_ready"], i + 1)
                        at_least(pe, S["qk_ready"], i)
                        for g in range(4):
                            for k in range(KD):
                                ins = pe.matmul(bank[5][:, P * g:P * g + P], wqk[:, k, P * g:P * g + P], xlnT[:, u, k, :],
                                                start=(k == 0), stop=(k == KD - 1))
                        ins.then_inc(S["qk_psum"], 1)
                    if stage == "v":
                        at_least(pe, S["v_ready"], i)
                        for k in range(KD):
                            ins = pe.matmul(bank[6][:, 0:256], xlnT[:, u, k, :], wv[:, k, :], start=(k == 0), stop=(k == KD - 1))
                        ins.then_inc(S["v_psum"], 1)

                def pairs(b, step):
                    if step == "landmarks":
                        pe.wait_ge(S["q_blk_ready"], b + 1)
                        for pr in range(PR):
                            ins = pe.matmul(bank[7][:, 64 * pr:64 * pr + 64], q_blk[:, pr // 4, 2 * (pr % 4):2 * (pr % 4) + 2, :],
                                            k_sum[:, pr // 4, :], start=True, stop=True)
                        ins.then_inc(S["s2_psum"], 1)
                    if step == "close":
                        pe.wait_ge(S["k_ready"], b + 1)
                        for half in range(2):
                            at_least(pe, S["e3T%s_ready" % "ab"[half]], PR * b + PR)
                            for pr in range(4 * half, 4 * half + 4):
                                ins = pe.transpose(bank[4 + half][:, P * (pr % 4):P * (pr % 4) + P], p_blk[:, pr, :], ident)
                            ins.then_inc(S["kT_psum"], 1)
                    if not isinstance(step, int):
                        return
                    if step < PR:
                        n, pr = PR * b + step, step
                        if step == 0:
                            at_least(pe, S["s1_shifted"], 2 * BT * b)
                        else:
                            at_least(pe, S["e3_ready"], PR * b + step - 1)
                        for c in range(2):
                            ins = pe.matmul(bank[2 * (step % 2) + c][:, :], q_blk[:, pr // 4, 2 * (pr % 4):2 * (pr % 4) + 2, :],
                                            kT[:, pr // 4, 512 * c:512 * c + 512], start=True, stop=True)
                        ins.then_inc(S["s3_psum"], 1)
                    if step >= 2:
                        n, pr, u = PR * b + step - 2, step - 2, step % 2
                        pe.wait_ge(S["e3Ta_ready"], n + 1)
                        pe.wait_ge(S["e3Tb_ready"], n + 1)
                        if step == 2:
                            at_least(pe, S["logits_read"], BT * b)
                        for s in range(BT):
                            ins = pe.matmul(bank[6][:, 32 * pr:32 * pr + 32], e3T[:, u, s, :], v[:, s, 32 * pr:32 * pr + 32],
                                            start=(s == 0), stop=(s == BT - 1))
                        ins.then_inc(S["b3_psum"], 1)
                    if 1 <= step <= PR:
                        n, u = PR * b + step - 1, (step - 1) % 2
                        pe.wait_ge(S["e3_ready"], n + 1)
                        if step == 1:
                            at_least(pe, S["o_ready"], BT * b)
                            at_least(pe, S["x_chain"], 5 * BT * b - 4)
                        for c in range(2):
                            at_least(pe, S["e3T%s_ready" % "ab"[c]], n)
                            for s in range(4 * c, 4 * c + 4):
                                ins = pe.transpose(bank[4 + c][:, P * (s % 4):P * (s % 4) + P], e3[:, u, P * s:P * s + P], ident)
                            ins.then_inc(S["e3T_psum"], 1)

                def inverse(b, n, what, group):
                    ab = "ab"[group]
                    xb, yb = bank[2 * group], bank[1 + 2 * group]
                    xs, ys = S["x%s_psum" % ab], S["y%s_psum" % ab]
                    g4 = range(4 * group, 4 * group + 4)
                    if n < 0:
                        pe.wait_ge(S["kT_blk_ready"], 2 * b + 2)
                        pe.wait_ge(S["kT_ready"], b + 1)
                        pe.wait_ge(S["w_ready"], b + 1)
                    else:
                        pe.wait_ge(S["x%s_read" % ab], x_count(b, n, what - 1) if what else x_count(b, n - 1, 2))
                        if what == 0:
                            pe.wait_ge(S["y%s_read" % ab], y_count(b, n - 1))
                    if what < 2:
                        for pr in g4:
                            ins = pe.matmul(xb[:, 64 * (pr % 4):64 * (pr % 4) + 64], p_blk[:, pr, :], (q1, q2)[what][:, pr, :],
                                            start=True, stop=True)
                        ins.then_inc(xs, 1)
                        return
                    lo = 0 if n < ITERS - 1 else 64
                    for pr in g4:
                        ins = pe.matmul(yb[:, 80 * (pr % 4) + lo:80 * (pr % 4) + 80], q3_blk[:, pr, :], pw[:, pr, lo:80],
                                        start=True, stop=True)
                    ins.then_inc(ys, 1)
                    if n < ITERS - 1:
                        for pr in g4:
                            ins = pe.matmul(xb[:, 64 * (pr % 4):64 * (pr % 4) + 64], p_blk[:, pr, :], q3[:, pr, :],
                                            start=True, stop=True)
                        ins.then_inc(xs, 1)

                def rows(b, step):
                    if step < BT:
                        i = BT * b + step
                        if step == 0:
                            pe.wait_ge(S["q_moved"], b + 1)
                            pe.wait_ge(S["k_blk_ready"], b + 1)
                            for ab in "ab":
                                pe.wait_ge(S["y%s_read" % ab], Y_PER * (b + 1))
                        for half in range(2):
                            at_least(pe, S["s1_shifted"], 2 * BT * b + max(2 * step + half - 1, 0))
                            pe.matmul(bank[half][:, :], qT[:, half, P * step:P * step + P], k_blk[:, half, :, :],
                                      start=True, stop=True).then_inc(S["s1_psum"], 1)
                    if 0 <= step - 2 < BT:
                        i, u = BT * b + step - 2, step % 2
                        pe.wait_ge(S["o_ready"], i + 1)
                        at_least(pe, S["x_chain"], 5 * BT * b + max(5 * (step - 3) + 1, 0))
                        for k in range(KD):
                            ins = pe.transpose(bank[5][:, P * k:P * k + P], o[:, u, P * k:P * k + P], ident)
                        ins.then_inc(S["oT_psum"], 1)
                    if 0 <= step - 1 < BT:
                        i, u = BT * b + step - 1, (step - 1) % 2
                        pe.wait_ge(S["e1_ready"], 2 * i + 2)
                        for c in range(2):
                            at_least(pe, S["e1T%s_ready" % "ab"[c]], i)
                            for pr in range(4 * c, 4 * c + 4):
                                ins = pe.transpose(bank[2 + c][:, P * (pr % 4):P * (pr % 4) + P], e1[:, u, 2 * pr:2 * pr + 2, :], ident)
                            ins.then_inc(S["e1T_psum"], 1)
                    if 0 <= step - 2 < BT:
                        i = BT * b + step - 2
                        pe.wait_ge(S["oT_ready"], i + 1)
                        for k in range(KD):
                            ins = pe.matmul(bank[5][:, 256:512], oT[:, k, :], wo[:, k, :], start=(k == 0), stop=(k == KD - 1))
                        ins.then_inc(S["y_psum"], 1)
                    if 0 <= step - 3 < BT:
                        i, u = BT * b + step - 3, (step - 3) % 2
                        pe.wait_ge(S["xr_ready"], i + 1)
                        at_least(pe, S["logits_read"], i)
                        for k in range(KD):
                            ins = pe.transpose(bank[6][:, P * k:P * k + P], xr[:, u, P * k:P * k + P], ident)
                        ins.then_inc(S["xrT_psum"], 1)
                    if 0 <= step - 1 < BT:
                        i, u = BT * b + step - 1, (step - 1) % 2
                        at_least(pe, S["o_ready"], i)
                        for pr in range(PR):
                            if pr % 4 == 0:
                                pe.wait_ge(S["e1T%s_ready" % "ab"[pr // 4]], i + 1)
                            ins = pe.matmul(bank[4][:, 34 * pr:34 * pr + 34], e1T[:, pr, :], z_blk[:, pr, :], start=True, stop=True)
                        ins.then_inc(S["o_psum"], 1)
                    if 0 <= step - 3 < BT:
                        i = BT * b + step - 3
                        pe.wait_ge(S["xrT_ready"], i + 1)
                        for k in range(KD):
                            ins = pe.matmul(bank[6][:, 256:272], xrT[:, k, :], rw[:, k, :], start=(k == 0), stop=(k == KD - 1))
                        ins.then_inc(S["logits_psum"], 1)

                batches(pe, project, pairs, inverse, rows)

            @block.vector
            def _(dve):
                dve.wait_ge(S["loaded"], 16 * 8)
                dve.wait_ge(S["made"], 5)

                def variance(src, st, m, chain, done):
                    dve.memset(tick[:, 0:1], 0.0)
                    dve.bn_stats(st, src).then_inc(chain, 1)
                    at_least(dve, chain, done + 1)
                    dve.memset(tick[:, 1:2], 0.0)
                    dve.bn_aggr(m, st).then_inc(chain, 1)
                    at_least(dve, chain, done + 2)
                    dve.tensor_scalar(m[:, 1:2], m[:, 1:2], LN_EPS, None, ALU.add).then_inc(chain, 1)

                def project(b, t, stage):
                    i, u = BT * b + t, t % 2
                    if stage == "stats":
                        at_least(dve, S["xln_ready"], i)
                        variance(x[:, i, :], stats[:, :], mv[:, :], S["ln_chain"], 3 * i)
                    if stage == "normalise":
                        dve.wait_ge(S["rstd_ready"], i + 1)
                        at_least(dve, S["xlnT_psum"], i - 1)
                        dve.tensor_scalar(xln[:, u, :], x[:, i, :], mv[:, 0:1], rstd[:, :], ALU.subtract, ALU.mult).then_inc(S["xln_ready"], 1)
                    if stage == "v":
                        dve.wait_ge(S["v_psum"], i + 1)
                        if t == 0:
                            at_least(dve, S["b3_psum"], PR * b)
                        dve.tensor_tensor(v[:, t, :], bank[6][:, 0:256], bias_v[:, :], ALU.add).then_inc(S["v_ready"], 1)
                        dve.wait_ge(S["qk_ready"], i + 1)
                        if t == 0:
                            at_least(dve, S["k_blk_ready"], b)
                            at_least(dve, S["s2_psum"], b)
                        for dst, src in ((q_sum, q_next), (k_sum, kT)):
                            dve.tensor_reduce(dst[:, :, 8 * t:8 * t + 8], src[:, :, P * t:P * t + P].rearrange("p k (j l) -> p k j l", l=16),
                                              AX_X, ALU.add).then_inc(S["sums_ready"], 1)

                def pairs(b, step):
                    if step == "open":
                        dve.wait_ge(S["sums_ready"], 2 * BT * b + 2 * BT)
                        at_least(dve, S["s3_psum"], PR * b)
                        for k in range(KD):
                            ins = dve.tensor_tensor(q_blk[:, k, :, :], q_sum[:, k:k + 1, :].to_broadcast([P, 8, 64]),
                                                    cst[:, C_HEAD8:C_HEAD8 + 8].unsqueeze(2).to_broadcast([P, 8, 64]), ALU.mult)
                        ins.then_inc(S["q_blk_ready"], 1)
                    if step == "landmarks":
                        s2_ps = bank[7][:, :].rearrange("p (a c) -> p a c", a=PR)
                        dve.wait_ge(S["s2_psum"], b + 1)
                        dve.tensor_reduce(max2[:, :], s2_ps, AX_X, ALU.max).then_inc(S["s2_chain"], 1)
                        dve.wait_ge(S["s2_chain"], 3 * b + 1)
                        dve.tensor_tensor(s2[:, :, :], s2_ps, max2[:, :].unsqueeze(2).to_broadcast([P, PR, 64]), ALU.subtract).then_inc(S["s2_shifted"], 1)
                    if step == "close":
                        dve.wait_ge(S["kT_blk_ready"], 2 * b + 2)
                        for half in range(2):
                            src = bank[4 + half][:, :].rearrange("p (a s) -> p a s", a=4)
                            dve.tensor_copy(q3[TOP, 4 * half:4 * half + 4, :], src[TOP, :, 0:64])
                            ins = dve.tensor_copy(q3[LOW, 4 * half:4 * half + 4, :], src[LOW, :, 64:P])
                        ins.then_inc(S["kT_ready"], 1)
                        dve.wait_ge(S["e3_ready"], PR * b + PR)
                        dve.reciprocal(rec3[:, :], sum3[:, :]).then_inc(S["b3_chain"], 1)
                        dve.wait_ge(S["b3_psum"], PR * b + PR)
                        dve.wait_ge(S["b3_chain"], b + 1)
                        b3 = bank[6][:, 0:256].rearrange("p (a c) -> p a c", a=PR)
                        r3 = rec3[:, :].unsqueeze(2).to_broadcast([P, PR, 16])
                        dve.tensor_tensor(pw[TOP, :, 64:80], b3[TOP, :, 0:16], r3[TOP], ALU.mult)
                        dve.tensor_tensor(pw[LOW, :, 64:80], b3[LOW, :, 16:32], r3[LOW], ALU.mult).then_inc(S["w_ready"], 1)
                    if not isinstance(step, int):
                        return
                    if step < PR:
                        n = PR * b + step
                        dve.wait_ge(S["s3_psum"], n + 1)
                        dve.tensor_reduce(max3[:, step:step + 1], psum[:, 2 * (step % 2):2 * (step % 2) + 2, :], AX_XY, ALU.max).then_inc(S["s3_chain"], 1)
                        dve.wait_ge(S["s3_chain"], n + 1)
                        at_least(dve, S["e3_ready"], PR * b)
                        dve.tensor_scalar(neg3[:, step:step + 1], max3[:, step:step + 1], -SIM3, None, ALU.mult).then_inc(S["neg3_ready"], 1)
                    if 1 <= step <= PR:
                        n, u = PR * b + step - 1, (step - 1) % 2
                        dve.wait_ge(S["e3T_psum"], 2 * n + 2)
                        at_least(dve, S["b3_psum"], PR * b + max(step - 2, 0))
                        dve.tensor_copy(e3T[:, u, 4:8, :], bank[5][:, :].rearrange("p (a s) -> p a s", a=4)).then_inc(S["e3Tb_ready"], 1)
                    if step == 2:
                        dve.wait_ge(S["e2_ready"], b + 1)
                        dve.tensor_reduce(sum2[:, :], s2[:, :, :], AX_X, ALU.add).then_inc(S["s2_chain"], 1)
                        dve.wait_ge(S["s2_chain"], 3 * b + 2)
                        dve.reciprocal(max2[:, :], sum2[:, :]).then_inc(S["s2_chain"], 1)
                        dve.wait_ge(S["s2_chain"], 3 * b + 3)
                        rec2 = max2[:, :].unsqueeze(2).to_broadcast([P, PR, 64])
                        dve.tensor_tensor(pw[:, :, 0:64], s2[:, :, :], rec2, ALU.mult)
                        dve.tensor_tensor(p_blk[TOP, :, 0:64], s2[TOP, :, :], rec2[TOP], ALU.mult)
                        dve.tensor_tensor(p_blk[LOW, :, 64:P], s2[LOW, :, :], rec2[LOW], ALU.mult).then_inc(S["k_ready"], 1)

                def inverse(b, n, what, group):
                    ab = "ab"[group]
                    g4 = slice(4 * group, 4 * group + 4)
                    xb = bank[2 * group][:, 0:256].rearrange("p (a c) -> p a c", a=4)
                    if what == 2 and n == ITERS - 1:
                        return
                    dve.wait_ge(S["x%s_psum" % ab], x_count(b, n, what))
                    done = S["x%s_read" % ab]
                    if what == 2:
                        dve.scalar_tensor_tensor(q1[:, g4, :], xb, -1.0 if n < 0 else -0.25, eye[0], ALU.mult, ALU.add).then_inc(done, 1)
                    elif what == 0:
                        dve.scalar_tensor_tensor(q2[:, g4, :], xb, -1.0, eye[1], ALU.mult, ALU.add).then_inc(done, 1)
                    else:
                        dve.scalar_tensor_tensor(q3_blk[TOP, g4, 0:64], xb[TOP], -1.0, eye[2][TOP], ALU.mult, ALU.add)
                        dve.scalar_tensor_tensor(q3_blk[LOW, g4, 64:P], xb[LOW], -1.0, eye[2][LOW], ALU.mult, ALU.add)
                        dve.scalar_tensor_tensor(q3[:, g4, :], xb, -1.0, eye[2], ALU.mult, ALU.add).then_inc(done, 1)

                def rows(b, step):
                    if step < BT:
                        for half in range(2):
                            n = 2 * (BT * b + step) + half
                            s_ps = bank[half][:, :].rearrange("p (h j) -> p h j", h=8)
                            dve.wait_ge(S["s1_psum"], n + 1)
                            dve.tensor_reduce(max1[:, half, :], s_ps, AX_X, ALU.max).then_inc(S["s1_chain"], 1)
                            dve.wait_ge(S["s1_chain"], n + 1)
                            at_least(dve, S["e1_ready"], 2 * BT * b + max(2 * step + half - 1, 0))
                            dve.tensor_tensor(s1[:, half, :, :], s_ps, max1[:, half, :].unsqueeze(2).to_broadcast([P, 8, 64]),
                                              ALU.subtract).then_inc(S["s1_shifted"], 1)
                    if 0 <= step - 1 < BT:
                        i, u = BT * b + step - 1, (step - 1) % 2
                        dve.wait_ge(S["e1T_psum"], 2 * i + 2)
                        at_least(dve, S["o_psum"], i)
                        dve.tensor_copy(e1T[:, 4:8, :], bank[3][:, :].rearrange("p (a s) -> p a s", a=4)).then_inc(S["e1Tb_ready"], 1)
                    if 0 <= step - 2 < BT:
                        i, u = BT * b + step - 2, step % 2
                        dve.wait_ge(S["y_psum"], i + 1)
                        dve.tensor_tensor(x[:, i, :], x[:, i, :], bank[5][:, 256:512], ALU.add).then_inc(S["x_chain"], 1)
                        dve.wait_ge(S["x_chain"], 5 * i + 1)
                        dve.tensor_tensor(x[:, i, :], x[:, i, :], bias_o[:, :], ALU.add).then_inc(S["x_chain"], 1)
                        dve.wait_ge(S["x_chain"], 5 * i + 2)
                        variance(x[:, i, :], stats2[:, :], mv2[:, :], S["x_chain"], 5 * i + 2)
                    if 0 <= step - 1 < BT:
                        i, u = BT * b + step - 1, (step - 1) % 2
                        ops = bank[4][:, 0:272].rearrange("p (h e) -> p h e", h=16)
                        dve.wait_ge(S["o_psum"], i + 1)
                        dve.reciprocal(den[:, :], ops[:, :, 16]).then_inc(S["o_chain"], 1)
                        dve.wait_ge(S["o_chain"], i + 1)
                        at_least(dve, S["oT_psum"], BT * b + max(step - 2, 0))
                        dve.tensor_tensor(o[:, u, :].rearrange("p (h e) -> p h e", h=16), ops[:, :, 0:16],
                                          den[:, :].unsqueeze(2).to_broadcast([P, 16, 16]), ALU.mult).then_inc(S["o_ready"], 1)
                    if 0 <= step - 2 < BT:
                        i, u = BT * b + step - 2, step % 2
                        dve.wait_ge(S["r_rstd"], i + 1)
                        at_least(dve, S["xrT_psum"], BT * b + max(step - 3, 0))
                        at_least(dve, S["xr_kept"], BT * b + max(step - 3, 0))
                        dve.tensor_scalar(xr[:, u, :], x[:, i, :], mv2[:, 0:1], rstd2[:, :], ALU.subtract, ALU.mult).then_inc(S["xr_ready"], 1)
                    if 0 <= step - 3 < BT:
                        i = BT * b + step - 3
                        dve.wait_ge(S["logits_psum"], i + 1)
                        dve.tensor_tensor(logits[:, i, :], bank[6][:, 256:272], bias_r[:, :], ALU.add).then_inc(S["logits_read"], 1)

                batches(dve, project, pairs, inverse, rows)


class Core:
    pass


def build_program(nc, a, out):
    with ExitStack() as stack:
        B = Buffers(nc, stack)
        core = Core()
        core.NT, core.NE, core.CAP = 32, 16, 640
        slots, spare = core.NE * core.CAP, 2 * core.NT * P
        core.x = B.sb("x_tokens", [P, core.NT, 256])
        core.cst = B.sb("const", [P, C_WIDTH])
        core.cst_dram = a["const"]
        core.minus_half = B.sb("minus_half", [P, 1])
        core.gather_at = B.sb("gather_at", [P, 2 * core.NT], I32)
        core.weight = B.sb("gate_weight", [P, 2, core.NT])
        logits = B.sb("logits", [P, core.NT, core.NE])
        core.psum = B.ps("psum", [P, 8, 512])
        core.bank = [core.psum[:, i, :] for i in range(8)]
        core.slots_dram = nc.dram_tensor("slots_dram", [slots + spare, 256], F32, kind="Internal").ap()
        core.expert_out = nc.dram_tensor("expert_out", [slots, 256], F32, kind="Internal").ap()
        core.zeroed = B.sem("zeroed")
        core.shared = Shared(B)

        with ExitStack() as tokens:
            core.xn = Buffers(nc, tokens).sb("xn_tokens_a", [P, core.NT, 256])
            linear_attention(nc, core, a["x"], a["a_wqkT"], a["a_wvT"], a["a_woT"], a["a_bqk"], a["a_bv"], a["a_bo"],
                             a["rwT"], a["rb"], logits)
            route_and_dispatch(nc, core, logits, "f_", 0)
        experts(nc, core, a["w1"], a["b1"], a["w2"], a["b2"], "f_", 0)
        combine(nc, core, None, "f_", 0)
        with ExitStack() as tokens:
            core.xn = Buffers(nc, tokens).sb("xn_tokens_b", [P, core.NT, 256])
            nystrom_attention(nc, core, a["n_wqk"], a["n_wv"], a["n_wo"], a["n_bqk"], a["n_bv"], a["n_bo"],
                              a["rwT"], a["rb"], logits)
            route_and_dispatch(nc, core, logits, "g_", 1)
        experts(nc, core, a["w1"], a["b1"], a["w2"], a["b2"], "g_", 1)
        combine(nc, core, out, "g_", 1)


def kernel(**inputs):
    import concourse.bacc as _bacc
    from concourse.bass_utils import run_bass_kernel_spmd as _run

    z = {k.removeprefix("L0_"): np.asarray(v) for k, v in inputs.items()}
    wqkv, bqkv = z["attn_b_Wqkv"], z["attn_b_bqkv"]
    arrays = {
        "x": z["attn_a_x"].reshape(4096, 256),
        "const": constants(8, 32),
        "a_wqkT": np.concatenate([z["attn_a_Wq"], z["attn_a_Wk"]]).T,
        "a_wvT": z["attn_a_Wv"].T,
        "a_woT": z["attn_a_Wo"].T,
        "a_bqk": np.concatenate([z["attn_a_bq"], z["attn_a_bk"]]),
        "a_bv": z["attn_a_bv"],
        "a_bo": z["attn_a_bo"],
        "rwT": z["ffn_router_w"].T,
        "rb": z["ffn_router_b"],
        "w1": z["ffn_w1"],
        "b1": z["ffn_b1"].reshape(16, 8, P).transpose(0, 2, 1),
        "w2": z["ffn_w2"],
        "b2": z["ffn_b2"],
        "n_wqk": wqkv[:, :512],
        "n_wv": wqkv[:, 512:],
        "n_wo": z["attn_b_Wout"],
        "n_bqk": bqkv[:512],
        "n_bv": bqkv[512:],
        "n_bo": z["attn_b_bout"],
    }
    arrays = {k: np.ascontiguousarray(v) for k, v in arrays.items()}
    nc = _bacc.Bacc("TRN2", target_bir_lowering=False, num_devices=1)
    aps = {k: nc.dram_tensor("in_" + k, v.shape, mybir.dt.from_np(v.dtype), kind="ExternalInput").ap() for k, v in arrays.items()}
    out = nc.dram_tensor("out", [4096, 256], F32, kind="ExternalOutput").ap()
    build_program(nc, aps, out)
    r = _run(nc, [{"in_" + k: v for k, v in arrays.items()}], core_ids=[0])
    return np.asarray(r.results[0]["out"]).reshape(4, 1024, 256)
```

```python
from contextlib import ExitStack

import concourse.bass as bass
import numpy as np
from concourse import mybir

F32 = mybir.dt.float32
BF16 = mybir.dt.bfloat16
F32R = mybir.dt.float32r
I32 = mybir.dt.int32
ALU = mybir.AluOpType
ACT = mybir.ActivationFunctionType
AX_X = mybir.AxisListType.X
AX_XY = mybir.AxisListType.XY

P = 128
LN_EPS = 1e-5
DEN_EPS = 1e-6

C_IDENT = 0
C_CAUSAL = 128
C_HEAD8 = 256
C_BLOCK = 264
C_KEEP = 536
C_STRICT = 568
C_IOTA = 696
C_EYE7 = 712
C_TRASH = 904
C_WIDTH = 968


def constants(batch_tiles, tiles):
    c = np.zeros((P, C_WIDTH), np.float32)
    p = np.arange(P)[:, None]
    col = np.arange(P)[None, :]
    c[:, C_IDENT:C_IDENT + P] = p == col
    c[:, C_CAUSAL:C_CAUSAL + P] = p <= col
    c[:, C_HEAD8:C_HEAD8 + 8] = p // 16 == np.arange(8)[None, :]
    c[:, C_BLOCK:C_BLOCK + 272] = p // 16 == (np.arange(272) // 17 % 8)[None, :]
    c[:, C_KEEP:C_KEEP + tiles] = (np.arange(tiles) + 1) % batch_tiles != 0
    c[:, C_STRICT:C_STRICT + P] = p < col
    c[:, C_IOTA:C_IOTA + 16] = np.arange(16)
    for n, f in enumerate((7.0, 15.0, 13.0)):
        c[:, C_EYE7 + 64 * n:C_EYE7 + 64 * n + 64] = f * (p % 64 == np.arange(64)[None, :])
    c[:, C_TRASH:C_TRASH + 2 * tiles] = np.arange(2 * tiles)[None, :] * P + p
    return c


def at_least(eng, sem, count):
    if isinstance(count, int) and count <= 0:
        return
    eng.wait_ge(sem, count)


def pipeline(eng, tiles, depth, turn_tiles, step, loop=True):
    def peeled(its):
        for it in its:
            step(it, it % turn_tiles, it // turn_tiles, lambda lag, it=it: 0 <= it - lag < tiles)

    if not loop:
        peeled(range(tiles + depth))
        return
    peeled(range(turn_tiles))
    with eng.Fori(1, tiles // turn_tiles) as turn:
        for u in range(turn_tiles):
            step(turn_tiles * turn + u, u, turn, lambda lag: True)
    peeled(range(tiles, tiles + depth))


class Buffers:

    def __init__(self, nc, stack):
        self.nc, self.stack = nc, stack

    def sb(self, name, shape, dt=F32):
        return self.stack.enter_context(self.nc.sbuf_tensor(name, shape, dt))

    def ps(self, name, shape=(P, 512), dt=F32):
        return self.stack.enter_context(self.nc.psum_tensor(name, list(shape), dt))

    def sem(self, name):
        return self.stack.enter_context(self.nc.semaphore(name))


class Shared:

    def __init__(self, buffers):
        self.buffers, self.made = buffers, {}

    def sem(self, name):
        if name not in self.made:
            self.made[name] = self.buffers.sem(name)
        return self.made[name]


def linear_attention(nc, core, x_in, wqkT, wvT, woT, bqk, bv, bo, rwT, rb):
    x, xn_all, cst, NT = core.x, core.xn, core.cst, core.NT
    NH, DH = 16, 16
    KD = 2
    LX, LA, LB, LC, LD, LE = 0, 1, 2, 3, 4, 5
    GT, NG = core.GT, NT // core.GT
    DONE = (GT - 1 + LE) % GT
    with ExitStack() as stack:
        B = Buffers(nc, stack)
        wqk = B.sb("a_wqk", [P, KD, 512])
        wv = B.sb("a_wv", [P, KD, 256])
        wo = B.sb("a_wo", [P, KD, 256])
        routing = Routing(core, B, "a_", 0)
        rw = B.sb("a_rw", [P, KD, 16])
        bias_qk = B.sb("a_bias_qk", [P, 4])
        bias_v = B.sb("a_bias_v", [P, 256])
        bias_o = B.sb("a_bias_o", [P, 256])
        bias_r = B.sb("a_bias_r", [P, 16])
        tick = B.sb("a_tick", [P, 2])
        stats = B.sb("a_stats", [P, 2, 6])
        mv = B.sb("a_mv", [P, 2, 2])
        rstd = B.sb("a_rstd", [P, 2])
        xln = B.sb("a_xln", [P, 2, 256])
        xlnT = B.sb("a_xlnT", [P, 2, KD, P])
        er = B.sb("a_er", [P, 2, 2, 4, P])
        phi = B.sb("a_phi", [P, 2, 4, P])
        phi_high = B.sb("a_phi_high", [P, 2, 4, P], F32R)
        phi_low = B.sb("a_phi_low", [P, 2, 4, P], F32R)
        qbd_high = B.sb("a_qbd_high", [P, 2, 2, 8, P], F32R)
        qbd_low = B.sb("a_qbd_low", [P, 2, 2, 8, P], F32R)
        vaug = B.sb("a_vaug", [P, 2, NH, DH + 1])
        ktok = B.sb("a_ktok", [P, 256])
        sc = B.sb("a_sc", [P, NH, P])
        state = B.sb("a_state", [P, 2, 136])
        stmp = B.sb("a_stmp", [P, 272])
        den = B.sb("a_den", [P, NH])
        rec = B.sb("a_rec", [P, NH])
        o = B.sb("a_o", [P, 2, 256])
        oT = B.sb("a_oT", [P, KD, P])
        stats2 = B.sb("a_stats2", [P, 2, 6])
        mv2 = B.sb("a_mv2", [P, 2, 2])
        rstd2 = B.sb("a_rstd2", [P, 2])
        xr = B.sb("a_xr", [P, 2, 256])
        xrT = B.sb("a_xrT", [P, KD, P])

        b_t, b_qk, b_v, b_s0, b_s1, b_o, b_st, b_c = [core.bank[i] for i in range(8)]
        b_s = [b_s0, b_s1]

        loaded = B.sem("a_loaded")
        x_here = B.sem("a_x_here")
        zero_made = B.sem("a_zero_made")
        zero = B.sb("a_zero", [P, 2560])
        made = B.sem("a_made")
        ln_chain = B.sem("a_ln_chain")
        ln_rstd = B.sem("a_ln_rstd")
        xln_ready = B.sem("a_xln_ready")
        xlnT_psum = B.sem("a_xlnT_psum")
        xlnT_ready = B.sem("a_xlnT_ready")
        qk_psum = B.sem("a_qk_psum")
        v_psum = B.sem("a_v_psum")
        er_ready = B.sem("a_er_ready")
        phi_ready = B.sem("a_phi_ready")
        v_ready = B.sem("a_v_ready")
        high_ready = B.sem("a_high_ready")
        low_ready = B.sem("a_low_ready")
        qbd_ready = B.sem("a_qbd_ready")
        qbd_low_ready = B.sem("a_qbd_low_ready")
        k_psum = B.sem("a_k_psum")
        ktok_ready = B.sem("a_ktok_ready")
        s_psum = B.sem("a_s_psum")
        s_ready = B.sem("a_s_ready")
        o_psum = B.sem("a_o_psum")
        o_chain = B.sem("a_o_chain")
        o_ready = B.sem("a_o_ready")
        st_psum = B.sem("a_st_psum")
        st_chain = B.sem("a_st_chain")
        st_ready = B.sem("a_st_ready")
        oT_psum = B.sem("a_oT_psum")
        oT_ready = B.sem("a_oT_ready")
        y_psum = B.sem("a_y_psum")
        x_chain = B.sem("a_x_chain")
        r_rstd = B.sem("a_r_rstd")
        xr_ready = B.sem("a_xr_ready")
        xr_kept = B.sem("a_xr_kept")
        xrT_psum = B.sem("a_xrT_psum")
        xrT_ready = B.sem("a_xrT_ready")
        logits_psum = B.sem("a_logits_psum")
        logits_read = B.sem("a_logits_read")

        ident = cst[:, C_IDENT:C_IDENT + P]

        N_LOADS = 9

        with nc.Block() as block:

            @block.sync
            def _(sp):
                def tokens(b):
                    sp.dma_start(x[:, 8 * b:8 * b + 8, :],
                                 x_in[1024 * b:1024 * b + 1024, :].rearrange("(t p) d -> p t d", p=P)).then_inc(x_here, 16)

                tokens(0)
                sp.dma_start(cst[:, :], core.cst_dram).then_inc(loaded, 16)
                for dst, src in ((wqk, wqkT), (wv, wvT), (wo, woT), (rw, rwT)):
                    sp.dma_start(dst[:, :, :], src.rearrange("(k p) n -> p k n", p=P)).then_inc(loaded, 16)
                sp.dma_start(bias_qk[:, :], bqk.rearrange("(g p) -> p g", p=P), allow_slow_non_contiguous=True).then_inc(loaded, 16)
                for dst, src, width in ((bias_v, bv, 256), (bias_o, bo, 256), (bias_r, rb, 16)):
                    sp.dma_start(dst[:, :], src[None, :].to_broadcast([P, width])).then_inc(loaded, 16)
                sp.wait_ge(x_here, 16)
                for b in range(1, 4):
                    tokens(b)
                load_w1(sp, core, *core.first_layer, 0, 0)
                load_w2(sp, core, core.second_layer, 0)
                sp.wait_ge(zero_made, 1)
                slots = core.NE * core.CAP
                sp.dma_start(core.slots_dram[0:slots, :].rearrange("(p a b) d -> p a (b d)", p=P, b=10),
                             zero[:, :].unsqueeze(1).to_broadcast([P, slots // P // 10, 2560])).then_inc(core.zeroed, 16)

            @block.gpsimd
            def _(pool):
                pool.memset(zero[:, :], 0.0).then_inc(zero_made, 1)
                pool.memset(core.minus_half[:, :], -0.5).then_inc(made, 1)
                pool.memset(state[:, :, :], 0.0).then_inc(made, 1)
                pool.memset(vaug[:, :, :, :], 1.0).then_inc(made, 1)
                pool.wait_ge(made, 3)
                pool.wait_ge(loaded, 16 * N_LOADS)

                FROM = GT + DONE + 3

                def step(it, u, turn, live):
                    par = u % 2
                    if live(LX):
                        i = it
                        at_least(pool, ln_chain, 3 * i + 3)
                        pool.tensor_tensor(rstd[:, par:par + 1], mv[:, par, 1:2], core.minus_half[:, :], ALU.pow).then_inc(ln_rstd, 1)
                    k = it - FROM
                    if k >= 0:
                        if k == 0:
                            pool.wait_ge(core.zeroed, 16)
                        pool.wait_ge(xr_kept, k + 1)
                        routing.scatter(pool, k)
                    if live(LA):
                        i = it - LA
                        q = (par + LA) % 2
                        at_least(pool, high_ready, i + 1)
                        at_least(pool, s_psum, 4 * (i - 1))
                        for half in range(2):
                            ins = pool.tensor_tensor(
                                qbd_high[:, q, half, :, :],
                                phi_high[:, q, half:half + 1, :].bitcast(F32).to_broadcast([P, 8, P]),
                                cst[:, C_HEAD8:C_HEAD8 + 8].unsqueeze(2).to_broadcast([P, 8, P]), ALU.mult)
                        ins.then_inc(qbd_ready, 1)
                    if live(LC):
                        i = it - LC
                        q = (par + LC) % 2
                        at_least(pool, x_chain, 5 * i + 5)
                        pool.tensor_tensor(rstd2[:, q:q + 1], mv2[:, q, 1:2], core.minus_half[:, :], ALU.pow).then_inc(r_rstd, 1)
                    if live(LC):
                        i = it - LC
                        q = (par + LC) % 2
                        at_least(pool, xr_ready, i + 1)
                        pool.tensor_copy(xn_all[:, i, :], xr[:, q, :]).then_inc(xr_kept, 1)

                pipeline(pool, NT, LE, GT, step, loop=False)
                for i in range(NT + LE - FROM, NT):
                    pool.wait_ge(xr_kept, i + 1)
                    routing.scatter(pool, i)
                for g in (NG - 2, NG - 1):
                    routing.wait_scattered(pool, g)

            @block.scalar
            def _(act):
                act.wait_ge(loaded, 16 * N_LOADS)

                def step(it, u, turn, live):
                    par = u % 2
                    if live(LA):
                        i, q = it - LA, (par + LA) % 2
                        at_least(act, xlnT_psum, i + 1)
                        at_least(act, v_psum, i - 1)
                        act.activation(xlnT[:, q, :, :], b_t[:, 0:256].rearrange("p (k t) -> p k t", k=KD), ACT.Copy).then_inc(xlnT_ready, 1)
                    if live(LC):
                        i = it - LC
                        at_least(act, oT_psum, i + 1)
                        at_least(act, y_psum, i)
                        act.activation(oT[:, :, :], b_c[:, 0:256].rearrange("p (k t) -> p k t", k=KD), ACT.Copy).then_inc(oT_ready, 1)
                    if live(LA):
                        i, q = it - LA, (par + LA) % 2
                        at_least(act, qk_psum, i + 1)
                        at_least(act, phi_ready, i - 1)
                        for g in range(4):
                            act.activation(er[:, q, 0, g, :], b_qk[:, P * g:P * g + P], ACT.Exp, bias=bias_qk[:, g:g + 1])
                        for g in range(4):
                            ins = act.activation(er[:, q, 1, g, :], b_qk[:, P * g:P * g + P], ACT.Relu, bias=bias_qk[:, g:g + 1])
                        ins.then_inc(er_ready, 1)
                        at_least(act, phi_ready, i + 1)
                        at_least(act, s_psum, 4 * (i - 1))
                        act.activation(phi_high[:, q, :, :], phi[:, q, :, :], ACT.Copy).then_inc(high_ready, 1)
                    if live(LD):
                        i = it - LD
                        at_least(act, xrT_psum, i + 1)
                        at_least(act, logits_psum, i)
                        act.activation(xrT[:, :, :], b_t[:, 256:512].rearrange("p (k t) -> p k t", k=KD), ACT.Copy).then_inc(xrT_ready, 1)
                    if live(LB):
                        i = it - LB
                        at_least(act, k_psum, i + 1)
                        at_least(act, st_psum, i)
                        act.activation(ktok[:, :], b_v[:, 256:512], ACT.Copy).then_inc(ktok_ready, 1)
                    if u == DONE + 2 and live(LE + GT + 1):
                        routing.exponentials(act, turn - 1)

                pipeline(act, NT, LE, GT, step)
                routing.exponentials(act, NG - 1)

            @block.tensor
            def _(pe):
                pe.wait_ge(loaded, 16 * N_LOADS)
                pe.wait_ge(made, 3)

                def scores(it, par, live, g):
                    if live(LB):
                        i, q, half = it - LB, (par + LB) % 2, g // 2
                        if g == 0:
                            at_least(pe, qbd_ready, i + 1)
                        if g % 2 == 0:
                            at_least(pe, qbd_low_ready, 2 * i + g // 2 + 1)
                        at_least(pe, s_ready, 4 * i + g - 1)
                        heads_4 = slice(4 * (g % 2), 4 * (g % 2) + 4)
                        out, high, low = b_s[g % 2][:, :], phi_high[:, q, 2 + half, :], phi_low[:, q, 2 + half, :]
                        pe.matmul(out, high, qbd_high[:, q, half, heads_4, :], start=True, stop=False)
                        pe.matmul(out, high, qbd_low[:, q, half, heads_4, :], start=False, stop=False)
                        pe.matmul(out, low, qbd_high[:, q, half, heads_4, :], start=False, stop=True).then_inc(s_psum, 1)

                def heads(it, par, live, g):
                    if live(LB):
                        i, q = it - LB, (par + LB) % 2
                        if g == 0:
                            at_least(pe, st_ready, i)
                            at_least(pe, o_ready, i)
                            for half in range(2):
                                pe.matmul(b_o[:, 136 * half:136 * half + 136], phi[:, q, half, :], state[:, half, :],
                                          start=(half == 0), stop=False, skip_group_check=True)
                        at_least(pe, s_ready, 4 * i + g + 1)
                        for h in range(4 * g, 4 * g + 4):
                            ins = pe.matmul(b_o[:, 17 * h:17 * h + 17], sc[:, h, :], vaug[:, q, h, :],
                                            start=False, stop=(h == NH - 1), skip_group_check=True)
                        if g == 3:
                            ins.then_inc(o_psum, 1)

                def step(it, u, turn, live):
                    par = u % 2
                    if live(LA):
                        i, q = it - LA, (par + LA) % 2
                        at_least(pe, xln_ready, i + 1)
                        at_least(pe, xlnT_ready, i)
                        at_least(pe, xrT_ready, it - LD)
                        for k in range(KD):
                            ins = pe.transpose(b_t[:, P * k:P * k + P], xln[:, q, P * k:P * k + P], ident)
                        ins.then_inc(xlnT_psum, 1)
                    scores(it, par, live, 0)
                    if live(LC):
                        i, q = it - LC, (par + LC) % 2
                        at_least(pe, o_ready, i + 1)
                        at_least(pe, x_chain, 5 * (i - 1) + 1)
                        for k in range(KD):
                            ins = pe.transpose(b_c[:, P * k:P * k + P], o[:, q, P * k:P * k + P], ident)
                        ins.then_inc(oT_psum, 1)
                    if live(LA):
                        i, q = it - LA, (par + LA) % 2
                        at_least(pe, xlnT_ready, i + 1)
                        at_least(pe, er_ready, i)
                        for g in range(4):
                            for k in range(KD):
                                ins = pe.matmul(b_qk[:, P * g:P * g + P], wqk[:, k, P * g:P * g + P], xlnT[:, q, k, :],
                                                start=(k == 0), stop=(k == KD - 1))
                        ins.then_inc(qk_psum, 1)
                    scores(it, par, live, 1)
                    if live(LE):
                        i = it - LE
                        at_least(pe, xrT_ready, i + 1)
                        at_least(pe, st_ready, min(it, NT + LB) - LB if isinstance(it, int) else it - LB)
                        at_least(pe, logits_read, i)
                        if u == DONE + 2 and live(LE + GT + 1):
                            routing.count(pe, turn - 1, b_st[:, 288:512])
                        for k in range(KD):
                            ins = pe.matmul(b_st[:, 272:288], xrT[:, k, :], rw[:, k, :], start=(k == 0), stop=(k == KD - 1))
                        ins.then_inc(logits_psum, 1)
                    heads(it, par, live, 0)
                    if live(LA):
                        i, q = it - LA, (par + LA) % 2
                        at_least(pe, v_ready, i)
                        at_least(pe, ktok_ready, i - 1)
                        for k in range(KD):
                            ins = pe.matmul(b_v[:, 0:256], xlnT[:, q, k, :], wv[:, k, :], start=(k == 0), stop=(k == KD - 1))
                        ins.then_inc(v_psum, 1)
                    scores(it, par, live, 2)
                    heads(it, par, live, 1)
                    if live(LC):
                        i = it - LC
                        at_least(pe, oT_ready, i + 1)
                        for k in range(KD):
                            ins = pe.matmul(b_c[:, 256:512], oT[:, k, :], wo[:, k, :], start=(k == 0), stop=(k == KD - 1))
                        ins.then_inc(y_psum, 1)
                    scores(it, par, live, 3)
                    heads(it, par, live, 2)
                    if live(LD):
                        i, q = it - LD, (par + LD) % 2
                        at_least(pe, xr_ready, i + 1)
                        if live(LA):
                            at_least(pe, xlnT_ready, it - LA + 1)
                        for k in range(KD):
                            ins = pe.transpose(b_t[:, 256 + P * k:256 + P * k + P], xr[:, q, P * k:P * k + P], ident)
                        ins.then_inc(xrT_psum, 1)
                    if live(LB):
                        i, q = it - LB, (par + LB) % 2
                        at_least(pe, v_ready, it - LA + 1 if live(LA) else i + 1)
                        for k in range(KD):
                            ins = pe.transpose(b_v[:, 256 + P * k:256 + P * k + P], phi[:, q, 2 + k, :], ident)
                        ins.then_inc(k_psum, 1)
                    heads(it, par, live, 3)
                    if live(LB):
                        i, q = it - LB, (par + LB) % 2
                        at_least(pe, ktok_ready, i + 1)
                        at_least(pe, logits_read, it - LE + 1)
                        if u == DONE + 2 and live(LE + GT + 1):
                            routing.wait_counts_taken(pe, turn - 1)
                        for half in range(2):
                            ins = pe.matmul(b_st[:, 136 * half:136 * half + 136], ktok[:, P * half:P * half + P],
                                            vaug[:, q, 8 * half:8 * half + 8, :], start=True, stop=True)
                        ins.then_inc(st_psum, 1)

                pipeline(pe, NT, LE, GT, step)
                pe.wait_ge(logits_read, NT)
                routing.count(pe, NG - 1, b_st[:, 288:512])

            @block.vector
            def _(dve):
                dve.wait_ge(loaded, 16 * N_LOADS)
                dve.wait_ge(made, 3)
                routing.prepare(dve)

                def variance(src, st, m, chain, done):
                    dve.memset(tick[:, 0:1], 0.0)
                    dve.bn_stats(st, src).then_inc(chain, 1)
                    at_least(dve, chain, done + 1)
                    dve.memset(tick[:, 1:2], 0.0)
                    dve.bn_aggr(m, st).then_inc(chain, 1)
                    at_least(dve, chain, done + 2)
                    dve.tensor_scalar(m[:, 1:2], m[:, 1:2], LN_EPS, None, ALU.add).then_inc(chain, 1)

                def low_blocks(q, half):
                    dve.tensor_tensor(
                        qbd_low[:, q, half, :, :],
                        phi_low[:, q, half:half + 1, :].bitcast(F32).to_broadcast([P, 8, P]),
                        cst[:, C_HEAD8:C_HEAD8 + 8].unsqueeze(2).to_broadcast([P, 8, P]), ALU.mult).then_inc(qbd_low_ready, 1)

                def mask(it, live, g):
                    if live(LB):
                        i = it - LB
                        at_least(dve, s_psum, 4 * i + g + 1)
                        at_least(dve, o_psum, i)
                        dve.tensor_tensor(sc[:, 4 * g:4 * g + 4, :],
                                          b_s[g % 2][:, :].rearrange("p (h t) -> p h t", h=4),
                                          cst[:, C_CAUSAL:C_CAUSAL + P].unsqueeze(1).to_broadcast([P, 4, P]),
                                          ALU.mult).then_inc(s_ready, 1)

                counts = b_st[:, 288:512]

                def route(k, u, turn, live):
                    if u == DONE and k >= 4 and live(LE + GT - 1):
                        routing.vector(dve, turn - 1, routing.CHOOSE[k - 4])
                    if u == DONE + 1 and k < 4 and live(LE + GT):
                        routing.vector(dve, turn - 1, routing.CHOOSE[8 + k])
                    if u == DONE + 2 and k >= 4 and live(LE + GT + 1):
                        routing.vector(dve, turn - 1, routing.PLACE[k - 4])
                    if u == DONE + 3 and k < 10 and live(LE + GT + 2):
                        routing.vector(dve, turn - 1, routing.PLACE[8 + k])

                def step(it, u, turn, live):
                    par = u % 2
                    if live(LX):
                        if isinstance(it, int) and it in (0, 5):
                            dve.wait_ge(x_here, 16 if it == 0 else 64)
                        variance(x[:, it, :], stats[:, par, :], mv[:, par, :], ln_chain, 3 * it)
                    route(0, u, turn, live)
                    mask(it, live, 0)
                    route(1, u, turn, live)
                    if live(LX):
                        at_least(dve, ln_rstd, it + 1)
                        at_least(dve, xlnT_psum, it - 1)
                        dve.tensor_scalar(xln[:, par, :], x[:, it, :], mv[:, par, 0:1], rstd[:, par:par + 1],
                                          ALU.subtract, ALU.mult).then_inc(xln_ready, 1)
                    route(2, u, turn, live)
                    mask(it, live, 1)
                    if live(LB):
                        low_blocks((par + LB) % 2, 1)
                    route(3, u, turn, live)
                    if live(LE):
                        i = it - LE
                        at_least(dve, logits_psum, i + 1)
                        dve.tensor_tensor(routing.logits[:, (u - LE) % GT, :], b_st[:, 272:288], bias_r[:, :], ALU.add).then_inc(logits_read, 1)
                    if u == DONE + 2 and live(LE + GT + 1):
                        for n in routing.TAKE_COUNTS:
                            routing.vector(dve, turn - 1, n, counts)
                    if u == DONE and live(LE + GT - 1):
                        dve.wait_ge(logits_read, GT * turn)
                    if live(LA):
                        i, q = it - LA, (par + LA) % 2
                        at_least(dve, er_ready, i + 1)
                        at_least(dve, o_psum, i - 1)
                        at_least(dve, high_ready, i - 1)
                        dve.scalar_tensor_tensor(phi[:, q, :, :], er[:, q, 0, :, :], 1.0, er[:, q, 1, :, :],
                                                 ALU.min, ALU.add).then_inc(phi_ready, 1)
                    route(4, u, turn, live)
                    if live(LA):
                        i, q = it - LA, (par + LA) % 2
                        at_least(dve, v_psum, i + 1)
                        at_least(dve, st_psum, i - 1)
                        dve.tensor_tensor(vaug[:, q, :, 0:DH], b_v[:, 0:256].rearrange("p (h e) -> p h e", h=NH),
                                          bias_v[:, :].rearrange("p (h e) -> p h e", h=NH), ALU.add).then_inc(v_ready, 1)
                    route(5, u, turn, live)
                    mask(it, live, 2)
                    if live(LA):
                        i, q = it - LA, (par + LA) % 2
                        at_least(dve, high_ready, i + 1)
                        at_least(dve, s_psum, 4 * (i - 1))
                        dve.tensor_tensor(phi_low[:, q, :, :], phi[:, q, :, :], phi_high[:, q, :, :].bitcast(F32), ALU.subtract).then_inc(low_ready, 1)
                    route(6, u, turn, live)
                    if live(LA):
                        at_least(dve, low_ready, it - LA + 1)
                        low_blocks((par + LA) % 2, 0)
                    mask(it, live, 3)
                    route(7, u, turn, live)
                    if live(LC):
                        i, q = it - LC, (par + LC) % 2
                        at_least(dve, y_psum, i + 1)
                        dve.tensor_tensor(x[:, i, :], x[:, i, :], b_c[:, 256:512], ALU.add).then_inc(x_chain, 1)
                        at_least(dve, x_chain, 5 * i + 1)
                        dve.tensor_tensor(x[:, i, :], x[:, i, :], bias_o[:, :], ALU.add).then_inc(x_chain, 1)
                        at_least(dve, x_chain, 5 * i + 2)
                        variance(x[:, i, :], stats2[:, q, :], mv2[:, q, :], x_chain, 5 * i + 2)
                    route(8, u, turn, live)
                    if live(LB):
                        i, q = it - LB, (par + LB) % 2
                        at_least(dve, o_psum, i + 1)
                        ops = b_o[:, 0:272].rearrange("p (h e) -> p h e", h=NH)
                        dve.tensor_scalar(den[:, :], ops[:, :, DH], DEN_EPS, None, ALU.max).then_inc(o_chain, 1)
                        at_least(dve, o_chain, 2 * i + 1)
                        dve.reciprocal(rec[:, :], den[:, :]).then_inc(o_chain, 1)
                        at_least(dve, o_chain, 2 * i + 2)
                        at_least(dve, oT_psum, i - 1)
                        dve.tensor_tensor(o[:, q, :].rearrange("p (h e) -> p h e", h=NH), ops[:, :, 0:DH],
                                          rec[:, :].unsqueeze(2).to_broadcast([P, NH, DH]), ALU.mult).then_inc(o_ready, 1)
                    route(9, u, turn, live)
                    if live(LB):
                        i, q = it - LB, (par + LB) % 2
                        keep = cst[:, bass.ds(i + C_KEEP, 1)]
                        at_least(dve, st_psum, i + 1)
                        dve.scalar_tensor_tensor(stmp[:, :], b_st[:, 0:272], keep, cst[:, C_BLOCK:C_BLOCK + 272],
                                                 ALU.mult, ALU.mult).then_inc(st_chain, 1)
                        at_least(dve, st_chain, i + 1)
                        dve.scalar_tensor_tensor(state[:, :, :].rearrange("p a b -> p (a b)"),
                                                 state[:, :, :].rearrange("p a b -> p (a b)"), keep, stmp[:, :],
                                                 ALU.mult, ALU.add).then_inc(st_ready, 1)
                    route(10, u, turn, live)
                    if live(LC):
                        i, q = it - LC, (par + LC) % 2
                        at_least(dve, r_rstd, i + 1)
                        at_least(dve, xrT_psum, i - 1)
                        at_least(dve, xr_kept, i - 1)
                        dve.tensor_scalar(xr[:, q, :], x[:, i, :], mv2[:, q, 0:1], rstd2[:, q:q + 1],
                                          ALU.subtract, ALU.mult).then_inc(xr_ready, 1)
                    route(11, u, turn, live)

                pipeline(dve, NT, LE, GT, step)
                for n in [*routing.CHOOSE[8:], *routing.TAKE_COUNTS, *routing.PLACE]:
                    routing.vector(dve, NG - 1, n, counts)


class Routing:

    CHOOSE = range(1, 13)
    TAKE_COUNTS = range(13, 15)
    PLACE = range(15, 33)
    STEPS = 32

    def __init__(self, core, buffers, name, call):
        B, NT, NE, GT = buffers, core.NT, core.NE, core.GT
        self.core, self.first = core, NT // GT * call
        self.logits = B.sb(name + "r_logits", [P, GT, NE])
        self.key = B.sb(name + "r_key", [P, GT, NE])
        self.eq = B.sb(name + "r_eq", [P, GT, NE])
        self.rest = B.sb(name + "r_rest", [P, GT, NE])
        self.hot = B.sb(name + "r_hot", [P, 2, GT, NE])
        self.hot_pad = B.sb(name + "r_hot_pad", [P, (2 * GT + 1) * NE], BF16)
        self.strict = B.sb(name + "r_strict", [P, P], BF16)
        self.ones = B.sb(name + "r_ones", [P, P], BF16)
        self.base = B.sb(name + "r_base", [P, NE])
        self.top = B.sb(name + "r_top", [P, 2, GT])
        self.which = B.sb(name + "r_which", [P, 2, GT])
        self.pos = B.sb(name + "r_pos", [P, 2, GT])
        self.kept = B.sb(name + "r_kept", [P, 2, GT])
        self.where = B.sb(name + "r_where", [P, 2, GT])
        self.gate = B.sb(name + "r_gate", [P, 2, GT])
        self.gap = B.sb(name + "r_gap", [P, 2, GT])
        self.total = B.sb(name + "r_total", [P, GT])
        self.scatter_at = B.sb(name + "r_scatter_at", [P, 2, NT], I32)
        sem = core.shared.sem
        self.chain = sem("r_chain")
        self.chosen = sem("r_chosen")
        self.exp_ready = sem("r_exp_ready")
        self.counts_psum = sem("r_counts_psum")
        self.slots_ready = sem("r_slots_ready")
        self.scattered = [sem(f"r_scattered{odd}") for odd in range(2)]

    def prepare(self, dve):
        dve.tensor_copy(self.strict[:, :], self.core.cst[:, C_STRICT:C_STRICT + P])
        dve.memset(self.ones[:, :], 1.0)
        dve.memset(self.hot_pad[:, :], 0.0)
        dve.memset(self.base[:, :], 0.0)

    def vector(self, dve, g, n, at=None):
        core = self.core
        NE, GT, NT, CAP = core.NE, core.GT, core.NT, core.CAP
        SLOTS = NE * CAP
        wide = [P, GT, NE]
        tiles = bass.ds(g * GT, GT)
        iota = core.cst[:, C_IOTA:C_IOTA + NE].unsqueeze(1).to_broadcast(wide)
        trash = core.cst[:, C_TRASH:C_TRASH + 2 * NT].rearrange("p (r t) -> p r t", r=2)[:, :, tiles]
        key, eq, rest, hot, which, top = self.key, self.eq, self.rest, self.hot, self.which, self.top
        pos, kept, gate, gap, total, where = self.pos, self.kept, self.gate, self.gap, self.total, self.where
        if n > 1:
            dve.wait_ge(self.chain, self.STEPS * (g + self.first) + n - 1)
        if n <= 11:
            r, part = (0, n) if n <= 6 else (1, n - 6)
            scores = (self.logits if r == 0 else rest)[:, :, :]
            if part == 1:
                ins = dve.tensor_reduce(top[:, r, :], scores, AX_X, ALU.max)
            elif part == 2:
                ins = dve.tensor_tensor(eq[:, :, :], scores, top[:, r, :].unsqueeze(2).to_broadcast(wide), ALU.is_equal)
            elif part == 3:
                ins = dve.scalar_tensor_tensor(key[:, :, :], eq[:, :, :], -float(NE), iota, ALU.mult, ALU.add)
            elif part == 4:
                ins = dve.tensor_reduce(which[:, r, :], key[:, :, :], AX_X, ALU.min)
            elif part == 5:
                ins = dve.tensor_tensor(hot[:, r, :, :], key[:, :, :], which[:, r, :].unsqueeze(2).to_broadcast(wide), ALU.is_equal)
            else:
                ins = dve.scalar_tensor_tensor(rest[:, :, :], hot[:, 0, :, :], -3.0e38, scores, ALU.mult, ALU.add)
        elif n == 12:
            ins = dve.tensor_tensor(self.hot_pad[:, NE * GT:2 * NE * GT].rearrange("p (t e) -> p t e", e=NE), hot[:, 0, :, :], hot[:, 1, :, :], ALU.add)
        elif n == 13:
            dve.wait_ge(self.counts_psum, g + self.first + 1)
            ins = dve.tensor_tensor(key[:, :, :], at[:, 0:NE * GT].rearrange("p (t e) -> p t e", e=NE),
                                    self.base[:, :].unsqueeze(1).to_broadcast(wide), ALU.add)
        elif n == 14:
            ins = dve.tensor_tensor(self.base[:, :], self.base[:, :], at[:, NE * GT:NE * (GT + 1)], ALU.add)
        elif n in (15, 17):
            ins = dve.tensor_tensor(eq[:, :, :], hot[:, (n - 15) // 2, :, :], key[:, :, :], ALU.mult)
        elif n in (16, 18):
            ins = dve.tensor_reduce(pos[:, (n - 16) // 2, :], eq[:, :, :], AX_X, ALU.add)
        elif n == 19:
            ins = dve.tensor_scalar(kept[:, :, :], pos[:, :, :], float(CAP), None, ALU.is_lt)
        elif n == 20:
            ins = dve.scalar_tensor_tensor(pos[:, :, :], which[:, :, :], float(CAP), pos[:, :, :], ALU.mult, ALU.add)
        elif n == 21:
            ins = dve.tensor_tensor(where[:, :, :], pos[:, :, :], trash, ALU.subtract)
        elif n == 22:
            ins = dve.tensor_tensor(where[:, :, :], where[:, :, :], kept[:, :, :], ALU.mult)
        elif n == 23:
            ins = dve.tensor_tensor(where[:, :, :], where[:, :, :], trash, ALU.add)
        elif n == 24:
            dve.tensor_scalar(self.scatter_at[:, :, tiles], where[:, :, :], float(SLOTS), None, ALU.add).then_inc(self.slots_ready, 1)
            ins = dve.scalar_tensor_tensor(core.gather_at[:, :, tiles], pos[:, :, :], float(SLOTS), kept[:, :, :], ALU.add, ALU.mult)
        elif n == 25:
            dve.wait_ge(self.exp_ready, g + self.first + 1)
            ins = dve.tensor_scalar(total[:, :], gap[:, 1, :], 1.0, None, ALU.add)
        elif n == 26:
            ins = dve.reciprocal(gate[:, 0, :], total[:, :])
        elif n == 27:
            ins = dve.tensor_tensor(gate[:, 1, :], gate[:, 0, :], gap[:, 1, :], ALU.mult)
        elif n == 28:
            ins = dve.tensor_tensor(gate[:, :, :], gate[:, :, :], kept[:, :, :], ALU.mult)
        elif n == 29:
            ins = dve.tensor_tensor(total[:, :], gate[:, 0, :], gate[:, 1, :], ALU.add)
        elif n == 30:
            ins = dve.tensor_scalar(total[:, :], total[:, :], 1e-9, None, ALU.add)
        elif n == 31:
            ins = dve.reciprocal(total[:, :], total[:, :])
        else:
            ins = dve.tensor_tensor(core.weight[:, :, tiles], gate[:, :, :], total[:, :].unsqueeze(1).to_broadcast([P, 2, GT]), ALU.mult)
        ins.then_inc(self.chain, 1)
        if n == 12:
            dve.wait_ge(self.chain, self.STEPS * (g + self.first) + n)
            dve.tensor_tensor(gap[:, 0, :], top[:, 1, :], top[:, 0, :], ALU.subtract).then_inc(self.chosen, 1)

    def exponentials(self, act, g):
        act.wait_ge(self.chosen, g + self.first + 1)
        act.activation(self.gap[:, 1, :], self.gap[:, 0, :], ACT.Exp).then_inc(self.exp_ready, 1)

    def count(self, pe, g, at):
        NE, GT = self.core.NE, self.core.GT
        width = NE * (GT + 1)
        pe.wait_ge(self.chosen, g + self.first + 1)
        pe.matmul(at[:, 0:width], self.strict[:, :], self.hot_pad[:, NE * GT:NE * GT + width], start=True, stop=False)
        for back in range(1, GT + 1):
            ins = pe.matmul(at[:, 0:width], self.ones[:, :], self.hot_pad[:, NE * (GT - back):NE * (GT - back) + width],
                            start=False, stop=(back == GT))
        ins.then_inc(self.counts_psum, 1)

    def wait_counts_taken(self, pe, g):
        pe.wait_ge(self.chain, self.STEPS * (g + self.first) + 14)

    def scatter(self, pool, i):
        core = self.core
        pool.wait_ge(self.slots_ready, i // core.GT + self.first + 1)
        for r in range(2):
            pool.indirect_dma_start(
                out=core.slots_dram[:, :], out_offset=bass.IndirectOffsetOnAxis(ap=self.scatter_at[:, r, i:i + 1], axis=0),
                in_=core.xn[:, i % core.xn.shape[1], :], in_offset=None).then_inc(self.scattered[i // core.GT % 2], 16)

    def wait_scattered(self, pool, g):
        pool.wait_ge(self.scattered[g % 2], 16 * 2 * self.core.GT * (self.first // 2 + g // 2 + 1))


def load_w1(sp, core, w1, b1, e, u):
    loaded = core.shared.sem("e_w1_loaded")
    sp.dma_start(core.w1b[:, :, :], w1[bass.ds(e, 1), :, :].rearrange("o (k p) f -> p (o k) f", p=P)).then_inc(loaded, 16)
    sp.dma_start(core.b1b[:, u, :], b1[bass.ds(e, 1), :, :].rearrange("o p c -> (o p) c")).then_inc(loaded, 16)


def load_w2(sp, core, w2, e):
    loaded = core.shared.sem("e_w2_loaded")
    sp.dma_start(core.w2b[:, :, :], w2[bass.ds(e, 1), :, :].rearrange("o (c p) d -> p (o c) d", p=P)).then_inc(loaded, 16)


def experts(nc, core, w1, b1, w2, b2, name, call):
    NE, CAP = core.NE, core.CAP
    D, F = w1.shape[1], w1.shape[2]
    KD, KF, TS = D // P, F // P, CAP // P
    HALF = CAP // 2
    LT, LM = 0, 1
    BEFORE = NE * call
    with ExitStack() as stack:
        B = Buffers(nc, stack)
        w1b, w2b, b1b = core.w1b, core.w2b, core.b1b
        w1_high = B.sb(name + "e_w1_high", [P, KD, F], F32R)
        w1_low = B.sb(name + "e_w1_low", [P, KD, F], F32R)
        w2_high = B.sb(name + "e_w2_high", [P, KF, D], F32R)
        w2_low = B.sb(name + "e_w2_low", [P, KF, D], F32R)
        b2b = B.sb(name + "e_b2", [P, 2, D])
        tok = B.sb(name + "e_tok", [P, 2, TS, D])
        tokT_high = B.sb(name + "e_tokT_high", [P, 2, KD, CAP], F32R)
        tokT_low = B.sb(name + "e_tokT_low", [P, 2, KD, CAP], F32R)
        RING = 4
        h = B.sb(name + "e_h", [P, RING, CAP])
        hT_high = B.sb(name + "e_hT_high", [P, KF, CAP], F32R)
        hT_low = B.sb(name + "e_hT_low", [P, KF, CAP], F32R)
        y = B.sb(name + "e_y", [P, 2, TS, D])
        psum, bank = core.psum, core.bank

        w1_loaded = core.shared.sem("e_w1_loaded")
        w2_loaded = core.shared.sem("e_w2_loaded")
        b2_loaded = [core.shared.sem(f"e_b2_loaded{u}") for u in range(2)]
        tok_loaded = [core.shared.sem(f"e_tok_loaded{u}") for u in range(2)]
        w1_halved = core.shared.sem("e_w1_halved")
        w1_split = core.shared.sem("e_w1_split")
        w2_halved = core.shared.sem("e_w2_halved")
        w2_split = core.shared.sem("e_w2_split")
        tokT_psum = core.shared.sem("e_tokT_psum")
        tokT_chain = core.shared.sem("e_tokT_chain")
        tokT_ready = core.shared.sem("e_tokT_ready")
        h_psum = core.shared.sem("e_h_psum")
        h_made = core.shared.sem("e_h_made")
        h_high = core.shared.sem("e_h_high")
        h_split = core.shared.sem("e_h_split")
        y_psum = core.shared.sem("e_y_psum")
        y_ready = core.shared.sem("e_y_ready")
        y_stored = [core.shared.sem(f"e_y_stored{u}") for u in range(2)]
        ident = core.cst[:, C_IDENT:C_IDENT + P]
        T_AFTER = [1, 3, 5]
        T_GROUPS = [(6, [(0, 0, 4)]), (7, [(1, 0, 4)]), (6, [(0, 4, TS - 4), (1, 4, TS - 4)])]

        def turns(eng, depth, step):
            first = 4
            for it in range(first):
                step(it, it % 2, it // 2, lambda lag, it=it: 0 <= it - lag < NE)
            with eng.Fori(first // 2, NE // 2) as turn:
                for u in range(2):
                    step(2 * turn + u, u, turn, lambda lag: True)
            for it in range(NE, NE + depth):
                step(it, it % 2, it // 2, lambda lag, it=it: 0 <= it - lag < NE)

        with nc.Block() as block:

            @block.sync
            def _(sp):
                def step(it, u, turn, live):
                    if live(0):
                        e, g = it, it + BEFORE
                        at_least(sp, tokT_psum, 3 * (g - 1))
                        sp.dma_start(tok[:, u, :, :], core.slots_dram[bass.ds(e * CAP, CAP), :].rearrange("(p t) d -> p t d", t=TS)).then_inc(tok_loaded[u], 16)
                        if not (isinstance(it, int) and it == 0):
                            at_least(sp, w1_split, g)
                            load_w1(sp, core, w1, b1, e, u)
                        at_least(sp, y_ready, TS * (g - 1))
                        sp.dma_start(b2b[:, u, :], b2[bass.ds(e, 1), :].to_broadcast([P, D])).then_inc(b2_loaded[u], 16)
                        if not (isinstance(it, int) and it == 0):
                            at_least(sp, w2_split, g)
                            load_w2(sp, core, w2, e)
                    if live(2):
                        e, g = it - 2, it - 2 + BEFORE
                        at_least(sp, y_ready, TS * (g + 1))
                        sp.dma_start(core.expert_out[bass.ds(e * CAP, CAP), :].rearrange("(p t) d -> p t d", t=TS), y[:, u, :, :]).then_inc(y_stored[u], 16)

                turns(sp, 2, step)
                for u in range(2):
                    sp.wait_ge(y_stored[u], 16 * (NE // 2) * (call + 1))

            @block.gpsimd
            def _(pool):
                def step(it, u, turn, live):
                    e, g = it, it + BEFORE
                    pool.wait_ge(w1_halved, g + 1)
                    pool.tensor_tensor(w1_low[:, :, :], w1b[:, :, :], w1_high[:, :, :].bitcast(F32), ALU.subtract).then_inc(w1_split, 1)
                    pool.wait_ge(w2_halved, g + 1)
                    pool.tensor_tensor(w2_low[:, :, :], w2b[:, :, :], w2_high[:, :, :].bitcast(F32), ALU.subtract).then_inc(w2_split, 1)

                turns(pool, 0, step)

            @block.tensor
            def _(pe):
                def transposes(g, u, turn, n):
                    b, runs = T_GROUPS[n]
                    if n == 0:
                        pe.wait_ge(tok_loaded[u], 16 * ((turn + BEFORE // 2) + 1))
                    at_least(pe, tokT_ready, 3 * g + n - 1 if n != 1 else 3 * g - 1)
                    at = 0
                    for k, t0, m in runs:
                        for t in range(t0, t0 + m):
                            ins = pe.transpose(bank[b][:, at:at + P], tok[:, u, t, P * k:P * k + P], ident)
                            at += P
                    ins.then_inc(tokT_psum, 1)

                def step(it, u, turn, live):
                    if not live(LM):
                        for n in range(3):
                            transposes(it + BEFORE, u, turn, n)
                        return
                    e, g, v = it - LM, it - LM + BEFORE, 1 - u
                    pe.wait_ge(w1_split, g + 1)
                    pe.wait_ge(tokT_ready, 3 * (g + 1))
                    for c in range(KF):
                        at_least(pe, h_made, KF * g + c - 1)
                        f = slice(P * c, P * c + P)
                        for half in range(2):
                            s = slice(HALF * half, HALF * half + HALF)
                            for k in range(KD):
                                out = bank[2 * (c % 2) + half][:, 0:HALF]
                                high, low = w1_high[:, k, f], w1_low[:, k, f]
                                pe.matmul(out, high, tokT_high[:, v, k, s], start=(k == 0), stop=False)
                                pe.matmul(out, high, tokT_low[:, v, k, s], start=False, stop=False)
                                ins = pe.matmul(out, low, tokT_high[:, v, k, s], start=False, stop=(k == KD - 1))
                        ins.then_inc(h_psum, 1)
                        if live(LT) and c in T_AFTER:
                            transposes(it + BEFORE, u, turn, T_AFTER.index(c))
                    pe.wait_ge(w2_split, g + 1)

                    def product(t, chunks):
                        s = slice(P * t, P * t + P)
                        for c in chunks:
                            if t == 0 or c == KF - 1:
                                pe.wait_ge(h_split, KF * g + c + 1)
                            out = bank[4 + t % 2][:, 0:D]
                            high, low = hT_high[:, c, s], hT_low[:, c, s]
                            pe.matmul(out, high, w2_high[:, c, :], start=(c == 0), stop=False)
                            pe.matmul(out, high, w2_low[:, c, :], start=False, stop=False)
                            ins = pe.matmul(out, low, w2_high[:, c, :], start=False, stop=(c == KF - 1))
                        return ins

                    at_least(pe, y_ready, TS * g)
                    for t in range(2):
                        product(t, range(KF - 1))
                    for t in range(2):
                        product(t, [KF - 1]).then_inc(y_psum, 1)
                    for t in range(2, TS):
                        at_least(pe, y_ready, TS * g + t - 1)
                        product(t, range(KF)).then_inc(y_psum, 1)

                turns(pe, 1, step)

            @block.scalar
            def _(act):
                def step(it, u, turn, live):
                    if live(LM):
                        e, g, v = it - LM, it - LM + BEFORE, 1 - u
                        act.wait_ge(w2_loaded, 16 * (g + 1))
                        at_least(act, y_psum, TS * g)
                        act.activation(w2_high[:, :, :], w2b[:, :, :], ACT.Copy).then_inc(w2_halved, 1)
                        for c in range(KF + 1):
                            if c < KF:
                                act.wait_ge(h_psum, KF * g + c + 1)
                                at_least(act, h_split, KF * g + c - RING + 1)
                                act.activation(h[:, c % RING, :].rearrange("p (a b) -> p a b", a=2), psum[:, 2 * (c % 2):2 * (c % 2) + 2, 0:HALF],
                                               ACT.Gelu, bias=b1b[:, v, c:c + 1]).then_inc(h_made, 1)
                            if c >= 1:
                                act.wait_ge(h_made, KF * g + c)
                                act.activation(hT_high[:, c - 1, :], h[:, (c - 1) % RING, :], ACT.Copy).then_inc(h_high, 1)
                    if live(0):
                        e, g = it, it + BEFORE
                        act.wait_ge(w1_loaded, 32 * (g + 1))
                        at_least(act, h_psum, KF * g)
                        act.activation(w1_high[:, :, :], w1b[:, :, :], ACT.Copy).then_inc(w1_halved, 1)

                turns(act, 1, step)

            @block.vector
            def _(dve):
                def transposed(g, u, n):
                    b, runs = T_GROUPS[n]
                    dve.wait_ge(tokT_psum, 3 * g + n + 1)
                    k0, t0, m = runs[0]
                    if len(runs) == 1:
                        at, src = (slice(None), u, k0, slice(P * t0, P * (t0 + m))), bank[b][:, 0:P * m]
                    else:
                        at = (slice(None), u, slice(None), slice(P * t0, P * (t0 + m)))
                        src = bank[b][:, 0:KD * P * m].rearrange("p (k s) -> p k s", k=KD)
                    dve.tensor_copy(tokT_high[at], src).then_inc(tokT_chain, 1)
                    dve.wait_ge(tokT_chain, 3 * g + n + 1)
                    dve.tensor_tensor(tokT_low[at], src, tokT_high[at].bitcast(F32), ALU.subtract).then_inc(tokT_ready, 1)

                def step(it, u, turn, live):
                    if not live(LM):
                        for n in range(3):
                            transposed(it + BEFORE, u, n)
                    else:
                        e, g = it - LM, it - LM + BEFORE
                        for c in range(KF):
                            dve.wait_ge(h_high, KF * g + c + 1)
                            dve.tensor_tensor(hT_low[:, c, :], h[:, c % RING, :], hT_high[:, c, :].bitcast(F32), ALU.subtract).then_inc(h_split, 1)
                            if live(LT) and c in T_AFTER:
                                transposed(it + BEFORE, u, T_AFTER.index(c))
                    if live(LM):
                        e, g, v = it - LM, it - LM + BEFORE, 1 - u
                        before = turn - 1 if u == 0 else turn
                        at_least(dve, y_stored[v], 16 * (before + BEFORE // 2))
                        dve.wait_ge(b2_loaded[v], 16 * (before + 1 + BEFORE // 2))
                        for t in range(TS):
                            dve.wait_ge(y_psum, TS * g + t + 1)
                            dve.tensor_tensor(y[:, v, t, :], bank[4 + t % 2][:, 0:D], b2b[:, v, :], ALU.add).then_inc(y_ready, 1)

                turns(dve, 1, step)


class Gathered:

    RING = 4

    def __init__(self, core, buffers, name, call):
        self.core, self.turns, self.tiles = core, core.NT // self.RING * call, core.NT * call
        self.rows = buffers.sb(name + "g_rows", [P, self.RING, 2, 256])
        self.fetched = [core.shared.sem(f"g_fetched{u}") for u in range(self.RING)]
        self.added = core.shared.sem("g_added")

    def gather(self, pool, i):
        core, R = self.core, self.RING
        if i >= R:
            pool.wait_ge(self.added, 2 * (i - R + 1 + self.tiles))
        for r in range(2):
            pool.indirect_dma_start(
                out=self.rows[:, i % R, r, :], out_offset=None, in_=core.expert_out[:, :],
                in_offset=bass.IndirectOffsetOnAxis(ap=core.gather_at[:, r, i:i + 1], axis=0)).then_inc(self.fetched[i % R], 16)

    def add(self, dve, turn, u, i):
        x = self.core.x
        dve.wait_ge(self.fetched[u], 32 * (turn + 1 + self.turns))
        for r in range(2):
            dve.scalar_tensor_tensor(x[:, i, :], self.rows[:, u, r, :], self.core.weight[:, r, bass.ds(i, 1)], x[:, i, :],
                                     ALU.mult, ALU.add).then_inc(self.added, 1)
            dve.wait_ge(self.added, 2 * (i + self.tiles) + r + 1)


def combine(nc, core, out):
    NT, x, R = core.NT, core.x, Gathered.RING
    with ExitStack() as stack:
        B = Buffers(nc, stack)
        rows_in = Gathered(core, B, "c_", 1)
        stored = B.sem("c_stored")
        with nc.Block() as block:

            @block.gpsimd
            def _(pool):
                for i in range(NT):
                    rows_in.gather(pool, i)

            @block.vector
            def _(dve):
                with dve.Fori(0, NT // R) as turn:
                    for u in range(R):
                        rows_in.add(dve, turn, u, R * turn + u)

            @block.sync
            def _(sp):
                with sp.Fori(0, NT // R) as turn:
                    sp.wait_ge(rows_in.added, 2 * (R * (turn + 1) + rows_in.tiles))
                    sp.dma_start(out[bass.ds(turn * R * P, R * P), :].rearrange("(t p) d -> p t d", p=P),
                                 x[:, bass.ds(turn * R, R), :]).then_inc(stored, 16)
                sp.wait_ge(stored, 16 * (NT // R))


def nystrom_attention(nc, core, wqkT, wvT, woT, bqk, bv, bo, rwT, rb):
    x, xn_all, cst, NT = core.x, core.xn, core.cst, core.NT
    KD, BT = 2, 8
    NB = NT // BT
    PR = 8
    ITERS = 6
    SIM1, SIM2, SIM3 = 1.0 / 64, 1.0 / 1024, 1.0 / 64
    with ExitStack() as stack:
        B = Buffers(nc, stack)
        wqk = B.sb("n_wqk", [P, KD, 512])
        wv = B.sb("n_wv", [P, KD, 256])
        wo = B.sb("n_wo", [P, KD, 256])
        rw = B.sb("n_rw", [P, KD, 16])
        bias_qk = B.sb("n_bias_qk", [P, 4])
        bias_v = B.sb("n_bias_v", [P, 256])
        bias_o = B.sb("n_bias_o", [P, 256])
        bias_r = B.sb("n_bias_r", [P, 16])
        tick = B.sb("n_tick", [P, 2])
        stats = B.sb("n_stats", [P, 6])
        mv = B.sb("n_mv", [P, 2])
        rstd = B.sb("n_rstd", [P, 1])
        xln = B.sb("n_xln", [P, 2, 256])
        xlnT = B.sb("n_xlnT", [P, 2, KD, P])
        q_next = B.sb("n_q_next", [P, KD, BT * P])
        qT = B.sb("n_qT", [P, KD, BT * P])
        kT = B.sb("n_kT", [P, KD, BT * P])
        v = B.sb("n_v", [P, BT, 256])
        q_sum = B.sb("n_q_sum", [P, KD, 64])
        k_sum = B.sb("n_k_sum", [P, KD, 64])
        q_blk = B.sb("n_q_blk", [P, KD, 8, 64])
        k_blk = B.sb("n_k_blk", [P, KD, 8, 64])
        e3 = B.sb("n_e3", [P, 2, BT * P])
        e3T = B.sb("n_e3T", [P, 2, BT, P])
        max3 = B.sb("n_max3", [P, PR])
        neg3 = B.sb("n_neg3", [P, PR])
        sum3 = B.sb("n_sum3", [P, PR])
        rec3 = B.sb("n_rec3", [P, PR])
        max2 = B.sb("n_max2", [P, PR])
        sum2 = B.sb("n_sum2", [P, PR])
        s2 = B.sb("n_s2", [P, PR, 64])
        pw = B.sb("n_pw", [P, PR, 80])
        p_blk = B.sb("n_p_blk", [P, PR, P])
        q1 = B.sb("n_q1", [P, PR, 64])
        q2 = B.sb("n_q2", [P, PR, 64])
        q3 = B.sb("n_q3", [P, PR, 64])
        q3_blk = B.sb("n_q3_blk", [P, PR, P])
        z_blk = B.sb("n_z_blk", [P, PR, 34])
        max1 = B.sb("n_max1", [P, 2, 8])
        s1 = B.sb("n_s1", [P, 2, 8, 64])
        e1 = B.sb("n_e1", [P, 2, 16, 64])
        e1T = B.sb("n_e1T", [P, PR, P])
        den = B.sb("n_den", [P, 16])
        o = B.sb("n_o", [P, 2, 256])
        oT = B.sb("n_oT", [P, KD, P])
        stats2 = B.sb("n_stats2", [P, 6])
        mv2 = B.sb("n_mv2", [P, 2])
        rstd2 = B.sb("n_rstd2", [P, 1])
        xr = B.sb("n_xr", [P, 2, 256])
        xrT = B.sb("n_xrT", [P, KD, P])
        psum, bank = core.psum, core.bank
        routing = Routing(core, B, "n_", 1)
        rows_in = Gathered(core, B, "n_", 0)

        names = ("loaded made ln_chain rstd_ready xln_ready xlnT_psum xlnT_ready qk_psum v_psum qk_ready v_ready sums_ready "
                 "q_moved q_blk_ready k_blk_ready s2_psum s2_chain s2_shifted e2_ready k_ready kT_psum kT_ready kT_blk_ready "
                 "s3_psum s3_chain neg3_ready e3_ready e3T_psum e3Ta_ready e3Tb_ready b3_psum b3_chain w_ready "
                 "xa_psum xb_psum xa_read xb_read ya_psum yb_psum ya_read yb_read "
                 "s1_psum s1_chain s1_shifted e1_ready e1T_psum e1Ta_ready e1Tb_ready o_psum o_chain o_ready oT_psum oT_ready "
                 "y_psum x_chain r_rstd xr_ready xr_kept xrT_psum xrT_ready logits_psum logits_read").split()
        S = {name: B.sem("n_" + name) for name in names}
        ident = cst[:, C_IDENT:C_IDENT + P]
        eye = [cst[:, C_EYE7 + 64 * n:C_EYE7 + 64 * n + 64].unsqueeze(1).to_broadcast([P, 4, 64]) for n in range(3)]
        TOP, LOW = slice(0, 64), slice(64, P)

        X_PER, Y_PER = 1 + 3 * ITERS - 1, 1 + ITERS

        def x_count(b, n, what):
            return X_PER * b + (1 if n < 0 else 1 + 3 * n + what + 1)

        def y_count(b, n):
            return Y_PER * b + n + 2

        def first(b):
            return isinstance(b, int) and b == 0

        SLOTS = 2 * (BT - 1) + 7

        def stages(slot, project, b):
            for lag, stage in ((2, "normalise"), (3, "transpose"), (5, "v"), (4, "qk"), (0, "add"), (1, "stats"), (6, "sums")):
                t, odd = divmod(slot - lag, 2)
                if not odd and 0 <= t < BT:
                    project(b, t, stage)

        def batches(eng, project, pairs, inverse, rows, loop=True):
            def tail(b, step):
                if not first(b + 1):
                    rows(b, BT + step)

            def body(b, more):
                pairs(b, "open")
                tail(b - 1, 0)
                if eng is nc.tensor:
                    pairs(b, "landmarks")
                    pairs(b, 0)
                    tail(b - 1, 1)
                else:
                    tail(b - 1, 1)
                    pairs(b, 0)
                    pairs(b, "landmarks")
                pairs(b, 1)
                tail(b - 1, 2)
                for step in range(2, PR):
                    pairs(b, step)
                if more:
                    stages(0, project, b + 1)
                pairs(b, PR)
                if more:
                    stages(1, project, b + 1)
                pairs(b, "close")
                if more:
                    stages(2, project, b + 1)
                pairs(b, PR + 1)
                for slot in range(3 * ITERS + 1):
                    for group in range(2):
                        inverse(b, (slot + 2) // 3 - 1, (slot + 2) % 3, group)
                    if more:
                        stages(slot + 3, project, b + 1)
                for step in range(BT):
                    rows(b, step)

            for slot in range(SLOTS):
                stages(slot, project, 0)
            body(0, True)
            if loop:
                with eng.Fori(1, NB - 1) as b:
                    body(b, True)
            else:
                for b in range(1, NB - 1):
                    body(b, True)
            body(NB - 1, False)
            for step in range(3):
                tail(NB - 1, step)

        with nc.Block() as block:

            @block.sync
            def _(sp):
                for dst, src in ((wqk, wqkT), (wv, wvT), (wo, woT), (rw, rwT)):
                    sp.dma_start(dst[:, :, :], src.rearrange("(k p) n -> p k n", p=P)).then_inc(S["loaded"], 16)
                sp.dma_start(bias_qk[:, :], bqk.rearrange("(g p) -> p g", p=P), allow_slow_non_contiguous=True).then_inc(S["loaded"], 16)
                sp.dma_start(bias_v[:, :], bv[None, :].to_broadcast([P, 256])).then_inc(S["loaded"], 16)
                sp.dma_start(bias_o[:, :], bo[None, :].to_broadcast([P, 256])).then_inc(S["loaded"], 16)
                sp.dma_start(bias_r[:, :], rb[None, :].to_broadcast([P, 16])).then_inc(S["loaded"], 16)
                load_w1(sp, core, *core.first_layer, 0, 0)
                load_w2(sp, core, core.second_layer, 0)

            @block.gpsimd
            def _(pool):
                AHEAD = 2
                pool.memset(p_blk[:, :, :], 0.0).then_inc(S["made"], 1)
                pool.memset(q3_blk[:, :, :], 0.0).then_inc(S["made"], 1)
                pool.memset(z_blk[:, :, :], 0.0).then_inc(S["made"], 1)
                pool.wait_ge(S["made"], 3)
                pool.memset(z_blk[TOP, :, 16:17], 1.0).then_inc(S["made"], 1)
                pool.memset(z_blk[LOW, :, 33:34], 1.0).then_inc(S["made"], 1)

                def project(b, t, stage):
                    if stage == "stats":
                        pool.wait_ge(S["ln_chain"], 3 * (BT * b + t) + 3)
                        pool.tensor_tensor(rstd[:, :], mv[:, 1:2], core.minus_half[:, :], ALU.pow).then_inc(S["rstd_ready"], 1)
                        if BT * b + t + AHEAD < NT:
                            rows_in.gather(pool, BT * b + t + AHEAD)

                def pairs(b, step):
                    if step == 2:
                        pool.wait_ge(S["sums_ready"], 2 * BT * b + 2 * BT)
                        at_least(pool, S["s1_psum"], 2 * BT * b)
                        for k in range(KD):
                            ins = pool.tensor_tensor(k_blk[:, k, :, :], k_sum[:, k:k + 1, :].to_broadcast([P, 8, 64]),
                                                     cst[:, C_HEAD8:C_HEAD8 + 8].unsqueeze(2).to_broadcast([P, 8, 64]), ALU.mult)
                        ins.then_inc(S["k_blk_ready"], 1)
                        pool.tensor_copy(qT[:, :, :], q_next[:, :, :]).then_inc(S["q_moved"], 1)

                def inverse(b, n, what, group):
                    tile, odd = divmod(3 * (n + 1) + what - 3, 2)
                    if group == 1 and not odd and 0 <= tile < BT and b > 0:
                        send(BT * (b - 1) + tile)

                def rows(b, step):
                    if 0 <= step - 2 < BT:
                        i = BT * b + step - 2
                        pool.wait_ge(S["x_chain"], 5 * i + 5)
                        pool.tensor_tensor(rstd2[:, :], mv2[:, 1:2], core.minus_half[:, :], ALU.pow).then_inc(S["r_rstd"], 1)
                        pool.wait_ge(S["xr_ready"], i + 1)
                        if step == 2 and b >= 2:
                            routing.wait_scattered(pool, b - 2)
                        pool.tensor_copy(xn_all[:, i % (2 * BT), :], xr[:, step % 2, :]).then_inc(S["xr_kept"], 1)

                def send(i):
                    pool.wait_ge(S["xr_kept"], i + 1)
                    routing.scatter(pool, i)

                for i in range(AHEAD):
                    rows_in.gather(pool, i)
                batches(pool, project, pairs, inverse, rows, loop=False)
                for i in range(NT - BT, NT):
                    send(i)
                for g in (NB - 2, NB - 1):
                    routing.wait_scattered(pool, g)

            @block.scalar
            def _(act):
                act.wait_ge(S["loaded"], 16 * 8)
                act.wait_ge(S["made"], 5)

                def project(b, t, stage):
                    i = BT * b + t
                    if stage == "transpose":
                        act.wait_ge(S["xlnT_psum"], i + 1)
                        at_least(act, S["v_psum"], i - 1)
                        act.activation(xlnT[:, t % 2, :, :], bank[4][:, 0:256].rearrange("p (k t) -> p k t", k=KD), ACT.Copy).then_inc(S["xlnT_ready"], 1)
                    if stage == "qk":
                        act.wait_ge(S["qk_psum"], i + 1)
                        if t == 0:
                            at_least(act, S["q_moved"], b)
                            at_least(act, S["s3_psum"], PR * b)
                        for g in range(4):
                            dst = (q_next, kT)[g // 2]
                            ins = act.activation(dst[:, g % 2, P * t:P * t + P], bank[5][:, P * g:P * g + P], ACT.Identity, bias=bias_qk[:, g:g + 1])
                        ins.then_inc(S["qk_ready"], 1)

                def pairs(b, step):
                    if step == "landmarks":
                        act.wait_ge(S["s2_shifted"], b + 1)
                        act.activation(s2[:, :, :], s2[:, :, :], ACT.Exp, scale=SIM2).then_inc(S["e2_ready"], 1)
                    elif isinstance(step, int):
                        if step == 5 and not first(b):
                            routing.exponentials(act, b - 1)
                        if step < PR:
                            n = PR * b + step
                            act.wait_ge(S["neg3_ready"], n + 1)
                            at_least(act, S["e3T_psum"], 2 * (PR * b + max(step - 1, 0)))
                            act.activation(e3[:, step % 2, :].rearrange("p (a s) -> p a s", a=2),
                                           psum[:, 2 * (step % 2):2 * (step % 2) + 2, :], ACT.Exp, scale=SIM3,
                                           bias=neg3[:, step:step + 1], accum_out=sum3[:, step:step + 1]).then_inc(S["e3_ready"], 1)
                        if 1 <= step <= PR:
                            n, u = PR * b + step - 1, (step - 1) % 2
                            act.wait_ge(S["e3T_psum"], 2 * n + 1)
                            at_least(act, S["b3_psum"], PR * b + max(step - 2, 0))
                            act.activation(e3T[:, u, 0:4, :], bank[4][:, :].rearrange("p (a s) -> p a s", a=4), ACT.Copy).then_inc(S["e3Ta_ready"], 1)
                    elif step == "close":
                        act.wait_ge(S["kT_psum"], 2 * b + 2)
                        for half in range(2):
                            src = bank[4 + half][:, :].rearrange("p (a s) -> p a s", a=4)
                            act.activation(q3_blk[TOP, 4 * half:4 * half + 4, 0:64], src[TOP, :, 0:64], ACT.Copy)
                            act.activation(q3_blk[LOW, 4 * half:4 * half + 4, 64:P], src[LOW, :, 64:P], ACT.Copy).then_inc(S["kT_blk_ready"], 1)

                def inverse(b, n, what, group):
                    if what != 2:
                        return
                    g4 = slice(4 * group, 4 * group + 4)
                    scale = 1.0 if n < 0 else 0.25
                    y = bank[1 + 2 * group][:, 0:320].rearrange("p (a c) -> p a c", a=4)
                    act.wait_ge(S["y%s_psum" % "ab"[group]], y_count(b, n))
                    if n == ITERS - 1:
                        at_least(act, S["o_psum"], BT * b)
                        act.activation(z_blk[TOP, g4, 0:16], y[TOP, :, 64:80], ACT.Copy, scale=scale)
                        act.activation(z_blk[LOW, g4, 17:33], y[LOW, :, 64:80], ACT.Copy, scale=scale).then_inc(S["y%s_read" % "ab"[group]], 1)
                        return
                    act.wait_ge(S["x%s_psum" % "ab"[group]], x_count(b, n, 2))
                    act.activation(p_blk[TOP, g4, 0:64], y[TOP, :, 0:64], ACT.Copy, scale=scale)
                    act.activation(p_blk[LOW, g4, 64:P], y[LOW, :, 0:64], ACT.Copy, scale=scale)
                    act.activation(pw[:, g4, :], y[:, :, :], ACT.Copy, scale=scale).then_inc(S["y%s_read" % "ab"[group]], 1)

                def rows(b, step):
                    def exponentials(half):
                        if step < BT:
                            act.wait_ge(S["s1_shifted"], 2 * (BT * b + step) + half + 1)
                            at_least(act, S["e1T_psum"], 2 * (BT * b + max(step - 1, 0)))
                            act.activation(e1[:, step % 2, 8 * half:8 * half + 8, :], s1[:, half, :, :], ACT.Exp, scale=SIM1).then_inc(S["e1_ready"], 1)

                    exponentials(0)
                    if 0 <= step - 2 < BT:
                        i = BT * b + step - 2
                        act.wait_ge(S["oT_psum"], i + 1)
                        at_least(act, S["y_psum"], i)
                        act.activation(oT[:, :, :], bank[5][:, 0:256].rearrange("p (k t) -> p k t", k=KD), ACT.Copy).then_inc(S["oT_ready"], 1)
                    exponentials(1)
                    if 0 <= step - 1 < BT:
                        i = BT * b + step - 1
                        act.wait_ge(S["e1T_psum"], 2 * i + 1)
                        at_least(act, S["o_psum"], i)
                        act.activation(e1T[:, 0:4, :], bank[2][:, :].rearrange("p (a s) -> p a s", a=4), ACT.Copy).then_inc(S["e1Ta_ready"], 1)
                    if 0 <= step - 3 < BT:
                        i = BT * b + step - 3
                        act.wait_ge(S["xrT_psum"], i + 1)
                        at_least(act, S["logits_psum"], i)
                        act.activation(xrT[:, :, :], bank[6][:, 0:256].rearrange("p (k t) -> p k t", k=KD), ACT.Copy).then_inc(S["xrT_ready"], 1)

                batches(act, project, pairs, inverse, rows)
                routing.exponentials(act, NB - 1)

            @block.tensor
            def _(pe):
                pe.wait_ge(S["loaded"], 16 * 8)
                pe.wait_ge(S["made"], 5)

                def project(b, t, stage):
                    i, u = BT * b + t, t % 2
                    if stage == "transpose":
                        pe.wait_ge(S["xln_ready"], i + 1)
                        at_least(pe, S["xlnT_ready"], i)
                        for k in range(KD):
                            ins = pe.transpose(bank[4][:, P * k:P * k + P], xln[:, u, P * k:P * k + P], ident)
                        ins.then_inc(S["xlnT_psum"], 1)
                    if stage == "qk":
                        pe.wait_ge(S["xlnT_ready"], i + 1)
                        at_least(pe, S["qk_ready"], i)
                        for g in range(4):
                            for k in range(KD):
                                ins = pe.matmul(bank[5][:, P * g:P * g + P], wqk[:, k, P * g:P * g + P], xlnT[:, u, k, :],
                                                start=(k == 0), stop=(k == KD - 1))
                        ins.then_inc(S["qk_psum"], 1)
                    if stage == "v":
                        at_least(pe, S["v_ready"], i)
                        for k in range(KD):
                            ins = pe.matmul(bank[6][:, 0:256], xlnT[:, u, k, :], wv[:, k, :], start=(k == 0), stop=(k == KD - 1))
                        ins.then_inc(S["v_psum"], 1)

                def pairs(b, step):
                    if step == "landmarks":
                        pe.wait_ge(S["q_blk_ready"], b + 1)
                        for pr in range(PR):
                            ins = pe.matmul(bank[7][:, 64 * pr:64 * pr + 64], q_blk[:, pr // 4, 2 * (pr % 4):2 * (pr % 4) + 2, :],
                                            k_sum[:, pr // 4, :], start=True, stop=True)
                        ins.then_inc(S["s2_psum"], 1)
                    if step == "close":
                        pe.wait_ge(S["k_ready"], b + 1)
                        for half in range(2):
                            at_least(pe, S["e3T%s_ready" % "ab"[half]], PR * b + PR)
                            for pr in range(4 * half, 4 * half + 4):
                                ins = pe.transpose(bank[4 + half][:, P * (pr % 4):P * (pr % 4) + P], p_blk[:, pr, :], ident)
                            ins.then_inc(S["kT_psum"], 1)
                    if not isinstance(step, int):
                        return
                    if step == 5 and not first(b):
                        pe.wait_ge(S["s2_shifted"], b + 1)
                        routing.count(pe, b - 1, bank[7])
                    if step < PR:
                        n, pr = PR * b + step, step
                        if step == 0:
                            at_least(pe, S["s1_shifted"], 2 * BT * b)
                        else:
                            at_least(pe, S["e3_ready"], PR * b + step - 1)
                        for c in range(2):
                            ins = pe.matmul(bank[2 * (step % 2) + c][:, :], q_blk[:, pr // 4, 2 * (pr % 4):2 * (pr % 4) + 2, :],
                                            kT[:, pr // 4, 512 * c:512 * c + 512], start=True, stop=True)
                        ins.then_inc(S["s3_psum"], 1)
                    if step == 2 and not first(b):
                        row_logits(BT * b - 1)
                    if step >= 2:
                        n, pr, u = PR * b + step - 2, step - 2, step % 2
                        pe.wait_ge(S["e3Ta_ready"], n + 1)
                        pe.wait_ge(S["e3Tb_ready"], n + 1)
                        if step == 2:
                            at_least(pe, S["logits_read"], BT * b)
                        for s in range(BT):
                            ins = pe.matmul(bank[6][:, 32 * pr:32 * pr + 32], e3T[:, u, s, :], v[:, s, 32 * pr:32 * pr + 32],
                                            start=(s == 0), stop=(s == BT - 1))
                        ins.then_inc(S["b3_psum"], 1)
                    if 1 <= step <= PR:
                        n, u = PR * b + step - 1, (step - 1) % 2
                        pe.wait_ge(S["e3_ready"], n + 1)
                        if step == 1:
                            at_least(pe, S["o_ready"], BT * b)
                            at_least(pe, S["x_chain"], 5 * BT * b - 4)
                        for c in range(2):
                            at_least(pe, S["e3T%s_ready" % "ab"[c]], n)
                            for s in range(4 * c, 4 * c + 4):
                                ins = pe.transpose(bank[4 + c][:, P * (s % 4):P * (s % 4) + P], e3[:, u, P * s:P * s + P], ident)
                            ins.then_inc(S["e3T_psum"], 1)

                def inverse(b, n, what, group):
                    ab = "ab"[group]
                    xb, yb = bank[2 * group], bank[1 + 2 * group]
                    xs, ys = S["x%s_psum" % ab], S["y%s_psum" % ab]
                    g4 = range(4 * group, 4 * group + 4)
                    if n < 0:
                        pe.wait_ge(S["kT_blk_ready"], 2 * b + 2)
                        pe.wait_ge(S["kT_ready"], b + 1)
                        pe.wait_ge(S["w_ready"], b + 1)
                    else:
                        pe.wait_ge(S["x%s_read" % ab], x_count(b, n, what - 1) if what else x_count(b, n - 1, 2))
                        if what == 0:
                            pe.wait_ge(S["y%s_read" % ab], y_count(b, n - 1))
                    if what < 2:
                        for pr in g4:
                            ins = pe.matmul(xb[:, 64 * (pr % 4):64 * (pr % 4) + 64], p_blk[:, pr, :], (q1, q2)[what][:, pr, :],
                                            start=True, stop=True)
                        ins.then_inc(xs, 1)
                        return
                    lo = 0 if n < ITERS - 1 else 64
                    for pr in g4:
                        ins = pe.matmul(yb[:, 80 * (pr % 4) + lo:80 * (pr % 4) + 80], q3_blk[:, pr, :], pw[:, pr, lo:80],
                                        start=True, stop=True)
                    ins.then_inc(ys, 1)
                    if n < ITERS - 1:
                        for pr in g4:
                            ins = pe.matmul(xb[:, 64 * (pr % 4):64 * (pr % 4) + 64], p_blk[:, pr, :], q3[:, pr, :],
                                            start=True, stop=True)
                        ins.then_inc(xs, 1)

                def rows(b, step):
                    if step < BT:
                        i = BT * b + step
                        if step == 0:
                            pe.wait_ge(S["q_moved"], b + 1)
                            pe.wait_ge(S["k_blk_ready"], b + 1)
                            for ab in "ab":
                                pe.wait_ge(S["y%s_read" % ab], Y_PER * (b + 1))
                        for half in range(2):
                            at_least(pe, S["s1_shifted"], 2 * BT * b + max(2 * step + half - 1, 0))
                            pe.matmul(bank[half][:, :], qT[:, half, P * step:P * step + P], k_blk[:, half, :, :],
                                      start=True, stop=True).then_inc(S["s1_psum"], 1)
                    if 0 <= step - 2 < BT:
                        i, u = BT * b + step - 2, step % 2
                        pe.wait_ge(S["o_ready"], i + 1)
                        at_least(pe, S["x_chain"], 5 * BT * b + max(5 * (step - 3) + 1, 0))
                        for k in range(KD):
                            ins = pe.transpose(bank[5][:, P * k:P * k + P], o[:, u, P * k:P * k + P], ident)
                        ins.then_inc(S["oT_psum"], 1)
                    if 0 <= step - 1 < BT:
                        i, u = BT * b + step - 1, (step - 1) % 2
                        pe.wait_ge(S["e1_ready"], 2 * i + 2)
                        for c in range(2):
                            at_least(pe, S["e1T%s_ready" % "ab"[c]], i)
                            for pr in range(4 * c, 4 * c + 4):
                                ins = pe.transpose(bank[2 + c][:, P * (pr % 4):P * (pr % 4) + P], e1[:, u, 2 * pr:2 * pr + 2, :], ident)
                            ins.then_inc(S["e1T_psum"], 1)
                    if 0 <= step - 2 < BT:
                        i = BT * b + step - 2
                        pe.wait_ge(S["oT_ready"], i + 1)
                        for k in range(KD):
                            ins = pe.matmul(bank[5][:, 256:512], oT[:, k, :], wo[:, k, :], start=(k == 0), stop=(k == KD - 1))
                        ins.then_inc(S["y_psum"], 1)
                    if 0 <= step - 3 < BT:
                        i, u = BT * b + step - 3, (step - 3) % 2
                        pe.wait_ge(S["xr_ready"], i + 1)
                        at_least(pe, S["logits_read"], i)
                        for k in range(KD):
                            ins = pe.transpose(bank[6][:, P * k:P * k + P], xr[:, u, P * k:P * k + P], ident)
                        ins.then_inc(S["xrT_psum"], 1)
                    if 0 <= step - 1 < BT:
                        i, u = BT * b + step - 1, (step - 1) % 2
                        at_least(pe, S["o_ready"], i)
                        for pr in range(PR):
                            if pr % 4 == 0:
                                pe.wait_ge(S["e1T%s_ready" % "ab"[pr // 4]], i + 1)
                            ins = pe.matmul(bank[4][:, 34 * pr:34 * pr + 34], e1T[:, pr, :], z_blk[:, pr, :], start=True, stop=True)
                        ins.then_inc(S["o_psum"], 1)
                    if 0 <= step - 3 < BT - 1 or (step - 3 == BT - 1 and isinstance(b, int) and b == NB - 1):
                        row_logits(BT * b + step - 3)

                def row_logits(i):
                    pe.wait_ge(S["xrT_ready"], i + 1)
                    for k in range(KD):
                        ins = pe.matmul(bank[6][:, 256:272], xrT[:, k, :], rw[:, k, :], start=(k == 0), stop=(k == KD - 1))
                    ins.then_inc(S["logits_psum"], 1)

                batches(pe, project, pairs, inverse, rows)
                routing.count(pe, NB - 1, bank[7])

            @block.vector
            def _(dve):
                dve.wait_ge(S["loaded"], 16 * 8)
                dve.wait_ge(S["made"], 5)
                routing.prepare(dve)

                def variance(src, st, m, chain, done):
                    dve.memset(tick[:, 0:1], 0.0)
                    dve.bn_stats(st, src).then_inc(chain, 1)
                    at_least(dve, chain, done + 1)
                    dve.memset(tick[:, 1:2], 0.0)
                    dve.bn_aggr(m, st).then_inc(chain, 1)
                    at_least(dve, chain, done + 2)
                    dve.tensor_scalar(m[:, 1:2], m[:, 1:2], LN_EPS, None, ALU.add).then_inc(chain, 1)

                def project(b, t, stage):
                    i, u = BT * b + t, t % 2
                    if stage == "stats":
                        at_least(dve, S["xln_ready"], i)
                        variance(x[:, i, :], stats[:, :], mv[:, :], S["ln_chain"], 3 * i)
                    if stage == "add":
                        rows_in.add(dve, BT // rows_in.RING * b + t // rows_in.RING, t % rows_in.RING, i)
                    if stage == "normalise":
                        dve.wait_ge(S["rstd_ready"], i + 1)
                        at_least(dve, S["xlnT_psum"], i - 1)
                        dve.tensor_scalar(xln[:, u, :], x[:, i, :], mv[:, 0:1], rstd[:, :], ALU.subtract, ALU.mult).then_inc(S["xln_ready"], 1)
                    if stage == "v":
                        dve.wait_ge(S["v_psum"], i + 1)
                        if t == 0:
                            at_least(dve, S["b3_psum"], PR * b)
                        dve.tensor_tensor(v[:, t, :], bank[6][:, 0:256], bias_v[:, :], ALU.add).then_inc(S["v_ready"], 1)
                    if stage == "sums":
                        dve.wait_ge(S["qk_ready"], i + 1)
                        if t == 0:
                            at_least(dve, S["k_blk_ready"], b)
                            at_least(dve, S["s2_psum"], b)
                        for dst, src in ((q_sum, q_next), (k_sum, kT)):
                            dve.tensor_reduce(dst[:, :, 8 * t:8 * t + 8], src[:, :, P * t:P * t + P].rearrange("p k (j l) -> p k j l", l=16),
                                              AX_X, ALU.add).then_inc(S["sums_ready"], 1)

                ROUTE = {2: range(1, 5), 3: range(5, 9), 4: range(9, 13), 6: range(13, 19), 7: range(19, 25),
                         8: range(25, 29), PR + 1: range(29, 33)}

                def pairs(b, step):
                    if step == "open":
                        dve.wait_ge(S["sums_ready"], 2 * BT * b + 2 * BT)
                        at_least(dve, S["s3_psum"], PR * b)
                        for k in range(KD):
                            ins = dve.tensor_tensor(q_blk[:, k, :, :], q_sum[:, k:k + 1, :].to_broadcast([P, 8, 64]),
                                                    cst[:, C_HEAD8:C_HEAD8 + 8].unsqueeze(2).to_broadcast([P, 8, 64]), ALU.mult)
                        ins.then_inc(S["q_blk_ready"], 1)
                    if step == "landmarks":
                        s2_ps = bank[7][:, :].rearrange("p (a c) -> p a c", a=PR)
                        dve.wait_ge(S["s2_psum"], b + 1)
                        dve.tensor_reduce(max2[:, :], s2_ps, AX_X, ALU.max).then_inc(S["s2_chain"], 1)
                        dve.wait_ge(S["s2_chain"], 3 * b + 1)
                        dve.tensor_tensor(s2[:, :, :], s2_ps, max2[:, :].unsqueeze(2).to_broadcast([P, PR, 64]), ALU.subtract).then_inc(S["s2_shifted"], 1)
                    if step == "close":
                        dve.wait_ge(S["kT_blk_ready"], 2 * b + 2)
                        for half in range(2):
                            src = bank[4 + half][:, :].rearrange("p (a s) -> p a s", a=4)
                            dve.tensor_copy(q3[TOP, 4 * half:4 * half + 4, :], src[TOP, :, 0:64])
                            ins = dve.tensor_copy(q3[LOW, 4 * half:4 * half + 4, :], src[LOW, :, 64:P])
                        ins.then_inc(S["kT_ready"], 1)
                        dve.wait_ge(S["e3_ready"], PR * b + PR)
                        dve.reciprocal(rec3[:, :], sum3[:, :]).then_inc(S["b3_chain"], 1)
                        dve.wait_ge(S["b3_psum"], PR * b + PR)
                        dve.wait_ge(S["b3_chain"], b + 1)
                        b3 = bank[6][:, 0:256].rearrange("p (a c) -> p a c", a=PR)
                        r3 = rec3[:, :].unsqueeze(2).to_broadcast([P, PR, 16])
                        dve.tensor_tensor(pw[TOP, :, 64:80], b3[TOP, :, 0:16], r3[TOP], ALU.mult)
                        dve.tensor_tensor(pw[LOW, :, 64:80], b3[LOW, :, 16:32], r3[LOW], ALU.mult).then_inc(S["w_ready"], 1)
                    if step in ROUTE and not first(b):
                        if step == 2:
                            dve.wait_ge(S["logits_read"], BT * b)
                        for k in ROUTE[step]:
                            routing.vector(dve, b - 1, k, bank[7])
                    if not isinstance(step, int):
                        return
                    if step < PR:
                        n = PR * b + step
                        dve.wait_ge(S["s3_psum"], n + 1)
                        dve.tensor_reduce(max3[:, step:step + 1], psum[:, 2 * (step % 2):2 * (step % 2) + 2, :], AX_XY, ALU.max).then_inc(S["s3_chain"], 1)
                        dve.wait_ge(S["s3_chain"], n + 1)
                        at_least(dve, S["e3_ready"], PR * b)
                        dve.tensor_scalar(neg3[:, step:step + 1], max3[:, step:step + 1], -SIM3, None, ALU.mult).then_inc(S["neg3_ready"], 1)
                    if 1 <= step <= PR:
                        n, u = PR * b + step - 1, (step - 1) % 2
                        dve.wait_ge(S["e3T_psum"], 2 * n + 2)
                        at_least(dve, S["b3_psum"], PR * b + max(step - 2, 0))
                        dve.tensor_copy(e3T[:, u, 4:8, :], bank[5][:, :].rearrange("p (a s) -> p a s", a=4)).then_inc(S["e3Tb_ready"], 1)
                    if step == 2:
                        dve.wait_ge(S["e2_ready"], b + 1)
                        dve.tensor_reduce(sum2[:, :], s2[:, :, :], AX_X, ALU.add).then_inc(S["s2_chain"], 1)
                        dve.wait_ge(S["s2_chain"], 3 * b + 2)
                        dve.reciprocal(max2[:, :], sum2[:, :]).then_inc(S["s2_chain"], 1)
                        dve.wait_ge(S["s2_chain"], 3 * b + 3)
                        rec2 = max2[:, :].unsqueeze(2).to_broadcast([P, PR, 64])
                        dve.tensor_tensor(pw[:, :, 0:64], s2[:, :, :], rec2, ALU.mult)
                        dve.tensor_tensor(p_blk[TOP, :, 0:64], s2[TOP, :, :], rec2[TOP], ALU.mult)
                        dve.tensor_tensor(p_blk[LOW, :, 64:P], s2[LOW, :, :], rec2[LOW], ALU.mult).then_inc(S["k_ready"], 1)

                def inverse(b, n, what, group):
                    ab = "ab"[group]
                    g4 = slice(4 * group, 4 * group + 4)
                    xb = bank[2 * group][:, 0:256].rearrange("p (a c) -> p a c", a=4)
                    if what == 2 and n == ITERS - 1:
                        return
                    dve.wait_ge(S["x%s_psum" % ab], x_count(b, n, what))
                    done = S["x%s_read" % ab]
                    if what == 2:
                        dve.scalar_tensor_tensor(q1[:, g4, :], xb, -1.0 if n < 0 else -0.25, eye[0], ALU.mult, ALU.add).then_inc(done, 1)
                    elif what == 0:
                        dve.scalar_tensor_tensor(q2[:, g4, :], xb, -1.0, eye[1], ALU.mult, ALU.add).then_inc(done, 1)
                    else:
                        dve.scalar_tensor_tensor(q3_blk[TOP, g4, 0:64], xb[TOP], -1.0, eye[2][TOP], ALU.mult, ALU.add)
                        dve.scalar_tensor_tensor(q3_blk[LOW, g4, 64:P], xb[LOW], -1.0, eye[2][LOW], ALU.mult, ALU.add)
                        dve.scalar_tensor_tensor(q3[:, g4, :], xb, -1.0, eye[2], ALU.mult, ALU.add).then_inc(done, 1)

                def rows(b, step):
                    if step < BT:
                        for half in range(2):
                            n = 2 * (BT * b + step) + half
                            s_ps = bank[half][:, :].rearrange("p (h j) -> p h j", h=8)
                            dve.wait_ge(S["s1_psum"], n + 1)
                            dve.tensor_reduce(max1[:, half, :], s_ps, AX_X, ALU.max).then_inc(S["s1_chain"], 1)
                            dve.wait_ge(S["s1_chain"], n + 1)
                            at_least(dve, S["e1_ready"], 2 * BT * b + max(2 * step + half - 1, 0))
                            dve.tensor_tensor(s1[:, half, :, :], s_ps, max1[:, half, :].unsqueeze(2).to_broadcast([P, 8, 64]),
                                              ALU.subtract).then_inc(S["s1_shifted"], 1)
                    if 0 <= step - 1 < BT:
                        i, u = BT * b + step - 1, (step - 1) % 2
                        dve.wait_ge(S["e1T_psum"], 2 * i + 2)
                        at_least(dve, S["o_psum"], i)
                        dve.tensor_copy(e1T[:, 4:8, :], bank[3][:, :].rearrange("p (a s) -> p a s", a=4)).then_inc(S["e1Tb_ready"], 1)
                    if 0 <= step - 2 < BT:
                        i, u = BT * b + step - 2, step % 2
                        dve.wait_ge(S["y_psum"], i + 1)
                        dve.tensor_tensor(x[:, i, :], x[:, i, :], bank[5][:, 256:512], ALU.add).then_inc(S["x_chain"], 1)
                        dve.wait_ge(S["x_chain"], 5 * i + 1)
                        dve.tensor_tensor(x[:, i, :], x[:, i, :], bias_o[:, :], ALU.add).then_inc(S["x_chain"], 1)
                        dve.wait_ge(S["x_chain"], 5 * i + 2)
                        variance(x[:, i, :], stats2[:, :], mv2[:, :], S["x_chain"], 5 * i + 2)
                    if 0 <= step - 1 < BT:
                        i, u = BT * b + step - 1, (step - 1) % 2
                        ops = bank[4][:, 0:272].rearrange("p (h e) -> p h e", h=16)
                        dve.wait_ge(S["o_psum"], i + 1)
                        dve.reciprocal(den[:, :], ops[:, :, 16]).then_inc(S["o_chain"], 1)
                        dve.wait_ge(S["o_chain"], i + 1)
                        at_least(dve, S["oT_psum"], BT * b + max(step - 2, 0))
                        dve.tensor_tensor(o[:, u, :].rearrange("p (h e) -> p h e", h=16), ops[:, :, 0:16],
                                          den[:, :].unsqueeze(2).to_broadcast([P, 16, 16]), ALU.mult).then_inc(S["o_ready"], 1)
                    if 0 <= step - 2 < BT:
                        i, u = BT * b + step - 2, step % 2
                        dve.wait_ge(S["r_rstd"], i + 1)
                        at_least(dve, S["xrT_psum"], BT * b + max(step - 3, 0))
                        at_least(dve, S["xr_kept"], BT * b + max(step - 3, 0))
                        dve.tensor_scalar(xr[:, u, :], x[:, i, :], mv2[:, 0:1], rstd2[:, :], ALU.subtract, ALU.mult).then_inc(S["xr_ready"], 1)
                    if 0 <= step - 3 < BT:
                        i = BT * b + step - 3
                        dve.wait_ge(S["logits_psum"], i + 1)
                        dve.tensor_tensor(routing.logits[:, step - 3, :], bank[6][:, 256:272], bias_r[:, :], ALU.add).then_inc(S["logits_read"], 1)

                batches(dve, project, pairs, inverse, rows)
                dve.wait_ge(S["logits_read"], NT)
                for k in range(1, routing.STEPS + 1):
                    routing.vector(dve, NB - 1, k, bank[7])


class Core:
    pass


def build_program(nc, a, out):
    with ExitStack() as stack:
        B = Buffers(nc, stack)
        core = Core()
        core.NT, core.NE, core.CAP, core.GT = 32, 16, 640, 8
        slots, spare = core.NE * core.CAP, 2 * core.NT * P
        core.x = B.sb("x_tokens", [P, core.NT, 256])
        core.cst = B.sb("const", [P, C_WIDTH])
        core.cst_dram = a["const"]
        core.minus_half = B.sb("minus_half", [P, 1])
        core.gather_at = B.sb("gather_at", [P, 2, core.NT], I32)
        core.weight = B.sb("gate_weight", [P, 2, core.NT])
        core.psum = B.ps("psum", [P, 8, 512])
        core.bank = [core.psum[:, i, :] for i in range(8)]
        core.slots_dram = nc.dram_tensor("slots_dram", [slots + spare, 256], F32, kind="Internal").ap()
        core.expert_out = nc.dram_tensor("expert_out", [slots, 256], F32, kind="Internal").ap()
        core.zeroed = B.sem("zeroed")
        core.first_layer, core.second_layer = (a["w1"], a["b1"]), a["w2"]
        _, D, F = a["w1"].shape
        core.w1b = B.sb("expert_w1", [P, D // P, F])
        core.w2b = B.sb("expert_w2", [P, F // P, D])
        core.b1b = B.sb("expert_b1", [P, 2, F // P])
        core.shared = Shared(B)

        with ExitStack() as tokens:
            core.xn = Buffers(nc, tokens).sb("xn_tokens_a", [P, core.NT, 256])
            linear_attention(nc, core, a["x"], a["a_wqkT"], a["a_wvT"], a["a_woT"], a["a_bqk"], a["a_bv"], a["a_bo"],
                             a["rwT"], a["rb"])
        experts(nc, core, a["w1"], a["b1"], a["w2"], a["b2"], "f_", 0)
        with ExitStack() as tokens:
            core.xn = Buffers(nc, tokens).sb("xn_tokens_b", [P, 2 * core.GT, 256])
            nystrom_attention(nc, core, a["n_wqk"], a["n_wv"], a["n_wo"], a["n_bqk"], a["n_bv"], a["n_bo"],
                              a["rwT"], a["rb"])
        experts(nc, core, a["w1"], a["b1"], a["w2"], a["b2"], "g_", 1)
        combine(nc, core, out)


def kernel(**inputs):
    import concourse.bacc as _bacc
    from concourse.bass_utils import run_bass_kernel_spmd as _run

    z = {k.removeprefix("L0_"): np.asarray(v) for k, v in inputs.items()}
    wqkv, bqkv = z["attn_b_Wqkv"], z["attn_b_bqkv"]
    arrays = {
        "x": z["attn_a_x"].reshape(4096, 256),
        "const": constants(8, 32),
        "a_wqkT": np.concatenate([z["attn_a_Wq"], z["attn_a_Wk"]]).T,
        "a_wvT": z["attn_a_Wv"].T,
        "a_woT": z["attn_a_Wo"].T,
        "a_bqk": np.concatenate([z["attn_a_bq"], z["attn_a_bk"]]),
        "a_bv": z["attn_a_bv"],
        "a_bo": z["attn_a_bo"],
        "rwT": z["ffn_router_w"].T,
        "rb": z["ffn_router_b"],
        "w1": z["ffn_w1"],
        "b1": z["ffn_b1"].reshape(16, 8, P).transpose(0, 2, 1),
        "w2": z["ffn_w2"],
        "b2": z["ffn_b2"],
        "n_wqk": wqkv[:, :512],
        "n_wv": wqkv[:, 512:],
        "n_wo": z["attn_b_Wout"],
        "n_bqk": bqkv[:512],
        "n_bv": bqkv[512:],
        "n_bo": z["attn_b_bout"],
    }
    arrays = {k: np.ascontiguousarray(v) for k, v in arrays.items()}
    nc = _bacc.Bacc("TRN2", target_bir_lowering=False, num_devices=1)
    aps = {k: nc.dram_tensor("in_" + k, v.shape, mybir.dt.from_np(v.dtype), kind="ExternalInput").ap() for k, v in arrays.items()}
    out = nc.dram_tensor("out", [4096, 256], F32, kind="ExternalOutput").ap()
    build_program(nc, aps, out)
    r = _run(nc, [{"in_" + k: v for k, v in arrays.items()}], core_ids=[0])
    return np.asarray(r.results[0]["out"]).reshape(4, 1024, 256)
```
